# Optimizing a Trainium2 kernel written in Bass

```python
import numpy as np
import jax
import jax.numpy as jnp

def _softmax(x, axis=-1):
    return jax.nn.softmax(x, axis=axis)

def _gelu(x):
    return jax.nn.gelu(x, approximate=True)

def _silu(x):
    return jax.nn.silu(x)

def _sigmoid(x):
    return jax.nn.sigmoid(x)

def _layernorm(x, axis=-1, eps=1e-05):
    m = jnp.mean(x, axis=axis, keepdims=True)
    v = jnp.var(x, axis=axis, keepdims=True)
    return (x - m) / jnp.sqrt(v + eps)

def _scatter_add(tgt, idx, src, axis=0):
    return tgt.at[idx].add(src)

def _segment_sum(src, seg, n):
    return jax.ops.segment_sum(src, seg, n)
kernel_name = 'mk_gnn_ffn_d2_gnn_r8_303967'

def setup_inputs(seed: int=0):
    np.random.seed(seed)
    _w = jnp.asarray

    def _rec_inputs():
        import jax
        import jax.numpy as jnp
        _gk = jax.random.key(seed)
        x = -6.415e-05 + 1 * jax.random.normal(jax.random.fold_in(_gk, 1), (1250, 512), jnp.float32)
        src = jax.random.randint(jax.random.fold_in(_gk, 2), (20000,), 0, 1250, jnp.int32)
        dst = jnp.minimum((1250 * jax.random.uniform(jax.random.fold_in(_gk, 3), (20000,)) ** 2.0).astype(jnp.int32), 9999)
        _o = jnp.argsort(dst, stable=True)
        src = src[_o]
        dst = dst[_o]
        edge_attr_64 = 0.000279952 + 1.00013 * jax.random.normal(jax.random.fold_in(_gk, 11), (20000, 64), jnp.float32)
        node_vec1 = jax.random.uniform(jax.random.fold_in(_gk, 13), (1250, 1), jnp.float32, 0.0, 0.999957)
        return (x, src, dst, edge_attr_64, node_vec1)
    x, src, dst, edge_attr_64, node_vec1 = _rec_inputs()

    def _L0_gnn_setup():
        import jax, jax.numpy as jnp
        import numpy as np
        N_NODES = 2500
        N_EDGES = 40000
        HIDDEN = 512
        EDGE_DIM = 64
        LN_EPS = 1e-05

        def mish(x):
            return x * jnp.tanh(jax.nn.softplus(x))
        key = jax.random.key(seed)
        ks = jax.random.split(key, 8)
        s = lambda fan_in: 1.0 / np.sqrt(fan_in)
        return {'x': jax.random.normal(ks[0], (N_NODES, HIDDEN), dtype=jnp.float32), 'edge_index': jax.random.randint(ks[1], (2, N_EDGES), 0, N_NODES, dtype=jnp.int64), 'edge_attr': jax.random.normal(ks[2], (N_EDGES, EDGE_DIM), dtype=jnp.float32), 'W1': jax.random.normal(ks[3], (2 * HIDDEN + EDGE_DIM, HIDDEN), dtype=jnp.float32) * s(2 * HIDDEN + EDGE_DIM), 'b1': jnp.zeros((HIDDEN,), dtype=jnp.float32), 'W2': jax.random.normal(ks[4], (HIDDEN, HIDDEN), dtype=jnp.float32) * s(HIDDEN), 'b2': jnp.zeros((HIDDEN,), dtype=jnp.float32), 'W3': jax.random.normal(ks[5], (2 * HIDDEN, HIDDEN), dtype=jnp.float32) * s(2 * HIDDEN), 'b3': jnp.zeros((HIDDEN,), dtype=jnp.float32), 'W4': jax.random.normal(ks[6], (HIDDEN, HIDDEN), dtype=jnp.float32) * s(HIDDEN), 'b4': jnp.zeros((HIDDEN,), dtype=jnp.float32), 'gamma': jnp.ones((HIDDEN,), dtype=jnp.float32), 'beta': jnp.zeros((HIDDEN,), dtype=jnp.float32)}
    _L0_gnn_all = _L0_gnn_setup()
    _L0_gnn_in = {k: v for k, v in _L0_gnn_all.items() if k in ('W1', 'b1', 'W2', 'b2', 'W3', 'b3', 'W4', 'b4', 'gamma', 'beta')}
    del _L0_gnn_all

    def _L0_ffn_setup():
        import jax, jax.numpy as jnp
        import numpy as np
        K = 2
        EPS = 1e-06

        def _layernorm(x, gamma, beta):
            mu = jnp.mean(x, axis=-1, keepdims=True)
            var = jnp.mean(jnp.square(x - mu), axis=-1, keepdims=True)
            return (x - mu) * jax.lax.rsqrt(var + EPS) * gamma + beta
        key = jax.random.key(seed)
        ks = jax.random.split(key, 5)
        B, S, D, F, E = (8, 256, 512, 256, 8)
        x = jax.random.normal(ks[0], (B, S, D), dtype=jnp.float32)
        router_w = jax.random.normal(ks[1], (D, E), dtype=jnp.float32) * 0.02
        w1 = jax.random.normal(ks[2], (E, D, F), dtype=jnp.float32) * 0.02
        b1 = jnp.zeros((E, F), dtype=jnp.float32)
        w2 = jax.random.normal(ks[3], (E, F, D), dtype=jnp.float32) * 0.02
        b2 = jnp.zeros((E, D), dtype=jnp.float32)
        gamma = jnp.ones((E, D), dtype=jnp.float32)
        beta = jnp.zeros((E, D), dtype=jnp.float32)
        return {'x': x, 'router_w': router_w, 'w1': w1, 'b1': b1, 'w2': w2, 'b2': b2, 'gamma': gamma, 'beta': beta}
    _L0_ffn_all = _L0_ffn_setup()
    _L0_ffn_in = {k: v for k, v in _L0_ffn_all.items() if k in ('router_w', 'w1', 'b1', 'w2', 'b2', 'gamma', 'beta')}
    del _L0_ffn_all

    def _L1_gnn_setup():
        import jax, jax.numpy as jnp
        import numpy as np
        N_NODES = 40962
        LATENT_DIM = 512
        N_EDGES = 81924
        NUM_BLOCKS = 4
        NUM_HEADS = 4
        NUM_FREQ = 32
        BASE_PERIOD = 16
        NOISE_EMB_DIM = 16
        EPS = 1e-05

        def _cond_layer_norm(x, cond, sw, sb, bw, bb):
            mu = jnp.mean(x, axis=-1, keepdims=True)
            var = jnp.var(x, axis=-1, keepdims=True)
            xn = (x - mu) * jax.lax.rsqrt(var + EPS)
            scale = cond @ sw + sb
            bias = cond @ bw + bb
            return xn * (1.0 + scale) + bias

        def _sparse_attention(x, src, dst, wq, bq, wk, bk, wv, bv, wo, bo):
            N, D = x.shape
            H, Dh = (NUM_HEADS, D // NUM_HEADS)
            q = (x @ wq + bq).reshape(N, H, Dh) * Dh ** (-0.5)
            k = (x @ wk + bk).reshape(N, H, Dh)
            v = (x @ wv + bv).reshape(N, H, Dh)
            scores = jnp.einsum('ehd,ehd->eh', q[src], k[dst])
            smax = jax.ops.segment_max(scores, src, num_segments=N)
            ex = jnp.exp(scores - smax[src])
            denom = jax.ops.segment_sum(ex, src, num_segments=N)
            attn = ex / denom[src]
            out = jax.ops.segment_sum(attn[:, :, None] * v[dst], src, num_segments=N)
            return out.reshape(N, D) @ wo + bo

        def _forward(x, edge_index, noise_levels, f_w1, f_b1, f_w2, f_b2, s1_w, s1_b, b1_w, b1_b, wq, bq, wk, bk, wv, bv, wo, bo, s2_w, s2_b, b2_w, b2_b, m_w1, m_b1, m_w2, m_b2):
            src, dst = (edge_index[0], edge_index[1])
            freqs = jnp.arange(1, NUM_FREQ + 1, dtype=x.dtype) * (2.0 * np.pi / BASE_PERIOD)
            ph = noise_levels * freqs
            emb = jnp.concatenate([jnp.sin(ph), jnp.cos(ph)], axis=-1)
            cond = jax.nn.silu(emb @ f_w1 + f_b1) @ f_w2 + f_b2
            for i in range(NUM_BLOCKS):
                y = _cond_layer_norm(x, cond, s1_w[i], s1_b[i], b1_w[i], b1_b[i])
                y = _sparse_attention(y, src, dst, wq[i], bq[i], wk[i], bk[i], wv[i], bv[i], wo[i], bo[i])
                x = x + y
                y = _cond_layer_norm(x, cond, s2_w[i], s2_b[i], b2_w[i], b2_b[i])
                y = jax.nn.relu(y @ m_w1[i] + m_b1[i]) @ m_w2[i] + m_b2[i]
                x = x + y
            return x
        key = jax.random.key(seed)
        ks = jax.random.split(key, 20)

        def w(k, shape, s=0.02):
            return jax.random.normal(k, shape, dtype=jnp.float32) * s
        D, B, C = (LATENT_DIM, NUM_BLOCKS, NOISE_EMB_DIM)
        z = lambda *s: jnp.zeros(s, jnp.float32)
        return {'latent_mesh_nodes': jax.random.normal(ks[0], (N_NODES, D), dtype=jnp.float32), 'edge_index': jax.random.randint(ks[1], (2, N_EDGES), 0, N_NODES, dtype=jnp.int32), 'noise_levels': jax.random.uniform(ks[2], (N_NODES, 1), dtype=jnp.float32), 'f_w1': w(ks[3], (2 * NUM_FREQ, C)), 'f_b1': z(C), 'f_w2': w(ks[4], (C, C)), 'f_b2': z(C), 's1_w': w(ks[5], (B, C, D)), 's1_b': z(B, D), 'b1_w': w(ks[6], (B, C, D)), 'b1_b': z(B, D), 'wq': w(ks[7], (B, D, D)), 'bq': z(B, D), 'wk': w(ks[8], (B, D, D)), 'bk': z(B, D), 'wv': w(ks[9], (B, D, D)), 'bv': z(B, D), 'wo': w(ks[10], (B, D, D)), 'bo': z(B, D), 's2_w': w(ks[11], (B, C, D)), 's2_b': z(B, D), 'b2_w': w(ks[12], (B, C, D)), 'b2_b': z(B, D), 'm_w1': w(ks[13], (B, D, D)), 'm_b1': z(B, D), 'm_w2': w(ks[14], (B, D, D)), 'm_b2': z(B, D)}
    _L1_gnn_all = _L1_gnn_setup()
    _L1_gnn_in = {k: v for k, v in _L1_gnn_all.items() if k in ('f_w1', 'f_b1', 'f_w2', 'f_b2', 's1_w', 's1_b', 'b1_w', 'b1_b', 'wq', 'bq', 'wk', 'bk', 'wv', 'bv', 'wo', 'bo', 's2_w', 's2_b', 'b2_w', 'b2_b', 'm_w1', 'm_b1', 'm_w2', 'm_b2')}
    del _L1_gnn_all

    def _L1_ffn_setup():
        import jax, jax.numpy as jnp
        import numpy as np
        import math
        B, T, D = (4, 1024, 512)
        E, K, F = (8, 2, 256)
        CAP_FACTOR = 1.25
        key = jax.random.key(seed)
        ks = jax.random.split(key, 4)
        return {'x': jax.random.normal(ks[0], (B, T, D), jnp.float32), 'gate_w': jax.random.normal(ks[1], (E, D), jnp.float32) * 0.01, 'w1': jax.random.normal(ks[2], (E, D, F), jnp.float32) * (1.0 / np.sqrt(D)), 'b1': jnp.zeros((E, F), jnp.float32), 'w2': jax.random.normal(ks[3], (E, F, D), jnp.float32) * (1.0 / np.sqrt(F)), 'b2': jnp.zeros((E, D), jnp.float32)}
    _L1_ffn_all = _L1_ffn_setup()
    _L1_ffn_in = {k: v for k, v in _L1_ffn_all.items() if k in ('gate_w', 'w1', 'b1', 'w2', 'b2')}
    del _L1_ffn_all
    return {'x': x, 'src': src, 'dst': dst, 'edge_attr_64': edge_attr_64, 'node_vec1': node_vec1, 'L0_gnn_W1': _L0_gnn_in['W1'], 'L0_gnn_b1': _L0_gnn_in['b1'], 'L0_gnn_W2': _L0_gnn_in['W2'], 'L0_gnn_b2': _L0_gnn_in['b2'], 'L0_gnn_W3': _L0_gnn_in['W3'], 'L0_gnn_b3': _L0_gnn_in['b3'], 'L0_gnn_W4': _L0_gnn_in['W4'], 'L0_gnn_b4': _L0_gnn_in['b4'], 'L0_gnn_gamma': _L0_gnn_in['gamma'], 'L0_gnn_beta': _L0_gnn_in['beta'], 'L0_ffn_router_w': _L0_ffn_in['router_w'], 'L0_ffn_w1': _L0_ffn_in['w1'], 'L0_ffn_b1': _L0_ffn_in['b1'], 'L0_ffn_w2': _L0_ffn_in['w2'], 'L0_ffn_b2': _L0_ffn_in['b2'], 'L0_ffn_gamma': _L0_ffn_in['gamma'], 'L0_ffn_beta': _L0_ffn_in['beta'], 'L1_gnn_f_w1': _L1_gnn_in['f_w1'], 'L1_gnn_f_b1': _L1_gnn_in['f_b1'], 'L1_gnn_f_w2': _L1_gnn_in['f_w2'], 'L1_gnn_f_b2': _L1_gnn_in['f_b2'], 'L1_gnn_s1_w': _L1_gnn_in['s1_w'], 'L1_gnn_s1_b': _L1_gnn_in['s1_b'], 'L1_gnn_b1_w': _L1_gnn_in['b1_w'], 'L1_gnn_b1_b': _L1_gnn_in['b1_b'], 'L1_gnn_wq': _L1_gnn_in['wq'], 'L1_gnn_bq': _L1_gnn_in['bq'], 'L1_gnn_wk': _L1_gnn_in['wk'], 'L1_gnn_bk': _L1_gnn_in['bk'], 'L1_gnn_wv': _L1_gnn_in['wv'], 'L1_gnn_bv': _L1_gnn_in['bv'], 'L1_gnn_wo': _L1_gnn_in['wo'], 'L1_gnn_bo': _L1_gnn_in['bo'], 'L1_gnn_s2_w': _L1_gnn_in['s2_w'], 'L1_gnn_s2_b': _L1_gnn_in['s2_b'], 'L1_gnn_b2_w': _L1_gnn_in['b2_w'], 'L1_gnn_b2_b': _L1_gnn_in['b2_b'], 'L1_gnn_m_w1': _L1_gnn_in['m_w1'], 'L1_gnn_m_b1': _L1_gnn_in['m_b1'], 'L1_gnn_m_w2': _L1_gnn_in['m_w2'], 'L1_gnn_m_b2': _L1_gnn_in['m_b2'], 'L1_ffn_gate_w': _L1_ffn_in['gate_w'], 'L1_ffn_w1': _L1_ffn_in['w1'], 'L1_ffn_b1': _L1_ffn_in['b1'], 'L1_ffn_w2': _L1_ffn_in['w2'], 'L1_ffn_b2': _L1_ffn_in['b2']}

def reference(x, src, dst, edge_attr_64, node_vec1, L0_gnn_W1, L0_gnn_b1, L0_gnn_W2, L0_gnn_b2, L0_gnn_W3, L0_gnn_b3, L0_gnn_W4, L0_gnn_b4, L0_gnn_gamma, L0_gnn_beta, L0_ffn_router_w, L0_ffn_w1, L0_ffn_b1, L0_ffn_w2, L0_ffn_b2, L0_ffn_gamma, L0_ffn_beta, L1_gnn_f_w1, L1_gnn_f_b1, L1_gnn_f_w2, L1_gnn_f_b2, L1_gnn_s1_w, L1_gnn_s1_b, L1_gnn_b1_w, L1_gnn_b1_b, L1_gnn_wq, L1_gnn_bq, L1_gnn_wk, L1_gnn_bk, L1_gnn_wv, L1_gnn_bv, L1_gnn_wo, L1_gnn_bo, L1_gnn_s2_w, L1_gnn_s2_b, L1_gnn_b2_w, L1_gnn_b2_b, L1_gnn_m_w1, L1_gnn_m_b1, L1_gnn_m_w2, L1_gnn_m_b2, L1_ffn_gate_w, L1_ffn_w1, L1_ffn_b1, L1_ffn_w2, L1_ffn_b2):
    import jax
    import jax.numpy as jnp

    def _L0_gnn_ref(x, edge_index, edge_attr, W1, b1, W2, b2, W3, b3, W4, b4, gamma, beta):
        import jax, jax.numpy as jnp
        import numpy as np
        N_NODES = 2500
        N_EDGES = 40000
        HIDDEN = 512
        EDGE_DIM = 64
        LN_EPS = 1e-05

        def mish(x):
            return x * jnp.tanh(jax.nn.softplus(x))
        src, dst = (edge_index[0], edge_index[1])
        edge_feat = jnp.concatenate([x[src], x[dst], edge_attr], axis=-1)
        h = mish(edge_feat @ W1 + b1)
        messages = mish(h @ W2 + b2)
        agg = jax.ops.segment_sum(messages, dst, num_segments=x.shape[0])
        u = mish(jnp.concatenate([x, agg], axis=-1) @ W3 + b3)
        out = u @ W4 + b4
        y = x + out
        mu = jnp.mean(y, axis=-1, keepdims=True)
        var = jnp.mean(jnp.square(y - mu), axis=-1, keepdims=True)
        return (y - mu) * jax.lax.rsqrt(var + LN_EPS) * gamma + beta

    def _L0_ffn_ref(x, router_w, w1, b1, w2, b2, gamma, beta):
        import jax, jax.numpy as jnp
        import numpy as np
        K = 2
        EPS = 1e-06

        def _layernorm(x, gamma, beta):
            mu = jnp.mean(x, axis=-1, keepdims=True)
            var = jnp.mean(jnp.square(x - mu), axis=-1, keepdims=True)
            return (x - mu) * jax.lax.rsqrt(var + EPS) * gamma + beta
        B, S, D = x.shape
        E = w1.shape[0]
        xf = x.reshape(-1, D)
        logits = xf @ router_w
        gate_vals, idx = jax.lax.top_k(logits, K)
        gates = jax.nn.softmax(gate_vals, axis=-1)
        out = jnp.zeros_like(xf)
        for e in range(E):
            h = jax.nn.relu(xf @ w1[e] + b1[e]) @ w2[e] + b2[e]
            y = _layernorm(xf + h, gamma[e], beta[e])
            w = jnp.sum(jnp.where(idx == e, gates, 0.0), axis=-1)
            out = out + w[:, None] * y
        return out.reshape(B, S, D)

    def _L1_gnn_ref(latent_mesh_nodes, edge_index, noise_levels, f_w1, f_b1, f_w2, f_b2, s1_w, s1_b, b1_w, b1_b, wq, bq, wk, bk, wv, bv, wo, bo, s2_w, s2_b, b2_w, b2_b, m_w1, m_b1, m_w2, m_b2):
        import jax, jax.numpy as jnp
        import numpy as np
        N_NODES = 40962
        LATENT_DIM = 512
        N_EDGES = 81924
        NUM_BLOCKS = 4
        NUM_HEADS = 4
        NUM_FREQ = 32
        BASE_PERIOD = 16
        NOISE_EMB_DIM = 16
        EPS = 1e-05

        def _cond_layer_norm(x, cond, sw, sb, bw, bb):
            mu = jnp.mean(x, axis=-1, keepdims=True)
            var = jnp.var(x, axis=-1, keepdims=True)
            xn = (x - mu) * jax.lax.rsqrt(var + EPS)
            scale = cond @ sw + sb
            bias = cond @ bw + bb
            return xn * (1.0 + scale) + bias

        def _sparse_attention(x, src, dst, wq, bq, wk, bk, wv, bv, wo, bo):
            N, D = x.shape
            H, Dh = (NUM_HEADS, D // NUM_HEADS)
            q = (x @ wq + bq).reshape(N, H, Dh) * Dh ** (-0.5)
            k = (x @ wk + bk).reshape(N, H, Dh)
            v = (x @ wv + bv).reshape(N, H, Dh)
            scores = jnp.einsum('ehd,ehd->eh', q[src], k[dst])
            smax = jax.ops.segment_max(scores, src, num_segments=N)
            ex = jnp.exp(scores - smax[src])
            denom = jax.ops.segment_sum(ex, src, num_segments=N)
            attn = ex / denom[src]
            out = jax.ops.segment_sum(attn[:, :, None] * v[dst], src, num_segments=N)
            return out.reshape(N, D) @ wo + bo

        def _forward(x, edge_index, noise_levels, f_w1, f_b1, f_w2, f_b2, s1_w, s1_b, b1_w, b1_b, wq, bq, wk, bk, wv, bv, wo, bo, s2_w, s2_b, b2_w, b2_b, m_w1, m_b1, m_w2, m_b2):
            src, dst = (edge_index[0], edge_index[1])
            freqs = jnp.arange(1, NUM_FREQ + 1, dtype=x.dtype) * (2.0 * np.pi / BASE_PERIOD)
            ph = noise_levels * freqs
            emb = jnp.concatenate([jnp.sin(ph), jnp.cos(ph)], axis=-1)
            cond = jax.nn.silu(emb @ f_w1 + f_b1) @ f_w2 + f_b2
            for i in range(NUM_BLOCKS):
                y = _cond_layer_norm(x, cond, s1_w[i], s1_b[i], b1_w[i], b1_b[i])
                y = _sparse_attention(y, src, dst, wq[i], bq[i], wk[i], bk[i], wv[i], bv[i], wo[i], bo[i])
                x = x + y
                y = _cond_layer_norm(x, cond, s2_w[i], s2_b[i], b2_w[i], b2_b[i])
                y = jax.nn.relu(y @ m_w1[i] + m_b1[i]) @ m_w2[i] + m_b2[i]
                x = x + y
            return x
        return _forward(latent_mesh_nodes, edge_index, noise_levels, f_w1, f_b1, f_w2, f_b2, s1_w, s1_b, b1_w, b1_b, wq, bq, wk, bk, wv, bv, wo, bo, s2_w, s2_b, b2_w, b2_b, m_w1, m_b1, m_w2, m_b2)

    def _L1_ffn_ref(x, gate_w, w1, b1, w2, b2):
        import jax, jax.numpy as jnp
        import numpy as np
        import math
        B, T, D = (4, 1024, 512)
        E, K, F = (8, 2, 256)
        CAP_FACTOR = 1.25
        Bx, Tx, Dx = x.shape
        N = Bx * Tx
        C = math.ceil(CAP_FACTOR * N / E)
        xf = x.reshape(N, Dx)
        probs = jax.nn.softmax(xf @ gate_w.T, axis=-1)
        topk_vals, topk_idx = jax.lax.top_k(probs, K)
        topk_vals = topk_vals / topk_vals.sum(-1, keepdims=True)
        flat_e = topk_idx.reshape(N * K)
        onehot = jax.nn.one_hot(flat_e, E, dtype=jnp.int32)
        pos = jnp.cumsum(onehot, axis=0)[jnp.arange(N * K), flat_e] - 1
        keep = pos < C
        pos_safe = jnp.where(keep, pos, C)
        token_ids = jnp.repeat(jnp.arange(N), K)
        buf = jnp.zeros((E, C + 1, Dx), x.dtype).at[flat_e, pos_safe].set(xf[token_ids])
        expert_in = buf[:, :C]
        h = jax.nn.gelu(jnp.einsum('ecd,edf->ecf', expert_in, w1) + b1[:, None, :], approximate=False)
        expert_out = jnp.einsum('ecf,efd->ecd', h, w2) + b2[:, None, :]
        gathered = expert_out[flat_e, jnp.minimum(pos_safe, C - 1)]
        w = (topk_vals.reshape(N * K) * keep).astype(x.dtype)
        out = (gathered * w[:, None]).reshape(N, K, Dx).sum(axis=1)
        return out.reshape(Bx, Tx, Dx)
    edge_index = jnp.stack([src, dst])
    x = x + _L0_gnn_ref(_layernorm(x, axis=-1), edge_index, edge_attr_64, L0_gnn_W1, L0_gnn_b1, L0_gnn_W2, L0_gnn_b2, L0_gnn_W3, L0_gnn_b3, L0_gnn_W4, L0_gnn_b4, L0_gnn_gamma, L0_gnn_beta)
    x = x + _L0_ffn_ref(_layernorm(x, axis=-1)[None], L0_ffn_router_w, L0_ffn_w1, L0_ffn_b1, L0_ffn_w2, L0_ffn_b2, L0_ffn_gamma, L0_ffn_beta)[0]
    x = x + _L1_gnn_ref(_layernorm(x, axis=-1), edge_index, node_vec1, L1_gnn_f_w1, L1_gnn_f_b1, L1_gnn_f_w2, L1_gnn_f_b2, L1_gnn_s1_w, L1_gnn_s1_b, L1_gnn_b1_w, L1_gnn_b1_b, L1_gnn_wq, L1_gnn_bq, L1_gnn_wk, L1_gnn_bk, L1_gnn_wv, L1_gnn_bv, L1_gnn_wo, L1_gnn_bo, L1_gnn_s2_w, L1_gnn_s2_b, L1_gnn_b2_w, L1_gnn_b2_b, L1_gnn_m_w1, L1_gnn_m_b1, L1_gnn_m_w2, L1_gnn_m_b2)
    x = x + _L1_ffn_ref(_layernorm(x, axis=-1)[None], L1_ffn_gate_w, L1_ffn_w1, L1_ffn_b1, L1_ffn_w2, L1_ffn_b2)[0]
    return x

_drawn_inputs = setup_inputs


def setup_inputs(seed=0):
    import zlib

    import numpy as np

    out = dict(_drawn_inputs(seed))
    spreads = {'L0_gnn_b1': (0.0, 0.1),
     'L0_gnn_b2': (0.0, 0.1),
     'L0_gnn_b3': (0.0, 0.307),
     'L0_gnn_b4': (0.0, 0.1),
     'L0_gnn_gamma': (1.0, 0.2),
     'L0_gnn_beta': (0.0, 0.1),
     'L0_ffn_b1': (0.0, 0.735),
     'L0_ffn_b2': (0.0, 0.1),
     'L0_ffn_gamma': (1.0, 0.2),
     'L0_ffn_beta': (0.0, 0.1),
     'L1_gnn_f_b1': (0.0, 0.8),
     'L1_gnn_f_b2': (0.0, 0.8),
     'L1_gnn_s1_b': (0.0, 0.652),
     'L1_gnn_b1_b': (0.0, 0.433),
     'L1_gnn_bq': (0.0, 0.8),
     'L1_gnn_bk': (0.0, 0.8),
     'L1_gnn_bv': (0.0, 0.1),
     'L1_gnn_bo': (0.0, 0.1),
     'L1_gnn_s2_b': (0.0, 0.612),
     'L1_gnn_b2_b': (0.0, 0.522),
     'L1_gnn_m_b1': (0.0, 0.322),
     'L1_gnn_m_b2': (0.0, 0.1),
     'L1_ffn_b1': (0.0, 0.789),
     'L1_ffn_b2': (0.0, 0.553)}
    factors = {'node_vec1': 8.0,
     'L1_gnn_f_w1': 8.0,
     'L1_gnn_f_w2': 8.0,
     'L1_gnn_s1_w': 8.0,
     'L1_gnn_b1_w': 8.0,
     'L1_gnn_wq': 4.981,
     'L1_gnn_wk': 5.87,
     'L1_gnn_s2_w': 8.0,
     'L1_gnn_b2_w': 8.0}
    for name, (base, spread) in spreads.items():
        noise = np.random.default_rng([zlib.crc32(name.encode()), seed]).standard_normal(out[name].shape)
        drawn = base * np.exp(spread * noise) if base else spread * noise
        out[name] = jnp.asarray(drawn.astype(out[name].dtype))
    for name, factor in factors.items():
        out[name] = (out[name] * factor).astype(out[name].dtype)
    return out
```

```python
from contextlib import ExitStack

import concourse.bass as bass
from concourse import mybir

F32 = mybir.dt.float32
F32R = mybir.dt.float32r
BF16 = mybir.dt.bfloat16
F16 = mybir.dt.float16
I32 = mybir.dt.int32
U32 = mybir.dt.uint32
ALU = mybir.AluOpType
ACT = mybir.ActivationFunctionType
AX_X = mybir.AxisListType.X

NODES, D, EDGES, EDGE_DIM = 1250, 512, 20000, 64
P = 125
NT = NODES // P
KC = D // 128
GT = 4
GE = GT * P
NG = EDGES // GE
MISH_CLAMP = 20.0
LEAD = 2
MASKED = -1.0e30


def after(eng, sem, value):
    if isinstance(value, int) and value <= 0:
        return
    eng.wait_ge(sem, value)


def at(t, width):
    return bass.ds(t * width, width)


class Core:

    def __init__(self, nc, ctx):
        self.nc, self.ctx = nc, ctx

    def sb(self, name, shape, dt=F32, ctx=None):
        return (ctx or self.ctx).enter_context(self.nc.sbuf_tensor(name, shape, dt))

    def ps(self, name, shape, dt=F32, ctx=None):
        return (ctx or self.ctx).enter_context(self.nc.psum_tensor(name, shape, dt))

    def sem(self, name):
        return self.nc.alloc_semaphore(name=name)

    def stage(self, body, *args):
        with self.nc.cleanup_on_exit():
            body(self.nc, self, *args)




def layer_norm_stats(dve, x, stats, mv, var_eps, eps, s_stats, s_mv, s_var, s_gate, n):
    dve.bn_stats(stats, x).then_inc(s_stats, 1)
    dve.wait_ge(s_stats, n + 1)
    dve.sem_inc(s_gate, 1)
    dve.bn_aggr(mv, stats).then_inc(s_mv, 1)
    dve.wait_ge(s_mv, n + 1)
    dve.tensor_scalar(var_eps, mv[:, 1:2], eps, None, ALU.add).then_inc(s_var, 1)


def node_products(nc, core, a, keep):
    with ExitStack() as ctx:
        sb = lambda n, s, d=F32: core.sb(n, s, d, ctx)
        ps = lambda n, s, d=F32: core.ps(n, s, d, ctx)
        sem = lambda n: core.sem(n)
        w_src, w_dst, w_self = (sb(n, [128, KC, D]) for n in ("w_src", "w_dst", "w_self"))
        b3_rows = sb("b3_rows", [P, D])
        xn = sb("xn_cur", [P, 2, D])
        xnT = sb("xnT_cur", [128, 2, KC, P])
        ends = sb("ends_cur", [P, 2, 2, D])
        stats, mv = sb("p1_stats", [P, 2, 6]), sb("p1_mv", [P, 2, 2])
        var_eps, rstd = sb("p1_var", [P, 2, 1]), sb("p1_rstd", [P, 2, 1])
        dst_rows, extent = sb("dst_rows", [NG, GE], I32), sb("extent", [NG, 2])
        extents = sb("extents", [NT, NG, 2])
        gmax, gmin = extents[:, :, 0], extents[:, :, 1]
        hit, tmp = (sb(n, [NT, NG]) for n in ("hit", "tmp_r"))
        thr, gidx = sb("thr", [NT, 2]), sb("gidx", [NT, NG])
        bounds, bounds_i = sb("bounds", [NT, 2]), sb("bounds_i", [NT, 2])
        row, row_len = sb("bounds_row", [1, 2 * NT]), sb("len_row", [1, NT])
        cum = sb("cum_row", [1, NT])
        ones_row = sb("ones_row", [1, NT])
        pT = ps("p1_T", [128, 2, 512])
        pE = ps("p1_E", [P, 2, 2, 512])
        pS = ps("p1_S", [P, 2, 512])
        x_in, w_in, dst_in, row_in = sem("p1_x_in"), sem("p1_w_in"), sem("p1_dst_in"), sem("p1_row_in")
        consts, s_stats, s_mv, s_var, s_rstd, s_xn, gate = (sem("p1_" + n) for n in
            ("consts", "stats", "mv", "var", "rstd", "xn", "gate"))
        s_kept, s_T, s_xT, s_prod, s_ends, s_self = (sem("p1_" + n) for n in ("kept", "T", "xT", "prod", "ends", "self"))
        s_out = [sem("p1_out0"), sem("p1_out1")]
        s_extent, extent_out, extent_in = sem("p1_extent"), sem("p1_extent_out"), sem("p1_extent_in")
        s_rng, s_bounds = sem("p1_rng"), sem("p1_bounds")
        block = ctx.enter_context(nc.Block())

        @block.sync
        def _(sp):
            for s in (s_stats, s_mv, s_var, s_rstd, s_xn, s_kept, s_T, s_xT, s_prod, s_ends, s_self):
                sp.sem_inc(s, LEAD)
            for s in s_out:
                sp.sem_inc(s, 16)
            sp.dma_start(keep.x[:, :].rearrange("p (t d) -> p t d", d=D),
                         a["x"].rearrange("(t p) d -> p t d", p=P)).then_inc(x_in, 16)
            for w, r in ((w_src, 0), (w_dst, D)):
                sp.dma_start(w[:, :, :], a["L0_gnn_W1"][r:r + D, :].rearrange("(k p) n -> p k n", p=128)).then_inc(w_in, 16)
            sp.dma_start(w_self[:, :, :], a["L0_gnn_W3"][0:D, :].rearrange("(k p) n -> p k n", p=128)).then_inc(w_in, 16)
            sp.dma_start(b3_rows[:, :], a["L0_gnn_b3"].rearrange("(a n) -> a n", a=1).broadcast_to([P, D])).then_inc(w_in, 16)
            with sp.Fori(0, NT // 2) as i:
                for u in range(2):
                    t = 2 * i + u
                    sp.wait_ge(s_ends, LEAD + t + 1)
                    sp.dma_start(keep.ends_dram[bass.ds(t * P, P), :, :], ends[:, u, :, :]).then_inc(s_out[u], 16)
            for u in range(2):
                sp.wait_ge(s_out[u], 16 * NT // 2 + 16)

        @block.scalar
        def _(act):
            act.dma_start(dst_rows[:, :], a["dst"].rearrange("(g e) -> g e", g=NG)).then_inc(dst_in, 16)
            act.dma_start(keep.src_i[:, :], a["src_cols"]).then_inc(dst_in, 16)
            act.dma_start(keep.dst_i[:, :], a["dst_cols"]).then_inc(dst_in, 16)
            act.wait_ge(s_extent, 2)
            act.dma_start(keep.extent_dram, extent[:, :]).then_inc(extent_out, 16)
            act.wait_ge(extent_out, 16)
            act.dma_start(extents[:, :, :].rearrange("n g c -> n (g c)"),
                          keep.extent_dram.rearrange("g c -> (g c)").rearrange("(a e) -> a e", a=1).broadcast_to([NT, 2 * NG])
                          ).then_inc(extent_in, 16)
            with act.Fori(0, NT // 2) as i:
                for u in range(2):
                    t = 2 * i + u
                    act.wait_ge(s_T, LEAD + t + 1)
                    act.wait_ge(s_prod, LEAD + t)
                    act.activation(xnT[:, u, :, :].rearrange("p k m -> p (k m)"), pT[:, u, 0:KC * P], ACT.Copy).then_inc(s_xT, 1)
                for u in range(2):
                    t = 2 * i + u
                    act.wait_ge(s_prod, LEAD + t + 1)
                    act.wait_ge(s_out[u], 16 * i + 16)
                    act.activation(ends[:, u, :, :].rearrange("p a n -> p (a n)"), pE[:, u, :, :].rearrange("p a n -> p (a n)"),
                                   ACT.Copy).then_inc(s_ends, 1)
            act.wait_ge(s_bounds, 1)
            act.dma_start(row[:, :].rearrange("a (n c) -> a n c", c=2), bounds[:, :]).then_inc(row_in, 16)
            act.wait_ge(row_in, 16)

        @block.gpsimd
        def _(pool):
            pool.memset(keep.ident[:, :], 0.0).then_inc(consts, 1)
            pool.memset(keep.minus_half[:, :], -0.5).then_inc(consts, 1)
            pool.iota(keep.node_id[:, :], pattern=[[1, NODES]], base=0, channel_multiplier=0,
                      allow_small_or_imprecise_dtypes=True).then_inc(consts, 1)
            pool.iota(keep.node_id16[:, :], pattern=[[1, NODES]], base=0, channel_multiplier=0,
                      allow_small_or_imprecise_dtypes=True).then_inc(consts, 1)
            pool.iota(thr[:, 0:1], pattern=[[0, 1]], base=0, channel_multiplier=P,
                      allow_small_or_imprecise_dtypes=True).then_inc(consts, 1)
            pool.iota(thr[:, 1:2], pattern=[[0, 1]], base=P, channel_multiplier=P,
                      allow_small_or_imprecise_dtypes=True).then_inc(consts, 1)
            pool.iota(gidx[:, :], pattern=[[1, NG]], base=0, channel_multiplier=0,
                      allow_small_or_imprecise_dtypes=True).then_inc(consts, 1)
            pool.memset(ones_row[:, :], 1.0).then_inc(consts, 1)
            pool.wait_ge(consts, 8)
            pool.affine_select(out=keep.ident[:, :], in_=keep.ident[:, :], compare_op=ALU.not_equal, fill=1.0, base=0,
                               pattern=[[-1, 128]], channel_multiplier=1).then_inc(consts, 1)
            with pool.Fori(0, NT // 2) as i:
                for u in range(2):
                    t = 2 * i + u
                    pool.wait_ge(s_var, LEAD + t + 1)
                    pool.tensor_tensor(rstd[:, u, :], var_eps[:, u, :], keep.minus_half[:, :], ALU.pow).then_inc(s_rstd, 1)

        @block.tensor
        def _(pe):
            pe.wait_ge(consts, 9)
            pe.wait_ge(w_in, 64)
            with pe.Fori(0, NT // 2) as i:
                for u in range(2):
                    t = 2 * i + u
                    pe.wait_ge(s_xn, LEAD + t + 1)
                    pe.wait_ge(s_xT, LEAD + t)
                    for k in range(KC):
                        mm = pe.transpose(pT[:, u, k * P:(k + 1) * P], xn[:, u, k * 128:(k + 1) * 128], keep.ident[0:P, 0:P])
                    mm.then_inc(s_T, 1)
                for u in range(2):
                    t = 2 * i + u
                    pe.wait_ge(s_xT, LEAD + t + 1)
                    pe.wait_ge(s_ends, LEAD + t)
                    pe.wait_ge(s_self, LEAD + t)
                    for w, o in ((w_src, pE[:, u, 0, :]), (w_dst, pE[:, u, 1, :]), (w_self, pS[:, u, :])):
                        for k in range(KC):
                            mm = pe.matmul(o, xnT[:, u, k, :], w[:, k, :], start=(k == 0), stop=(k == KC - 1))
                    mm.then_inc(s_prod, 1)

        @block.vector
        def _(dve):
            chain = [0]

            def step(ins):
                chain[0] += 1
                ins.then_inc(s_rng, 1)
                dve.wait_ge(s_rng, chain[0])

            dve.wait_ge(dst_in, 48)
            dve.wait_ge(consts, 9)
            dve.wait_ge(x_in, 16)
            step(dve.tensor_copy(keep.src_f[:, :], keep.src_i[:, :]))
            step(dve.tensor_copy(keep.dst_f[:, :], keep.dst_i[:, :]))
            step(dve.tensor_scalar(keep.src_i[:, :], keep.src_f[:, :], 2.0, None, ALU.mult))
            step(dve.tensor_scalar(keep.dst_i[:, :], keep.dst_f[:, :], 2.0, 1.0, ALU.mult, ALU.add))
            dve.tensor_reduce(extent[:, 0:1], dst_rows[:, :], AX_X, ALU.max).then_inc(s_extent, 1)
            dve.tensor_reduce(extent[:, 1:2], dst_rows[:, :], AX_X, ALU.min).then_inc(s_extent, 1)
            dve.wait_ge(extent_in, 16)
            step(dve.tensor_scalar(tmp[:, :], gmin, thr[:, 1:2], None, ALU.is_lt))
            step(dve.scalar_tensor_tensor(hit[:, :], gmax, thr[:, 0:1], tmp[:, :], ALU.is_ge, ALU.mult))
            step(dve.scalar_tensor_tensor(tmp[:, :], gidx[:, :], 1.0, hit[:, :], ALU.add, ALU.mult))
            step(dve.tensor_reduce(bounds[:, 1:2], tmp[:, :], AX_X, ALU.max))
            step(dve.tensor_scalar(bounds[:, 1:2], bounds[:, 1:2], 1.0, None, ALU.max))
            step(dve.tensor_scalar(hit[:, :], hit[:, :], -1000.0, 1000.0, ALU.mult, ALU.add))
            step(dve.tensor_tensor(tmp[:, :], gidx[:, :], hit[:, :], ALU.add))
            step(dve.tensor_reduce(bounds[:, 0:1], tmp[:, :], AX_X, ALU.min))
            step(dve.tensor_scalar(bounds_i[:, 0:1], bounds[:, 1:2], -1.0, None, ALU.add))
            dve.tensor_tensor(bounds[:, 0:1], bounds[:, 0:1], bounds_i[:, 0:1], ALU.min).then_inc(s_bounds, 1)
            with dve.Fori(0, NT // 2) as i:
                for u in range(2):
                    t = 2 * i + u
                    xt = keep.x[:, at(t, D)]
                    layer_norm_stats(dve, xt, stats[:, u, :], mv[:, u, :], var_eps[:, u, :], 1e-5,
                                     s_stats, s_mv, s_var, gate, LEAD + t)
                for u in range(2):
                    t = 2 * i + u
                    xt = keep.x[:, at(t, D)]
                    dve.wait_ge(s_rstd, LEAD + t + 1)
                    dve.wait_ge(s_T, LEAD + t)
                    dve.tensor_scalar(xn[:, u, :], xt, mv[:, u, 0:1], rstd[:, u, :], ALU.subtract, ALU.mult).then_inc(s_xn, 1)
                for u in range(2):
                    t = 2 * i + u
                    dve.wait_ge(s_xn, LEAD + t + 1)
                    dve.tensor_copy(keep.xn[:, at(t, D)], xn[:, u, :]).then_inc(s_kept, 1)
                    dve.wait_ge(s_prod, LEAD + t + 1)
                    dve.tensor_tensor(keep.self_in[:, at(t, D)], pS[:, u, :], b3_rows[:, :], ALU.add).then_inc(s_self, 1)
                    dve.wait_ge(s_kept, LEAD + t + 1)
            dve.wait_ge(row_in, 16)
            lo, hi = (row[:, :].rearrange("a (n c) -> a n c", c=2)[:, :, c] for c in (0, 1))
            step(dve.tensor_tensor(row_len[:, :], hi, lo, ALU.subtract))
            step(dve.tensor_tensor_scan(cum[:, :], ones_row[:, :], row_len[:, :], 0.0, ALU.mult, ALU.add))
            step(dve.tensor_tensor(cum[:, :], cum[:, :], hi, ALU.subtract))
            step(dve.tensor_copy(keep.ranges[:, 0:NT], lo))
            step(dve.tensor_copy(keep.ranges[:, NT:2 * NT], hi))
            step(dve.tensor_scalar(keep.ranges[:, 2 * NT:3 * NT], cum[:, :], float(NG), None, ALU.add))


def edge_messages(nc, core, a, keep):
    with ExitStack() as ctx:
        sb = lambda n, s, d=F32: core.sb(n, s, d, ctx)
        sem = lambda n: core.sem("p2_" + n)
        w_attr, w2 = sb("w_attr", [EDGE_DIM, D]), sb("w2", [128, KC, D])
        b1_col, b2_rows = sb("b1_col", [128, KC]), sb("b2_rows", [P, D])
        idx_src, idx_dst = (sb(n, [P, 2, GT], I32) for n in ("idx_src", "idx_dst"))
        at_src, at_dst = (sb(n, [P, 2, GT, D]) for n in ("at_src", "at_dst"))
        attr = sb("attr", [EDGE_DIM, 2, GE])
        pre1, th1 = sb("pre1", [128, 2, KC, GE]), sb("th1", [128, KC, GE])
        pre2, th2 = sb("pre2", [P, 2, GT, D]), sb("th2", [P, GT, D])
        pA = core.ps("p2_A", [128, KC, 512], F32, ctx)
        pB = core.ps("p2_B", [P, GT, 512], F32, ctx)
        w_in, s_idx, s_gate, s_ends = sem("w_in"), sem("idx"), sem("gate"), sem("ends_added")
        s_rows = [sem("rows0"), sem("rows1")]
        s_attr = [sem("attr0"), sem("attr1")]
        s_out = [sem("out0"), sem("out1")]
        s_A, s_preA, s_clA, s_expA, s_lnA, s_tanhA, s_hid = (
            sem(n) for n in ("A", "preA", "clampA", "expA", "lnA", "tanhA", "hidden"))
        s_B, s_preB, s_clB, s_expB, s_lnB, s_tanhB, s_msg = (
            sem(n) for n in ("B", "preB", "clampB", "expB", "lnB", "tanhB", "message"))
        ROWS = 16 * 2 * GT
        block = ctx.enter_context(nc.Block())

        def steps(eng, step):
            for g in range(4):
                step(g, g % 2, g // 2)
            with eng.Fori(2, NG // 2 - 1) as i:
                for u in range(2):
                    step(2 * i + u, u, i)
            for g in range(NG - 2, NG + 3):
                step(g, g % 2, g // 2)

        def in_a(g):
            return not isinstance(g, int) or g < NG

        def in_b(g):
            return not isinstance(g, int) or 1 <= g <= NG

        def in_c(g):
            return not isinstance(g, int) or 2 <= g < NG + 2

        def in_d(g):
            return not isinstance(g, int) or g >= 3

        @block.sync
        def _(sp):
            sp.sem_inc(s_msg, 1)
            for s in s_out:
                sp.sem_inc(s, 16)
            sp.dma_start(w_attr[:, :], a["L0_gnn_W1"][2 * D:2 * D + EDGE_DIM, :]).then_inc(w_in, 16)
            sp.dma_start(w2[:, :, :], a["L0_gnn_W2"].rearrange("(k p) n -> p k n", p=128)).then_inc(w_in, 16)
            sp.dma_start(b1_col[:, :], a["b1_cols"]).then_inc(w_in, 16)
            sp.dma_start(b2_rows[:, :], a["L0_gnn_b2"].rearrange("(a n) -> a n", a=1).broadcast_to([P, D])).then_inc(w_in, 16)

            def attributes(g, u):
                after(sp, s_A, g - 1)
                sp.dma_start(attr[:, u, :], a["attr_T"][:, at(g, GE)]).then_inc(s_attr[u], 16)

            def step(g, u, half):
                if not isinstance(g, int) or g + 1 < NG:
                    attributes(g + 1, 1 - u)
                if in_d(g):
                    sp.wait_ge(s_msg, g - 2 + 1)
                    sp.dma_start(keep.msg_dram[at(g - 3, GE), :].rearrange("(j p) n -> p j n", p=P),
                                 pre2[:, 1 - u, :, :]).then_inc(s_out[1 - u], 16)

            attributes(0, 0)
            steps(sp, step)
            for u in range(2):
                sp.wait_ge(s_out[u], 16 * NG // 2 + 16)

        @block.gpsimd
        def _(pool):
            rows = keep.ends_dram.rearrange("n a d -> (n a) d")

            def step(g, u, half):
                if not in_a(g):
                    return
                after(pool, s_rows[u], ROWS * half)
                pool.sem_inc(s_gate, 1)
                pool.tensor_copy(idx_src[:, u, :], keep.src_i[:, at(g, GT)]).then_inc(s_idx, 1)
                pool.tensor_copy(idx_dst[:, u, :], keep.dst_i[:, at(g, GT)]).then_inc(s_idx, 1)
                pool.wait_ge(s_idx, 2 * g + 2)
                pool.sem_inc(s_gate, 1)
                after(pool, s_A, g - 1)
                pool.sem_inc(s_gate, 1)
                for j in range(GT):
                    for to, idx in ((at_src, idx_src), (at_dst, idx_dst)):
                        pool.indirect_dma_start(to[:, u, j, :], None, rows,
                                                bass.IndirectOffsetOnAxis(ap=idx[:, u, j:j + 1], axis=0)
                                                ).then_inc(s_rows[u], 16)

            steps(pool, step)

        @block.scalar
        def _(act):
            def step(g, u, half):
                if in_a(g):
                    act.wait_ge(s_clA, g + 1)
                    act.activation(th1[:, :, :], th1[:, :, :], ACT.Exp).then_inc(s_expA, 1)
                    act.wait_ge(s_expA, g + 1)
                    act.activation(th1[:, :, :], th1[:, :, :], ACT.Ln, bias=1.0).then_inc(s_lnA, 1)
                    act.wait_ge(s_lnA, g + 1)
                    act.activation(th1[:, :, :], th1[:, :, :], ACT.Tanh).then_inc(s_tanhA, 1)
                if in_c(g):
                    act.wait_ge(s_clB, g - 1)
                    act.activation(th2[:, :, :], th2[:, :, :], ACT.Exp).then_inc(s_expB, 1)
                    act.wait_ge(s_expB, g - 1)
                    act.activation(th2[:, :, :], th2[:, :, :], ACT.Ln, bias=1.0).then_inc(s_lnB, 1)
                    act.wait_ge(s_lnB, g - 1)
                    act.activation(th2[:, :, :], th2[:, :, :], ACT.Tanh).then_inc(s_tanhB, 1)

            steps(act, step)

        @block.tensor
        def _(pe):
            def step(g, u, half):
                if in_a(g):
                    after(pe, s_preA, KC * g)
                    pe.wait_ge(s_attr[u], 16 * half + 16)
                    pe.wait_ge(s_ends, g + 1)
                    for f in range(KC):
                        for j in range(GT):
                            pe.matmul(pA[:, f, j * P:(j + 1) * P], at_src[:, u, j, f * 128:(f + 1) * 128],
                                      keep.ident[0:P, 0:P], start=(j == 0), stop=False,
                                      is_transpose=True, skip_group_check=True)
                        mm = pe.matmul(pA[:, f, 0:GE], w_attr[:, f * 128:(f + 1) * 128], attr[:, u, :],
                                       start=False, stop=True, skip_group_check=True)
                    mm.then_inc(s_A, 1)
                if in_b(g):
                    pe.wait_ge(s_hid, g)
                    for j in range(GT):
                        after(pe, s_preB, GT * (g - 2) + j + 1)
                        for k in range(KC):
                            mm = pe.matmul(pB[:, j, :], pre1[:, 1 - u, k, j * P:(j + 1) * P], w2[:, k, :],
                                           start=(k == 0), stop=(k == KC - 1))
                        mm.then_inc(s_B, 1)

            pe.wait_ge(w_in, 64)
            steps(pe, step)

        @block.vector
        def _(dve):
            def add_ends(g, u, half):
                dve.wait_ge(s_rows[u], ROWS * half + ROWS)
                dve.tensor_tensor(at_src[:, u, :, :], at_src[:, u, :, :], at_dst[:, u, :, :], ALU.add).then_inc(s_ends, 1)

            def step(g, u, half):
                if in_c(g):
                    dve.wait_ge(s_out[u], 16 * half)
                    for j in range(GT):
                        dve.wait_ge(s_B, GT * (g - 2) + j + 1)
                        dve.tensor_tensor(pre2[:, u, j, :], pB[:, j, :], b2_rows[:, :], ALU.add).then_inc(s_preB, 1)
                if in_a(g):
                    after(dve, s_B, GT * (g - 1))
                    dve.wait_ge(s_A, g + 1)
                    for f in range(KC):
                        dve.tensor_scalar(pre1[:, u, f, :], pA[:, f, 0:GE], b1_col[:, f:f + 1], None, ALU.add).then_inc(s_preA, 1)
                    dve.wait_ge(s_preA, KC * g + KC)
                    after(dve, s_hid, g)
                    dve.tensor_scalar(th1[:, :, :], pre1[:, u, :, :], MISH_CLAMP, None, ALU.min).then_inc(s_clA, 1)
                if in_d(g):
                    dve.wait_ge(s_tanhB, g - 2)
                    dve.tensor_tensor(pre2[:, 1 - u, :, :], pre2[:, 1 - u, :, :], th2[:, :, :], ALU.mult).then_inc(s_msg, 1)
                if in_c(g):
                    dve.wait_ge(s_preB, GT * (g - 1))
                    dve.wait_ge(s_msg, g - 2 + 1)
                    dve.tensor_scalar(th2[:, :, :], pre2[:, u, :, :], MISH_CLAMP, None, ALU.min).then_inc(s_clB, 1)
                if not isinstance(g, int) or g + 1 < NG:
                    add_ends(g + 1, 1 - u, half + u)
                if in_a(g):
                    dve.wait_ge(s_tanhA, g + 1)
                    dve.tensor_tensor(pre1[:, u, :, :], pre1[:, u, :, :], th1[:, :, :], ALU.mult).then_inc(s_hid, 1)

            dve.wait_ge(w_in, 64)
            add_ends(0, 0, 0)
            steps(dve, step)


def segment_sums(nc, core, a, keep):
    with ExitStack() as ctx:
        sb = lambda n, s, d=F32: core.sb(n, s, d, ctx)
        sem = lambda n: core.sem("seg_" + n)
        msg = sb("msg_cur", [P, GT, D])
        hot = sb("hot_dst", [P, GT, P])
        hot16 = sb("hot_dst16", [P, GT, P], BF16)
        src16 = sb("hot_src16", [P, GT, NODES], BF16)
        zeros = sb("zeros16", [1, 512], BF16)
        sums = core.ps("p_sums", [P, 2, 512], F32, ctx)
        pairs = core.ps("p_pairs", [P, 2, 3, 512], F32, ctx)
        s_in = [sem(f"in{j}") for j in range(GT)]
        s_hot, s_seg, s_tile, s_read, s_zero = (sem(n) for n in ("hot", "seg", "tile", "read", "zero"))
        block = ctx.enter_context(nc.Block())

        def visits(eng, body, before=None, behind=None):
            with eng.Fori(0, NT // 2) as i:
                for u in range(2):
                    n = 2 * i + u
                    first = eng.value_load(keep.ranges[0:1, bass.ds(n, 1)], min_val=0, max_val=NG - 1)
                    last = eng.value_load(keep.ranges[0:1, bass.ds(n + NT, 1)], min_val=1, max_val=NG)
                    seen = eng.value_load(keep.ranges[0:1, bass.ds(n + 2 * NT, 1)], min_val=0, max_val=NG * (NT + 1))
                    if before:
                        before(n, u)
                    with eng.Fori(first, last) as g:
                        body(n, u, g, g + seen)
                    if behind:
                        behind(n, u)

        @block.sync
        def _(sp):
            sp.sem_inc(s_seg, GT * NG + GT)
            sp.sem_inc(s_hot, 3 * GT * NG)
            for s in s_in:
                sp.sem_inc(s, 16 * NG)
            sp.sem_inc(s_read, 2)

            def body(n, u, g, v):
                for j in range(GT):
                    sp.wait_ge(s_seg, GT * v + j + 1)
                    sp.dma_start(msg[:, j, :], keep.msg_dram[at(GT * g + j, P), :]).then_inc(s_in[j], 16)

            visits(sp, body)

        @block.vector
        def _(dve):
            dve.memset(zeros[:, :], 0.0).then_inc(s_zero, 1)

            def body(n, u, g, v):
                for j in range(GT):
                    dve.wait_ge(s_seg, GT * v + j + 1)
                    dst = keep.dst_f[:, bass.ds(GT * g + j, 1)]
                    dve.tensor_scalar(hot[:, j, :], keep.node_id[:, at(n, P)], dst, None, ALU.is_equal).then_inc(s_hot, 1)
                    dve.tensor_scalar(hot16[:, j, :], keep.node_id[:, at(n, P)], dst, None, ALU.is_equal).then_inc(s_hot, 1)
                    dve.tensor_scalar(src16[:, j, :], keep.node_id16[:, :], keep.src_f[:, bass.ds(GT * g + j, 1)], None,
                                      ALU.is_equal).then_inc(s_hot, 1)

            visits(dve, body)

        @block.tensor
        def _(pe):
            pe.wait_ge(s_zero, 1)

            def clear(n, u):
                pe.wait_ge(s_read, n + 1)
                for bank in (sums[:, u, :], *(pairs[:, u, b, :] for b in range(3))):
                    pe.matmul(bank, zeros[0:1, 0:P], zeros[0:1, :], start=True, stop=False, skip_group_check=True)

            def body(n, u, g, v):
                for j in range(GT):
                    pe.wait_ge(s_hot, 3 * (GT * v + j + 1))
                    for s in range(NT):
                        pe.matmul(pairs[:, u, s // 4, (s % 4) * P:(s % 4 + 1) * P], src16[:, j, s * P:(s + 1) * P],
                                  hot16[:, j, :], start=False, stop=False, skip_group_check=True)
                    pe.wait_ge(s_in[j], 16 * v + 16)
                    pe.matmul(sums[:, u, :], hot[:, j, :], msg[:, j, :], start=False, stop=False,
                              skip_group_check=True).then_inc(s_seg, 1)

            def close(n, u):
                for bank in (sums[:, u, :], *(pairs[:, u, b, :] for b in range(3))):
                    mm = pe.matmul(bank, zeros[0:1, 0:P], zeros[0:1, :], start=False, stop=True, skip_group_check=True)
                mm.then_inc(s_tile, 1)

            visits(pe, body, clear, close)

        @block.scalar
        def _(act):
            with act.Fori(0, NT // 2) as i:
                for u in range(2):
                    n = 2 * i + u
                    act.wait_ge(s_tile, n + 1)
                    act.activation(keep.agg[0:P, at(n, D)], sums[:, u, :], ACT.Copy)
                    for b, tiles in ((0, 4), (1, 4), (2, 2)):
                        copy = act.activation(keep.log_pairs[:, 4 * b:4 * b + tiles, at(n, P)],
                                              pairs[:, u, b, 0:tiles * P].rearrange("p (s d) -> p s d", d=P), ACT.Copy)
                    copy.then_inc(s_read, 1)


def bcast(v, rows=P):
    return v.rearrange("(a n) -> a n", a=1).broadcast_to([rows, v.shape[0]])


def weight_rows(w):
    return w.rearrange("(k p) n -> p k n", p=128)


def node_update(nc, core, a, keep):
    with ExitStack() as ctx:
        sb = lambda n, s, d=F32: core.sb(n, s, d, ctx)
        sem = lambda n: core.sem("p3_" + n)
        w3, w4 = sb("w3_agg", [128, KC, D]), sb("w4", [128, KC, D])
        b4, gamma, beta = sb("b4_rows", [P, D]), sb("gamma_rows", [P, D]), sb("beta_rows", [P, D])
        cur, curT = sb("p3_cur", [P, 2, D]), sb("p3_curT", [128, 2, KC, P])
        y = sb("p3_y", [P, 2, D])
        stats, mv = sb("p3_stats", [P, 2, 6]), sb("p3_mv", [P, 2, 2])
        var_eps, rstd = sb("p3_var", [P, 2, 1]), sb("p3_rstd", [P, 2, 1])
        pT = core.ps("p3_T", [128, 2, 512], F32, ctx)
        pU = core.ps("p3_U", [P, 2, 512], F32, ctx)
        w_in = sem("w_in")
        s_cur, s_T, s_curT, s_U, s_pre, s_sum, s_bias = (sem(n) for n in ("cur", "T", "curT", "U", "pre", "sum", "bias"))
        s_clamp, s_exp, s_ln, s_tanh, s_mish = (sem(n) for n in ("clamp", "exp", "ln", "tanh", "mish"))
        s_stats, s_mv, s_var, gate, s_rstd, s_y = (sem(n) for n in ("stats", "mv", "var", "gate", "rstd", "y"))
        block = ctx.enter_context(nc.Block())
        HALF = NT // 2 * D

        def pairs(eng, *stages, base=0):
            with eng.Fori(0, NT // 2) as i:
                for stage in stages:
                    for u in range(2):
                        stage(2 * i + u, u, 2 * i + u + base)

        @block.sync
        def _(sp):
            for s in (s_T, s_curT, s_U, s_pre, s_stats, s_mv, s_var, s_y, s_cur):
                sp.sem_inc(s, LEAD)
            sp.dma_start(w3[:, :, :], weight_rows(a["L0_gnn_W3"][D:2 * D, :])).then_inc(w_in, 16)
            sp.dma_start(w4[:, :, :], weight_rows(a["L0_gnn_W4"])).then_inc(w_in, 16)
            for rows, name in ((b4, "b4"), (gamma, "gamma"), (beta, "beta")):
                sp.dma_start(rows[:, :], bcast(a["L0_gnn_" + name])).then_inc(w_in, 16)

        @block.gpsimd
        def _(pool):
            pool.wait_ge(w_in, 80)

            def biases(t, u, c):
                pool.tensor_tensor(keep.xn[:, at(t, D)], keep.xn[:, at(t, D)], b4[:, :], ALU.add).then_inc(s_bias, 1)
                pool.tensor_tensor(keep.x[:, at(t, D)], keep.x[:, at(t, D)], beta[:, :], ALU.add).then_inc(s_bias, 1)

            def power(t, u, c):
                pool.wait_ge(s_var, LEAD + t + 1)
                pool.tensor_tensor(rstd[:, u, :], var_eps[:, u, :], keep.minus_half[:, :], ALU.pow).then_inc(s_rstd, 1)

            pairs(pool, biases)
            pairs(pool, power)

        @block.scalar
        def _(act):
            def take(rows):
                def stage(t, u, c):
                    act.wait_ge(s_T, LEAD + c - 1)
                    act.activation(cur[:, u, :], rows[:, at(t, D)], ACT.Copy).then_inc(s_cur, 1)
                return stage

            pairs(act, take(keep.agg[0:P, :]))
            for func, before, done, bias in ((ACT.Exp, s_clamp, s_exp, 0.0), (ACT.Ln, s_exp, s_ln, 1.0), (ACT.Tanh, s_ln, s_tanh, 0.0)):
                for h in range(2):
                    act.wait_ge(before, h + 1)
                    part = keep.agg[0:P, h * HALF:(h + 1) * HALF]
                    act.activation(part, part, func, bias=bias).then_inc(done, 1)
            act.wait_ge(s_mish, 2)
            pairs(act, take(keep.self_in), base=NT)

        @block.tensor
        def _(pe):
            pe.wait_ge(w_in, 80)

            def transposes(t, u, c):
                pe.wait_ge(s_cur, LEAD + c + 1)
                pe.wait_ge(s_curT, LEAD + c - 1)
                for k in range(KC):
                    mm = pe.transpose(pT[:, u, k * P:(k + 1) * P], cur[:, u, k * 128:(k + 1) * 128], keep.ident[0:P, 0:P])
                mm.then_inc(s_T, 1)

            def product(w):
                def stage(t, u, c):
                    pe.wait_ge(s_curT, LEAD + c + 1)
                    pe.wait_ge(s_pre, LEAD + c - 1)
                    for k in range(KC):
                        mm = pe.matmul(pU[:, u, :], curT[:, u, k, :], w[:, k, :], start=(k == 0), stop=(k == KC - 1))
                    mm.then_inc(s_U, 1)
                return stage

            pairs(pe, transposes, product(w3))
            pairs(pe, transposes, product(w4), base=NT)

        @block.vector
        def _(dve):
            def evacuate(t, u, c):
                dve.wait_ge(s_T, LEAD + c + 1)
                dve.wait_ge(s_U, LEAD + c - 1)
                dve.tensor_copy(curT[:, u, :, :].rearrange("p k m -> p (k m)"), pT[:, u, 0:KC * P]).then_inc(s_curT, 1)

            def add_self(t, u, c):
                dve.wait_ge(s_U, LEAD + c + 1)
                mine = keep.self_in[:, at(t, D)]
                dve.tensor_tensor(mine, pU[:, u, :], mine, ALU.add).then_inc(s_pre, 1)

            pairs(dve, evacuate, add_self)
            dve.wait_ge(s_pre, LEAD + NT)
            for h in range(2):
                part = slice(h * HALF, (h + 1) * HALF)
                dve.tensor_scalar(keep.agg[0:P, part], keep.self_in[:, part], MISH_CLAMP, None, ALU.min).then_inc(s_clamp, 1)
            for h in range(2):
                part = slice(h * HALF, (h + 1) * HALF)
                dve.wait_ge(s_tanh, h + 1)
                dve.tensor_tensor(keep.self_in[:, part], keep.self_in[:, part], keep.agg[0:P, part], ALU.mult).then_inc(s_mish, 1)
            dve.wait_ge(w_in, 80)
            dve.wait_ge(s_bias, 2 * NT)

            def residual(t, u, c):
                dve.wait_ge(s_U, LEAD + c + 1)
                dve.tensor_tensor(y[:, u, :], pU[:, u, :], keep.xn[:, at(t, D)], ALU.add).then_inc(s_pre, 1)
                dve.wait_ge(s_pre, LEAD + c + 1)
                layer_norm_stats(dve, y[:, u, :], stats[:, u, :], mv[:, u, :], var_eps[:, u, :], 1e-5,
                                 s_stats, s_mv, s_var, gate, LEAD + t)

            def norm(t, u, c):
                dve.wait_ge(s_rstd, t + 1)
                dve.tensor_scalar(y[:, u, :], y[:, u, :], mv[:, u, 0:1], rstd[:, u, :], ALU.subtract, ALU.mult).then_inc(s_y, 1)

            def scale(t, u, c):
                dve.tensor_tensor(y[:, u, :], y[:, u, :], gamma[:, :], ALU.mult).then_inc(s_sum, 1)

            def total(t, u, c):
                mine = keep.x[:, at(t, D)]
                dve.wait_ge(s_sum, t + 1)
                dve.tensor_tensor(mine, mine, y[:, u, :], ALU.add).then_inc(s_bias, 1)

            def norm_all(t, u, c):
                norm(t, u, c)
                dve.wait_ge(s_y, LEAD + t + 1)
                scale(t, u, c)
                total(t, u, c)

            pairs(dve, evacuate, residual, norm_all, base=NT)


EXPERTS, HIDDEN = 8, 256
FC = HIDDEN // 128
CAPACITY = -(-5 * NODES // (4 * EXPERTS))
CHUNKS = ((0, 500), (500, 500), (1000, 250))


def experts(nc, core, a, keep, name, acc, norm):
    with ExitStack() as ctx:
        sb = lambda n, s, d=F32: core.sb(f"{name}_{n}", s, d, ctx)
        ps = lambda n, s: core.ps(f"{name}_{n}", s, F32, ctx)
        sem = lambda n: core.sem(f"{name}_{n}")
        w1, w2 = sb("w1", [128, 2, KC, HIDDEN]), sb("w2", [128, 2, FC, D])
        b1 = sb("b1", [128, 2, FC])
        router = sb("router", [128, KC, EXPERTS])
        offsets = sb("offsets", [EXPERTS, D])
        b2, gamma = sb("b2", [P, 2, D]), sb("gamma", [P, 2, D])
        xf = sb("xf", [P, 2, D])
        xfT = keep.agg[:, 0:KC * NODES].rearrange("p (k n) -> p k n", k=KC)
        logT, gateT = sb("logT", [EXPERTS, NODES]), sb("gateT", [EXPERTS, NODES])
        log, m1, m2, gate_w = (sb(n, [P, NT, EXPERTS]) for n in ("log", "m1", "m2", "gate_w"))
        top, idx, idx_f = sb("top", [P, NT, 8]), sb("idx", [P, NT, 8], U32), sb("idx_f", [P, NT, 8])
        ids = sb("ids", [P, NT, EXPERTS])
        second, total = sb("second", [P, NT]), sb("total", [P, NT])
        before = sb("before", [P, NT, EXPERTS])
        tri, ones = sb("tri", [P, P]), sb("ones", [P, P])
        hT = sb("hT", [128, 2, FC, 2 * P])
        y, xb = sb("y", [P, 2, D]), sb("xb", [P, 2, D])
        stats, mv = sb("stats", [P, 2, 6]), sb("mv", [P, 2, 2])
        var_eps, rstd, shift = sb("var", [P, 2, 1]), sb("rstd", [P, 2, 1]), sb("shift", [P, 2, 2])
        pT, pH, pY = ps("pT", [128, 2, 512]), ps("pH", [128, 2, 512]), ps("pY", [P, 4, 512])
        pL, pR, pW, pA = pY[0:EXPERTS, 0:3, :], pY[:, 3, :], pY[0:EXPERTS, 0:3, :], pH
        w_in, consts = sem("w_in"), sem("consts")
        s_w = [sem("w0"), sem("w1")]
        s_stats, s_mv, s_var, gate, s_rstd, s_xf, s_T, s_xfT, s_kept = (
            sem(n) for n in ("stats", "mv", "var", "gate", "rstd", "xf", "T", "xfT", "kept"))
        s_logT, s_logE, s_log, s_lg, s_r, s_exp, s_pos, s_gT, s_gE, s_off, s_acc0 = (
            sem(n) for n in ("logT", "logE", "log", "lg", "route", "exp", "pos", "gT", "gE", "off", "acc0"))
        s_h, s_act, s_y, s_yr, s_xb, s_ln, s_acc, s_e = (sem(n) for n in ("h", "act", "y", "yr", "xb", "ln", "acc", "e"))
        s_chain = sem("chain")
        block = ctx.enter_context(nc.Block())
        PAIRS = NT // 2
        pre = "L0_ffn_" if norm else "L1_ffn_"

        def by_expert(eng, body):
            with eng.Fori(0, EXPERTS // 2) as h:
                for b in range(2):
                    e = 2 * h + b
                    for i in range(PAIRS):
                        body(e, b, i, PAIRS * e + i, (PAIRS * b + i) % 2)

        @block.sync
        def _(sp):
            for s in (s_stats, s_mv, s_var, s_xf, s_T, s_xfT, s_rstd, s_kept, s_h, s_act, s_yr, s_xb, s_acc, s_y, s_ln, s_e):
                sp.sem_inc(s, 4)
            sp.sem_inc(s_ln, 4)
            sp.dma_start(router[:, :, :], a["router0" if norm else "router1"]).then_inc(w_in, 16)
            sp.dma_start(offsets[:, :], a[pre + ("beta" if norm else "b2")]).then_inc(w_in, 16)
            with sp.Fori(0, EXPERTS // 2) as h:
                for b in range(2):
                    e = 2 * h + b
                    sp.wait_ge(s_e, e + 3)
                    sp.dma_start(w1[:, b, :, :], a[pre + "w1"].rearrange("e (k p) n -> e p k n", p=128)[bass.ds(e, 1), :, :, :]
                                 .rearrange("e p k n -> p (e k) n")).then_inc(s_w[b], 16)
                    sp.dma_start(w2[:, b, :, :], a[pre + "w2"].rearrange("e (k p) n -> e p k n", p=128)[bass.ds(e, 1), :, :, :]
                                 .rearrange("e p k n -> p (e k) n")).then_inc(s_w[b], 16)
                    sp.dma_start(b1[:, b, :], a["ffn0_b1_cols" if norm else "ffn1_b1_cols"][:, at(e, FC)]).then_inc(s_w[b], 16)
                    if norm:
                        sp.dma_start(b2[:, b, :], a[pre + "b2"][bass.ds(e, 1), :].broadcast_to([P, D])).then_inc(s_w[b], 16)
                        sp.dma_start(gamma[:, b, :], a[pre + "gamma"][bass.ds(e, 1), :].broadcast_to([P, D])).then_inc(s_w[b], 16)
        WB = 80 if norm else 48

        @block.gpsimd
        def _(pool):
            pool.memset(ones[:, :], 1.0).then_inc(consts, 1)
            pool.iota(ids[:, :, :], pattern=[[0, NT], [1, EXPERTS]], base=0, channel_multiplier=0,
                      allow_small_or_imprecise_dtypes=True).then_inc(consts, 1)
            pool.memset(tri[:, :], 1.0).then_inc(consts, 1)
            pool.wait_ge(consts, 3)
            pool.affine_select(out=tri[:, :], in_=tri[:, :], compare_op=ALU.is_ge, fill=0.0, base=-1,
                               pattern=[[1, P]], channel_multiplier=-1).then_inc(consts, 1)
            with pool.Fori(0, PAIRS) as i:
                for u in range(2):
                    t = 2 * i + u
                    pool.wait_ge(s_var, 4 + t + 1)
                    pool.tensor_tensor(rstd[:, u, :], var_eps[:, u, :], keep.minus_half[:, :], ALU.pow).then_inc(s_rstd, 1)
            if norm:
                pool.wait_ge(s_kept, 4 + NT)

                def body(e, b, i, c, odd):
                    for u in range(2):
                        pool.wait_ge(s_yr, 2 * c + u + 3)
                        pool.tensor_tensor(xb[:, u, :], keep.xn[:, at(2 * i + u, D)], b2[:, b, :], ALU.add).then_inc(s_xb, 1)
                    for u in range(2):
                        pool.wait_ge(s_var, 4 + NT + 2 * c + u + 1)
                        pool.tensor_tensor(rstd[:, u, :], var_eps[:, u, :], keep.minus_half[:, :], ALU.pow).then_inc(s_rstd, 1)

                with pool.Fori(0, EXPERTS // 2) as h:
                    for b in range(2):
                        pool.wait_ge(s_w[b], WB * h + WB)
                        for i in range(PAIRS):
                            body(2 * h + b, b, i, PAIRS * (2 * h + b) + i, 0)

        @block.scalar
        def _(act):
            with act.Fori(0, PAIRS) as i:
                for u in range(2):
                    t = 2 * i + u
                    act.wait_ge(s_T, 4 + t + 1)
                    act.activation(xfT[:, :, at(t, P)], pT[:, u, 0:KC * P].rearrange("p (k m) -> p k m", k=KC),
                                   ACT.Copy).then_inc(s_xfT, 1)
                    act.wait_ge(s_xf, 4 + t + 1)
                    act.activation(keep.xn[:, at(t, D)], xf[:, u, :], ACT.Copy).then_inc(s_kept, 1)
            act.wait_ge(s_logT, 1)
            for j, (c0, n) in enumerate(CHUNKS):
                act.activation(logT[:, c0:c0 + n], pL[:, j, 0:n], ACT.Copy).then_inc(s_logE, 1)
            act.wait_ge(s_r, 3)
            act.activation(second[:, :], second[:, :], ACT.Exp).then_inc(s_exp, 1)
            act.wait_ge(s_gT, 1)
            for j, (c0, n) in enumerate(CHUNKS):
                act.activation(gateT[:, c0:c0 + n], pW[:, j, 0:n], ACT.Copy).then_inc(s_gE, 1)
            for t in range(NT):
                act.wait_ge(s_off, t + 1)
                act.activation(acc[:, at(t, D)], pA[0:P, t % 2, :], ACT.Copy).then_inc(s_acc0, 1)

            def body(e, b, i, c, odd):
                act.wait_ge(s_h, 4 + c + 1)
                act.wait_ge(s_y, 2 * c + 2)
                for f in range(FC):
                    act.activation(hT[:, odd, f, :], pH[:, odd, f * 2 * P:(f + 1) * 2 * P], ACT.Relu if norm else ACT.Gelu,
                                   bias=b1[:, b, f:f + 1]).then_inc(s_act, 1)

            by_expert(act, body)

        @block.tensor
        def _(pe):
            with pe.Fori(0, PAIRS) as i:
                for u in range(2):
                    t = 2 * i + u
                    pe.wait_ge(s_xf, 4 + t + 1)
                    pe.wait_ge(s_xfT, 4 + t - 1)
                    for k in range(KC):
                        mm = pe.transpose(pT[:, u, k * P:(k + 1) * P], xf[:, u, k * 128:(k + 1) * 128], keep.ident[0:P, 0:P])
                    mm.then_inc(s_T, 1)
            pe.wait_ge(w_in, 32)
            pe.wait_ge(s_xfT, 4 + NT)
            for j, (c0, n) in enumerate(CHUNKS):
                for k in range(KC):
                    mm = pe.matmul(pL[:, j, 0:n], router[:, k, :], xfT[:, k, c0:c0 + n], start=(k == 0), stop=(k == KC - 1))
            mm.then_inc(s_logT, 1)
            pe.wait_ge(s_logE, 3)
            for t in range(NT):
                mm = pe.transpose(pR[:, t * EXPERTS:(t + 1) * EXPERTS], logT[:, t * P:(t + 1) * P], keep.ident[0:EXPERTS, 0:EXPERTS])
            mm.then_inc(s_log, 1)
            if not norm:
                pe.wait_ge(consts, 4)
                pe.wait_ge(s_pos, 1)
                pe.matmul(pR[:, 256:256 + NT * EXPERTS], tri[:, :], m1[:, :, :].rearrange("p t e -> p (t e)"), start=True, stop=False)
                pe.matmul(pR[:, 256:256 + NT * EXPERTS], ones[:, :], before[:, :, :].rearrange("p t e -> p (t e)"),
                          start=False, stop=True).then_inc(s_pos, 1)
            pe.wait_ge(s_lg, 2)
            for t in range(NT):
                mm = pe.transpose(pW[:, t // 4, (t % 4) * P:(t % 4 + 1) * P], gate_w[:, t, :], keep.ident[0:P, 0:P])
            mm.then_inc(s_gT, 1)
            pe.wait_ge(s_gE, 3)
            for t in range(NT):
                if t >= 2:
                    pe.wait_ge(s_acc0, t - 1)
                pe.matmul(pA[0:P, t % 2, :], gateT[:, t * P:(t + 1) * P], offsets[:, :], start=True, stop=True).then_inc(s_off, 1)
            pe.wait_ge(s_acc0, NT)

            def hidden(e, b, i, c, odd):
                pe.wait_ge(s_act, 2 * c + 2)
                for f in range(FC):
                    for k in range(KC):
                        mm = pe.matmul(pH[:, odd, f * 2 * P:(f + 1) * 2 * P], w1[:, b, k, f * 128:(f + 1) * 128],
                                       xfT[:, k, 2 * i * P:(2 * i + 2) * P], start=(k == 0), stop=(k == KC - 1))
                mm.then_inc(s_h, 1)

            def second_product(e, b, i, c, odd):
                pe.wait_ge(s_act, 4 + 2 * c + 2)
                for u in range(2):
                    pe.wait_ge(s_yr, 2 * c + u + 1)
                    for f in range(FC):
                        mm = pe.matmul(pY[:, 2 * odd + u, :], hT[:, odd, f, u * P:(u + 1) * P], w2[:, b, f, :],
                                       start=(f == 0), stop=(f == FC - 1))
                    mm.then_inc(s_y, 1)

            with pe.Fori(0, EXPERTS // 2) as h:
                for b in range(2):
                    e = 2 * h + b
                    pe.wait_ge(s_w[b], WB * h + WB)
                    hidden(e, b, 0, PAIRS * e, (PAIRS * b) % 2)
                    for i in range(PAIRS):
                        if i + 1 < PAIRS:
                            hidden(e, b, i + 1, PAIRS * e + i + 1, (PAIRS * b + i + 1) % 2)
                        second_product(e, b, i, PAIRS * e + i, (PAIRS * b + i) % 2)

        @block.vector
        def _(dve):
            with dve.Fori(0, PAIRS) as i:
                for u in range(2):
                    t = 2 * i + u
                    layer_norm_stats(dve, keep.x[:, at(t, D)], stats[:, u, :], mv[:, u, :], var_eps[:, u, :], 1e-5,
                                     s_stats, s_mv, s_var, gate, 4 + t)
                for u in range(2):
                    t = 2 * i + u
                    dve.wait_ge(s_rstd, 4 + t + 1)
                    dve.wait_ge(s_T, 4 + t - 1)
                    dve.wait_ge(s_kept, 4 + t - 1)
                    dve.tensor_scalar(xf[:, u, :], keep.x[:, at(t, D)], mv[:, u, 0:1], rstd[:, u, :],
                                      ALU.subtract, ALU.mult).then_inc(s_xf, 1)
            chain = [0]

            def step(ins):
                chain[0] += 1
                ins.then_inc(s_chain, 1)
                dve.wait_ge(s_chain, chain[0])

            dve.wait_ge(s_log, 1)
            step(dve.tensor_copy(log[:, :, :].rearrange("p t e -> p (t e)"), pR[:, 0:NT * EXPERTS]))
            for t in range(NT):
                step(dve.max(top[:, t, :], log[:, t, :]))
                step(dve.max_index(idx[:, t, :], top[:, t, :], log[:, t, :]))
            step(dve.tensor_copy(idx_f[:, :, :], idx[:, :, :]))
            dve.tensor_tensor(second[:, :], top[:, :, 1], top[:, :, 0], ALU.subtract).then_inc(s_r, 3)
            dve.wait_ge(s_exp, 1)
            dve.wait_ge(consts, 4)
            step(dve.tensor_scalar(total[:, :], second[:, :], 1.0, None, ALU.add))
            step(dve.reciprocal(total[:, :], total[:, :]))
            step(dve.tensor_tensor(second[:, :], second[:, :], total[:, :], ALU.mult))
            wide = lambda v: v.broadcast_to([P, NT, EXPERTS])
            step(dve.tensor_tensor(m1[:, :, :], ids[:, :, :], wide(idx_f[:, :, 0:1]), ALU.is_equal))
            step(dve.tensor_tensor(m2[:, :, :], ids[:, :, :], wide(idx_f[:, :, 1:2]), ALU.is_equal))
            step(dve.tensor_tensor(gate_w[:, :, :], m1[:, :, :], wide(total[:, :].rearrange("p (t o) -> p t o", o=1)), ALU.mult))
            step(dve.tensor_tensor(log[:, :, :], m2[:, :, :], wide(second[:, :].rearrange("p (t o) -> p t o", o=1)), ALU.mult))
            step(dve.tensor_tensor(gate_w[:, :, :], gate_w[:, :, :], log[:, :, :], ALU.add))
            if not norm:
                step(dve.tensor_tensor(m1[:, :, :], m1[:, :, :], m2[:, :, :], ALU.add))
                step(dve.memset(before[:, 0, :], 0.0))
                for t in range(1, NT):
                    step(dve.tensor_tensor(before[:, t, :], before[:, t - 1, :], m1[:, t - 1, :], ALU.add))
                dve.sem_inc(s_pos, 1)
                dve.wait_ge(s_pos, 2)
                flat = lambda v: v[:, :, :].rearrange("p t e -> p (t e)")
                step(dve.scalar_tensor_tensor(flat(gate_w), pR[:, 256:256 + NT * EXPERTS], float(CAPACITY), flat(gate_w),
                                              ALU.is_lt, ALU.mult))
            dve.sem_inc(s_lg, 2)
            dve.wait_ge(s_acc0, NT)

            def sum_norm(e, b, i, c):
                for u in range(2):
                    dve.wait_ge(s_y, 4 + 2 * c + u + 1)
                    dve.wait_ge(s_xb, 4 + 2 * c + u + 1)
                    dve.wait_ge(s_ln, 8 * c + 4 * u + 4)
                    dve.tensor_tensor(y[:, u, :], pY[:, 2 * ((PAIRS * b + i) % 2) + u, :], xb[:, u, :], ALU.add).then_inc(s_yr, 1)
                for u in range(2):
                    dve.wait_ge(s_yr, 4 + 2 * c + u + 1)
                    layer_norm_stats(dve, y[:, u, :], stats[:, u, :], mv[:, u, :], var_eps[:, u, :], 1e-6,
                                     s_stats, s_mv, s_var, gate, 4 + NT + 2 * c + u)
                for u in range(2):
                    t = 2 * i + u
                    n = 4 * (2 * c + u)
                    dve.wait_ge(s_rstd, 4 + NT + 2 * c + u + 1)
                    dve.tensor_scalar(shift[:, u, 0:1], rstd[:, u, :], gate_w[:, t, bass.ds(e, 1)], None, ALU.mult).then_inc(s_ln, 1)
                    dve.wait_ge(s_ln, n + 8 + 1)
                    dve.tensor_scalar(y[:, u, :], y[:, u, :], mv[:, u, 0:1], shift[:, u, 0:1], ALU.subtract, ALU.mult).then_inc(s_ln, 1)
                    dve.wait_ge(s_ln, n + 8 + 2)
                    dve.tensor_tensor(y[:, u, :], y[:, u, :], gamma[:, b, :], ALU.mult).then_inc(s_ln, 1)
                    dve.wait_ge(s_ln, n + 8 + 3)
                    dve.tensor_tensor(acc[:, at(t, D)], acc[:, at(t, D)], y[:, u, :], ALU.add).then_inc(s_ln, 1)

            def sum_plain(e, b, i, c):
                for u in range(2):
                    t = 2 * i + u
                    dve.wait_ge(s_y, 4 + 2 * c + u + 1)
                    dve.scalar_tensor_tensor(acc[:, at(t, D)], pY[:, 2 * ((PAIRS * b + i) % 2) + u, :], gate_w[:, t, bass.ds(e, 1)],
                                             acc[:, at(t, D)], ALU.mult, ALU.add).then_inc(s_yr, 1)

            with dve.Fori(0, EXPERTS // 2) as h:
                for b in range(2):
                    e = 2 * h + b
                    dve.wait_ge(s_w[b], WB * h + WB)
                    for i in range(PAIRS):
                        (sum_norm if norm else sum_plain)(e, b, i, PAIRS * e + i)
                    if norm:
                        dve.wait_ge(s_ln, 8 + 8 * PAIRS * e + 8 * PAIRS)
                    else:
                        dve.wait_ge(s_yr, 4 + 2 * PAIRS * e + 2 * PAIRS)
                    dve.sem_inc(s_e, 1)
            for t in range(NT):
                dve.tensor_tensor(keep.x[:, at(t, D)], keep.x[:, at(t, D)], acc[:, at(t, D)], ALU.add).then_inc(s_acc, 1)
            dve.wait_ge(s_acc, 4 + NT)


FREQS, COND = 32, 16
TWO_PI = 6.283185307179586
TWO_PI_HIGH = 6.28125
TWO_PI_LOW = TWO_PI - TWO_PI_HIGH
ROUND = 12582912.0
SIN_LIMIT = 3.1415925


def prepare_attention(nc, core, a, keep):
    with ExitStack() as ctx:
        sb = lambda n, s, d=F32: core.sb("p5_" + n, s, d, ctx)
        sem = lambda n: core.sem("p5_" + n)
        F2 = 2 * FREQS
        phase, turns, emb = sb("phase", [F2, NODES]), sb("turns", [F2, NODES]), sb("emb", [F2, NODES])
        freq, quarter = sb("freq", [F2, 1]), sb("quarter", [F2, 2])
        fw1, fw2 = sb("fw1", [F2, COND]), sb("fw2", [COND, COND])
        fb = sb("fb", [COND, 2])
        hid = sb("hid", [COND, NODES])
        none = sb("none", [P, 2, NODES])
        stats, mv = sb("stats", [P, 2, 6]), sb("mv", [P, 2, 2])
        var_eps, rstd = sb("var", [P, 2, 1]), sb("rstd", [P, 2, 1])
        pc = core.ps("p5_pc", [COND, 2, 3, 512], F32, ctx)
        w_in, consts, s_emb, s_sin, s_h, s_hid, s_c, s_cond = (
            sem(n) for n in ("w_in", "consts", "emb", "sin", "h", "hid", "c", "cond"))
        s_chain = sem("chain")
        s_none, s_one, s_ln, s_log, s_out = (sem(n) for n in ("none", "one", "ln", "log", "out"))
        s_stats, s_mv, s_var, gate, s_rstd, s_xn = (sem(n) for n in ("stats", "mv", "var", "gate", "rstd", "xn"))
        block = ctx.enter_context(nc.Block())

        @block.sync
        def _(sp):
            for s in (s_stats, s_mv, s_var, s_log, s_ln, s_none, s_one):
                sp.sem_inc(s, LEAD)
            sp.dma_start(phase[:, :], a["node_vec1"].rearrange("n o -> o n").broadcast_to([F2, NODES])).then_inc(w_in, 16)
            sp.dma_start(fw1[:, :], a["L1_gnn_f_w1"]).then_inc(w_in, 16)
            sp.dma_start(fw2[:, :], a["L1_gnn_f_w2"]).then_inc(w_in, 16)
            sp.dma_start(fb[:, 0:1], a["L1_gnn_f_b1"].rearrange("(n o) -> n o", o=1)).then_inc(w_in, 16)
            sp.dma_start(fb[:, 1:2], a["L1_gnn_f_b2"].rearrange("(n o) -> n o", o=1)).then_inc(w_in, 16)
            sp.dma_start(keep.x_dram.rearrange("(t p) d -> p t d", p=P), keep.x[:, :].rearrange("p (t d) -> p t d", d=D)).then_inc(s_out, 16)
            with sp.Fori(0, NT) as t:
                sp.wait_ge(s_log, LEAD + t + 1)
                sp.dma_start(keep.log_dram[bass.ds(t, 1), :, :].rearrange("t p d -> p (t d)"),
                             keep.log_pairs[:, bass.ds(t, 1), :].rearrange("p t d -> p (t d)")).then_inc(s_out, 16)
            sp.wait_ge(s_out, 16 * NT + 16)

        @block.gpsimd
        def _(pool):
            for r in range(2):
                pool.iota(freq[r * FREQS:(r + 1) * FREQS, :], pattern=[[0, 1]], base=1, channel_multiplier=1,
                          allow_small_or_imprecise_dtypes=True).then_inc(consts, 1)
                pool.memset(quarter[r * FREQS:(r + 1) * FREQS, 0:1], 0.25 * r).then_inc(consts, 1)
                pool.memset(quarter[r * FREQS:(r + 1) * FREQS, 1:2], 0.25 * TWO_PI * r).then_inc(consts, 1)
            pool.memset(keep.condT[:, :], 1.0).then_inc(consts, 1)
            with pool.Fori(0, NT // 2) as i:
                for u in range(2):
                    pool.wait_ge(s_var, LEAD + 2 * i + u + 1)
                    pool.tensor_tensor(rstd[:, u, :], var_eps[:, u, :], keep.minus_half[:, :], ALU.pow).then_inc(s_rstd, 1)

        @block.scalar
        def _(act):
            act.wait_ge(s_emb, 1)
            act.activation(emb[:, :], emb[:, :], ACT.Sin).then_inc(s_sin, 1)
            act.wait_ge(s_h, 1)
            for j, (c0, n) in enumerate(CHUNKS):
                act.activation(hid[:, c0:c0 + n], pc[:, 0, j, 0:n], ACT.Silu, bias=fb[:, 0:1]).then_inc(s_hid, 1)
            act.wait_ge(s_c, 1)
            act.wait_ge(consts, 7)
            for j, (c0, n) in enumerate(CHUNKS):
                act.activation(keep.condT[0:COND, c0:c0 + n], pc[:, 1, j, 0:n], ACT.Identity, bias=fb[:, 1:2]).then_inc(s_cond, 1)
            with act.Fori(0, NT) as t:
                act.wait_ge(s_one, LEAD + t + 1)
                part = keep.log_pairs[:, bass.ds(t, 1), :]
                act.activation(part, part, ACT.Ln).then_inc(s_ln, 1)

        @block.tensor
        def _(pe):
            pe.wait_ge(w_in, 80)
            pe.wait_ge(s_sin, 1)
            for j, (c0, n) in enumerate(CHUNKS):
                mm = pe.matmul(pc[:, 0, j, 0:n], fw1[:, :], emb[:, c0:c0 + n], start=True, stop=True)
            mm.then_inc(s_h, 1)
            pe.wait_ge(s_hid, 3)
            for j, (c0, n) in enumerate(CHUNKS):
                mm = pe.matmul(pc[:, 1, j, 0:n], fw2[:, :], hid[:, c0:c0 + n], start=True, stop=True)
            mm.then_inc(s_c, 1)

        @block.vector
        def _(dve):
            chain = [0]

            def step(ins):
                chain[0] += 1
                ins.then_inc(s_chain, 1)
                dve.wait_ge(s_chain, chain[0])

            dve.wait_ge(w_in, 80)
            dve.wait_ge(consts, 7)
            step(dve.tensor_scalar(freq[:, :], freq[:, :], TWO_PI / 16, None, ALU.mult))
            step(dve.tensor_scalar(phase[:, :], phase[:, :], freq[:, :], None, ALU.mult))
            step(dve.tensor_scalar(turns[:, :], phase[:, :], 1.0 / TWO_PI, None, ALU.mult))
            step(dve.tensor_scalar(turns[:, :], turns[:, :], quarter[:, 0:1], None, ALU.add))
            step(dve.tensor_scalar(turns[:, :], turns[:, :], ROUND, -ROUND, ALU.add, ALU.add))
            step(dve.scalar_tensor_tensor(phase[:, :], turns[:, :], -TWO_PI_HIGH, phase[:, :], ALU.mult, ALU.add))
            step(dve.scalar_tensor_tensor(phase[:, :], turns[:, :], -TWO_PI_LOW, phase[:, :], ALU.mult, ALU.add))
            step(dve.tensor_scalar(phase[:, :], phase[:, :], quarter[:, 1:2], None, ALU.add))
            dve.tensor_scalar(emb[:, :], phase[:, :], SIN_LIMIT, -SIN_LIMIT, ALU.min, ALU.max).then_inc(s_emb, 1)
            with dve.Fori(0, NT // 2) as i:
                for u in range(2):
                    t = 2 * i + u
                    layer_norm_stats(dve, keep.x[:, at(t, D)], stats[:, u, :], mv[:, u, :], var_eps[:, u, :], 1e-5,
                                     s_stats, s_mv, s_var, gate, LEAD + t)
                for u in range(2):
                    t = 2 * i + u
                    part = keep.log_pairs[:, bass.ds(t, 1), :]
                    dve.wait_ge(s_log, LEAD + t - 1)
                    dve.tensor_scalar(none[:, u:u + 1, :], part, 0.0, MASKED, ALU.is_equal, ALU.mult).then_inc(s_none, 1)
                    dve.wait_ge(s_none, LEAD + t + 1)
                    dve.tensor_scalar(part, part, 1.0, None, ALU.max).then_inc(s_one, 1)
                for u in range(2):
                    t = 2 * i + u
                    dve.wait_ge(s_rstd, t + 1)
                    dve.tensor_scalar(keep.xn[:, at(t, D)], keep.x[:, at(t, D)], mv[:, u, 0:1], rstd[:, u, :],
                                      ALU.subtract, ALU.mult).then_inc(s_xn, 1)
                for u in range(2):
                    t = 2 * i + u
                    part = keep.log_pairs[:, bass.ds(t, 1), :]
                    dve.wait_ge(s_ln, LEAD + t + 1)
                    dve.tensor_tensor(part, part, none[:, u:u + 1, :], ALU.add).then_inc(s_log, 1)


BLOCKS, HEADS, DH = 4, 4, 128
PAIRS = NT // 2
W2P = 2 * P
H = 4
EMPTY = -5.0e29


def attention_blocks(nc, core, a, keep):
    with ExitStack() as ctx:
        sb = lambda n, s, d=F32: core.sb("b_" + n, s, d, ctx)
        ps = lambda n, s: core.ps("b_" + n, s, F32, ctx)
        sem = lambda n: core.sem("b_" + n)
        X = keep.xn
        w = {n: sb(n, [128, KC, D]) for n in ("wo", "m_w1", "m_w2")}
        area = sb("area", [128, 3 * KC * D])
        for n, name in enumerate(("wq", "wk", "wv")):
            w[name] = area[:, n * KC * D:(n + 1) * KC * D].rearrange("p (k d) -> p k d", d=D)
        log_cur = area[0:P, 0:2 * NODES].rearrange("p (b n) -> p b n", b=2)
        prob = area[0:P, 2 * NODES:4 * NODES].rearrange("p (b n) -> p b n", b=2)
        att = area[0:P, 4 * NODES:4 * NODES + 2 * D].rearrange("p (b n) -> p b n", b=2)
        cond_w = sb("cond_w", [COND + 1, 2, D])
        cols = sb("cols", [128, 3, KC])
        rows = {n: sb(n + "_rows", [P, D]) for n in ("bv", "bo", "m_b2")}
        KT, V = sb("KT", [128, 2, HEADS, NODES], F32R), keep.self_in
        q_parts = sb("q_parts", [128, 2, 2, HEADS, P], F32R)
        QT = keep.agg[:, 0:HEADS * NODES].rearrange("p (h n) -> p h n", h=HEADS)
        cond = sb("cond_cur", [COND + 1, 2, P])
        z, zT = sb("z", [P, 2, D]), sb("zT", [128, KC, W2P])
        hT = sb("hT", [128, KC, W2P])
        stats, mv = sb("stats", [P, 2, 6]), sb("mv", [P, 2, 2])
        var_eps, rstd = sb("var", [P, 2, 1]), sb("rstd", [P, 2, 1])
        probT = sb("probT", [P, 2, NT, P])
        top, neg, den, inv = (sb(n, [P, 2, 1]) for n in ("top", "neg", "den", "inv"))
        attT = hT[:, :, 0:P]
        bank = ps("bank", [128, 8, 512])
        pair_row, pair_half = bank[:, 6:8, :], bank[:, 4:6, :]
        score = bank[0:P, 0:3, :].rearrange("p b n -> p (b n)")
        turned, att_sum, rest = bank[0:P, 3:6, :], bank[0:P, 6, :], bank[:, 7, :]
        TURN = ((0, 4), (4, 4), (8, 2))
        SCORE = ((0, 512), (512, 512), (1024, NODES - 1024))

        w_in = {n: sem("in_" + n) for n in ("qkv", "wo", "mlp", "cond_a", "cond_m")}
        log_in = [sem("log0"), sem("log1")]
        st = {}
        for kind in "am":
            for n in ("cond", "C", "stats", "mv", "var", "rstd", "z", "m1", "mod", "T", "zT", "bias"):
                st[kind, n] = sem(f"{n}_{kind}")
        gate, g2, g3 = sem("gate"), sem("gate2"), sem("gate3")
        s_K, s_Ke, s_Q, s_Qe, s_V, s_Ve = (sem(n) for n in ("K", "Ke", "Q", "Qe", "V", "Ve"))
        s_h, s_he, s_m2, s_x2 = (sem(n) for n in ("h", "he", "m2", "x2"))
        s_qc, s_S, s_max, s_neg, s_P, s_PT, s_O, s_inv, s_att = (
            sem(n) for n in ("qc", "S", "max", "neg", "P", "PT", "O", "inv", "att"))
        s_qh, s_Kh = sem("q_high"), sem("K_high")
        s_e = [sem(f"turn{b}") for b in range(3)]
        s_aT, s_aTe, s_wo, s_x = (sem(n) for n in ("aT", "aTe", "wo", "x"))
        started = [*(s for s in st.values()), s_K, s_Ke, s_Q, s_Qe, s_V, s_Ve, s_h, s_he, s_m2, s_x2, s_qc, s_S, s_max, s_neg,
                   s_P, s_PT, s_O, s_inv, s_att, *s_e, s_aT, s_aTe, s_wo, s_x, s_qh, s_Kh]
        block = ctx.enter_context(nc.Block())

        def blocks(eng, body):
            with eng.Fori(0, BLOCKS) as blk:
                body(blk)

        @block.sync
        def _(sp):
            for s in started:
                sp.sem_inc(s, H)
            for s in log_in:
                sp.sem_inc(s, 16)

            def load(to, name, blk, s):
                sp.dma_start(to[:, :, :], a["L1_gnn_" + name][bass.ds(blk, 1), :, :].rearrange("b (k p) n -> p (b k) n", p=128)).then_inc(s, 16)

            def body(blk):
                c0 = NT * blk
                sp.wait_ge(s_aT, H + c0)
                for n in ("wq", "wk", "wv"):
                    load(w[n], n, blk, w_in["qkv"])
                sp.wait_ge(s_Ve, H + c0)
                sp.wait_ge(s_Qe, H + c0)
                sp.dma_start(rows["bv"][:, :], a["L1_gnn_bv"][bass.ds(blk, 1), :].broadcast_to([P, D])).then_inc(w_in["qkv"], 16)
                sp.wait_ge(s_x, H + c0)
                load(w["wo"], "wo", blk, w_in["wo"])
                sp.wait_ge(st["a", "bias"], H + c0)
                sp.dma_start(rows["bo"][:, :], a["L1_gnn_bo"][bass.ds(blk, 1), :].broadcast_to([P, D])).then_inc(w_in["wo"], 16)
                sp.wait_ge(st["m", "C"], H + c0)
                sp.dma_start(cond_w[:, :, :], a["cond1"][bass.ds(blk, 1), :, :, :].rearrange("b c s n -> (b c) s n")).then_inc(w_in["cond_a"], 16)
                sp.wait_ge(s_he, H + c0)
                sp.dma_start(cols[:, :, :], a["cols"][bass.ds(blk, 1), :, :, :].rearrange("b p s k -> (b p) s k")).then_inc(w_in["qkv"], 16)
                sp.wait_ge(s_x2, H + c0)
                load(w["m_w1"], "m_w1", blk, w_in["mlp"])
                load(w["m_w2"], "m_w2", blk, w_in["mlp"])
                sp.wait_ge(st["m", "bias"], H + c0)
                sp.dma_start(rows["m_b2"][:, :], a["L1_gnn_m_b2"][bass.ds(blk, 1), :].broadcast_to([P, D])).then_inc(w_in["mlp"], 16)
                sp.wait_ge(st["a", "C"], H + c0 + NT)
                sp.dma_start(cond_w[:, :, :], a["cond2"][bass.ds(blk, 1), :, :, :].rearrange("b c s n -> (b c) s n")).then_inc(w_in["cond_m"], 16)
                sp.wait_ge(s_V, H + c0 + NT)
                sp.sem_inc(g3, 1)
                with sp.Fori(0, PAIRS) as i:
                    for u in range(2):
                        sp.wait_ge(s_max, H + HEADS * (c0 + 2 * i + u - 1))
                        sp.dma_start(log_cur[:, u, :], keep.log_dram[bass.ds(2 * i + u, 1), :, :].rearrange("t p d -> p (t d)")).then_inc(log_in[u], 16)

            blocks(sp, body)

        @block.gpsimd
        def _(pool):
            def stage(kind, bias, w_sem, per, blk, c0):
                pool.wait_ge(w_sem, per * blk + per)
                pool.sem_inc(g2, 1)
                with pool.Fori(0, PAIRS) as i:
                    for u in range(2):
                        c = c0 + 2 * i + u
                        pool.wait_ge(st[kind, "var"], H + c + 1)
                        pool.tensor_tensor(rstd[:, u, :], var_eps[:, u, :], keep.minus_half[:, :], ALU.pow).then_inc(st[kind, "rstd"], 1)
                    for u in range(2):
                        c = c0 + 2 * i + u
                        x = X[:, at(2 * i + u, D)]
                        pool.wait_ge(st[kind, "z"], H + c + 1)
                        pool.tensor_tensor(x, x, bias[:, :], ALU.add).then_inc(st[kind, "bias"], 1)

            def body(blk):
                stage("a", rows["bo"], w_in["wo"], 32, blk, NT * blk)
                with pool.Fori(0, PAIRS) as i:
                    for u in range(2):
                        c = NT * blk + 2 * i + u
                        pool.wait_ge(s_qh, H + c + 1)
                        pool.tensor_tensor(q_parts[:, u, 1, :, :], QT[:, :, at(2 * i + u, P)], q_parts[:, u, 0, :, :].bitcast(F32),
                                           ALU.subtract).then_inc(s_qc, 1)
                stage("m", rows["m_b2"], w_in["mlp"], 48, blk, NT * blk)

            blocks(pool, body)

        @block.scalar
        def _(act):
            def front(kind, c0):
                def conds(i):
                    for u in range(2):
                        act.wait_ge(st[kind, "C"], H + c0 + 2 * i + u - 1)
                        act.activation(cond[:, u, :], keep.condT[:, at(2 * i + u, P)], ACT.Copy).then_inc(st[kind, "cond"], 1)
                return conds

            def turn(kind, used, c0):
                def stage(i):
                    act.wait_ge(st[kind, "T"], H + c0 + 2 * i + 2)
                    act.wait_ge(used, H + c0 + 2 * i)
                    for u in range(2):
                        ins = act.activation(zT[:, :, u * P:(u + 1) * P], bank[:, 2 * u, 0:KC * P].rearrange("p (k m) -> p k m", k=KC), ACT.Copy)
                    ins.then_inc(st[kind, "zT"], 2)
                return stage

            def body(blk):
                c0 = NT * blk
                act.wait_ge(w_in["qkv"], 80 * blk + 80)
                conds, turned_a = front("a", c0), turn("a", s_V, c0)
                conds(0)
                turned_a(0)

                def back(i, ahead):
                    ahead()
                    for half in range(2):
                        act.wait_ge(s_K, H + c0 + 2 * i + half + 1)
                        for h in range(2):
                            head = 2 * half + h
                            ins = act.activation(KT[:, 0, head, at(i, W2P)], pair_half[:, half, h * W2P:(h + 1) * W2P], ACT.Identity,
                                                 bias=cols[:, 1, head:head + 1])
                        ins.then_inc(s_Kh, 1)

                with act.Fori(0, PAIRS - 1) as i:
                    back(i, lambda: conds(i + 1))
                    turned_a(i + 1)
                back(PAIRS - 1, lambda: None)

                def queries(i, u):
                    act.wait_ge(s_S, H + HEADS * (c0 + 2 * i + u - 1))
                    act.activation(q_parts[:, u, 0, :, :], QT[:, :, at(2 * i + u, P)], ACT.Copy).then_inc(s_qh, 1)

                def exponent(i, u, h):
                    q = HEADS * (c0 + 2 * i + u) + h
                    act.wait_ge(s_neg, H + q + 1)
                    act.activation(prob[:, h % 2, :], prob[:, h % 2, :], ACT.Exp, bias=neg[:, h % 2, :],
                                   accum_out=den[:, h % 2, :]).then_inc(s_P, 1)

                def slots(i, first, last):
                    for u in range(2):
                        for h in range(HEADS):
                            c = c0 + 2 * i + u
                            q = HEADS * c + h
                            more = not (last and u == 1 and h == HEADS - 1)
                            if h == 2 and not (last and u == 1):
                                queries(i + (u == 1), 1 - u)
                            if more:
                                nu, nh = (u, h + 1) if h + 1 < HEADS else (1 - u, 0)
                                exponent(i + (u == 1 and nh == 0), nu, nh)
                            act.wait_ge(s_PT, H + 3 * q + 3)
                            act.wait_ge(s_O, H + q - 1)
                            act.activation(probT[:, h % 2, 8:10, :], turned[:, 2, 0:2 * P].rearrange("p (t m) -> p t m", t=2),
                                           ACT.Copy).then_inc(s_e[2], 1)
                            if h == 2 and not (first and u == 0):
                                turn_att(c)

                def turn_att(c):
                    act.wait_ge(s_aT, H + c)
                    act.activation(attT, rest[:, 0:KC * P].rearrange("p (k m) -> p k m", k=KC), ACT.Copy).then_inc(s_aTe, 1)

                act.wait_ge(s_Qe, H + c0 + NT)
                queries(0, 0)
                exponent(0, 0, 0)
                slots(0, True, False)
                with act.Fori(1, PAIRS - 1) as i:
                    slots(i, False, False)
                slots(PAIRS - 1, False, True)
                turn_att(c0 + NT)

                conds, turned_m = front("m", c0), turn("m", s_h, c0)
                conds(0)
                turned_m(0)

                def back_m(i, ahead):
                    ahead()
                    for half in range(2):
                        act.wait_ge(s_h, H + c0 + 2 * i + half + 1)
                        act.wait_ge(s_m2, H + c0 + 2 * i)
                        for f in range(2):
                            ins = act.activation(hT[:, 2 * half + f, :], pair_half[:, half, f * W2P:(f + 1) * W2P], ACT.Relu,
                                                 bias=cols[:, 2, 2 * half + f:2 * half + f + 1])
                        ins.then_inc(s_he, 1)

                with act.Fori(0, PAIRS - 1) as i:
                    back_m(i, lambda: conds(i + 1))
                    turned_m(i + 1)
                back_m(PAIRS - 1, lambda: None)

            blocks(act, body)

        @block.tensor
        def _(pe):
            def modulation(kind, c0, i):
                for u in range(2):
                    c = c0 + 2 * i + u
                    pe.wait_ge(st[kind, "cond"], H + c + 1)
                    pe.wait_ge(st[kind, "zT"], H + c0 + 2 * i)
                    for s in range(2):
                        mm = pe.matmul(bank[0:P, 2 * u + s, :], cond[:, u, :], cond_w[:, s, :], start=True, stop=True)
                    mm.then_inc(st[kind, "C"], 1)

            def transposes(kind, c0, i):
                for u in range(2):
                    pe.wait_ge(st[kind, "mod"], H + c0 + 2 * i + u + 1)
                    for k in range(KC):
                        mm = pe.transpose(bank[:, 2 * u, k * P:(k + 1) * P], z[:, u, k * 128:(k + 1) * 128], keep.ident[0:P, 0:P])
                    mm.then_inc(st[kind, "T"], 1)

            def halves(weight, half, done):
                for h in range(2):
                    head = 2 * half + h
                    for k in range(KC):
                        mm = pe.matmul(pair_half[:, half, h * W2P:(h + 1) * W2P], weight[:, k, head * 128:(head + 1) * 128],
                                       zT[:, k, :], start=(k == 0), stop=(k == KC - 1))
                mm.then_inc(done, 1)

            def rows_of(source, weight, u, done):
                for k in range(KC):
                    mm = pe.matmul(pair_row[0:P, u, :], source[:, k, u * P:(u + 1) * P], weight[:, k, :], start=(k == 0), stop=(k == KC - 1))
                mm.then_inc(done, 1)

            def body(blk):
                c0 = NT * blk
                pe.wait_ge(w_in["cond_a"], 16 * blk + 16)
                pe.wait_ge(w_in["qkv"], 80 * blk + 80)
                modulation("a", c0, 0)
                transposes("a", c0, 0)

                def back(i, more):
                    if more:
                        modulation("a", c0, i + 1)
                    pe.wait_ge(st["a", "zT"], H + c0 + 2 * i + 2)
                    for half in range(2):
                        pe.wait_ge(s_Qe, H + c0 + 2 * i + half - 1)
                        halves(w["wk"], half, s_K)
                    for half in range(2):
                        pe.wait_ge(s_Ke, H + c0 + 2 * i + half + 1)
                        halves(w["wq"], half, s_Q)
                    for u in range(2):
                        pe.wait_ge(s_Ve, H + c0 + 2 * i + u - 1)
                        rows_of(zT, w["wv"], u, s_V)
                    if more:
                        transposes("a", c0, i + 1)

                with pe.Fori(0, PAIRS - 1) as i:
                    back(i, True)
                back(PAIRS - 1, False)

                def scores(i, u, h):
                    c = c0 + 2 * i + u
                    q = HEADS * c + h
                    pe.wait_ge(s_qc, H + c + 1)
                    pe.wait_ge(s_max, H + q)
                    for mine, other in ((0, 0), (0, 1), (1, 0)):
                        for at0, n in SCORE:
                            mm = pe.matmul(score[:, at0:at0 + n], q_parts[:, u, mine, h, :], KT[:, other, h, at0:at0 + n],
                                           start=(mine + other == 0), stop=(mine == 1))
                    mm.then_inc(s_S, 1)

                def slots(i, first, last):
                    for u in range(2):
                        for h in range(HEADS):
                            c = c0 + 2 * i + u
                            q = HEADS * c + h
                            if not (last and u == 1 and h == HEADS - 1):
                                nu, nh = (u, h + 1) if h + 1 < HEADS else (1 - u, 0)
                                scores(i + (u == 1 and nh == 0), nu, nh)
                            pe.wait_ge(s_P, H + q + 1)
                            for b, (t0, n) in enumerate(TURN):
                                pe.wait_ge(s_e[b], H + q)
                                for t in range(n):
                                    mm = pe.transpose(turned[:, b, t * P:(t + 1) * P], prob[:, h % 2, (t0 + t) * P:(t0 + t + 1) * P],
                                                      keep.ident[0:P, 0:P])
                                mm.then_inc(s_PT, 1)
                            if h == 2 and not (first and u == 0):
                                turn_att(c, 1 - u)
                            if h == 3 and not (first and u == 0):
                                project(c)
                            if not (first and u == 0 and h == 0):
                                values(q - 1, (h - 1) % HEADS)

                def values(q, h):
                    pe.wait_ge(s_att, H + q)
                    for b, (t0, n) in enumerate(TURN):
                        pe.wait_ge(s_e[b], H + q + 1)
                        for t in range(t0, t0 + n):
                            mm = pe.matmul(att_sum[:, h * DH:(h + 1) * DH], probT[:, h % 2, t, :],
                                           V[:, t * D + h * DH:t * D + (h + 1) * DH], start=(t == 0), stop=(t == NT - 1))
                    mm.then_inc(s_O, 1)

                def turn_att(c, u):
                    pe.wait_ge(s_att, H + HEADS * c)
                    pe.wait_ge(s_x, H + c - 1)
                    for k in range(KC):
                        mm = pe.transpose(rest[:, k * P:(k + 1) * P], att[:, u, k * 128:(k + 1) * 128], keep.ident[0:P, 0:P])
                    mm.then_inc(s_aT, 1)

                def project(c):
                    pe.wait_ge(s_aTe, H + c)
                    for k in range(KC):
                        mm = pe.matmul(rest[0:P, :], attT[:, k, :], w["wo"][:, k, :], start=(k == 0), stop=(k == KC - 1))
                    mm.then_inc(s_wo, 1)

                pe.wait_ge(w_in["wo"], 32 * blk + 32)
                pe.wait_ge(s_Ke, H + c0 + NT)
                pe.wait_ge(s_Qe, H + c0 + NT)
                pe.wait_ge(s_Ve, H + c0 + NT)
                scores(0, 0, 0)
                slots(0, True, False)
                with pe.Fori(1, PAIRS - 1) as i:
                    slots(i, False, False)
                slots(PAIRS - 1, False, True)
                values(HEADS * (c0 + NT) - 1, HEADS - 1)
                turn_att(c0 + NT, 1)
                project(c0 + NT)

                pe.wait_ge(w_in["cond_m"], 16 * blk + 16)
                pe.wait_ge(w_in["mlp"], 48 * blk + 48)
                pe.wait_ge(s_x, H + c0 + NT)
                modulation("m", c0, 0)
                transposes("m", c0, 0)

                def back_m(i, more):
                    if more:
                        modulation("m", c0, i + 1)
                    pe.wait_ge(st["m", "zT"], H + c0 + 2 * i + 2)
                    for half in range(2):
                        pe.wait_ge(s_he, H + c0 + 2 * i + half - 1)
                        halves(w["m_w1"], half, s_h)
                    if more:
                        transposes("m", c0, i + 1)
                    pe.wait_ge(s_he, H + c0 + 2 * i + 2)
                    for u in range(2):
                        pe.wait_ge(s_x2, H + c0 + 2 * i + u - 1)
                        rows_of(hT, w["m_w2"], u, s_m2)

                with pe.Fori(0, PAIRS - 1) as i:
                    back_m(i, True)
                back_m(PAIRS - 1, False)
                pe.wait_ge(s_x2, H + c0 + NT)

            blocks(pe, body)

        @block.vector
        def _(dve):
            def front(kind, ready, c0):
                S = lambda n: st[kind, n]

                def stage(i):
                    for u in range(2):
                        c = c0 + 2 * i + u
                        dve.wait_ge(ready, ready_at(kind, c0, c))
                        layer_norm_stats(dve, X[:, at(2 * i + u, D)], stats[:, u, :], mv[:, u, :], var_eps[:, u, :], 1e-5,
                                         S("stats"), S("mv"), S("var"), gate, H + c)
                    for u in range(2):
                        c = c0 + 2 * i + u
                        dve.wait_ge(S("rstd"), H + c + 1)
                        dve.wait_ge(S("T"), H + c - 1)
                        dve.tensor_scalar(z[:, u, :], X[:, at(2 * i + u, D)], mv[:, u, 0:1], rstd[:, u, :],
                                          ALU.subtract, ALU.mult).then_inc(S("z"), 1)
                        dve.wait_ge(S("C"), H + c + 1)
                        dve.wait_ge(S("z"), H + c + 1)
                        dve.scalar_tensor_tensor(z[:, u, :], bank[0:P, 2 * u, :], 1.0, z[:, u, :], ALU.add, ALU.mult).then_inc(S("m1"), 1)
                        dve.wait_ge(S("m1"), H + c + 1)
                        dve.tensor_tensor(z[:, u, :], z[:, u, :], bank[0:P, 2 * u + 1, :], ALU.add).then_inc(S("mod"), 1)
                return stage

            def ready_at(kind, c0, c):
                return H + c0 if kind == "a" else H + c + 1

            def body(blk):
                c0 = NT * blk
                front_a = front("a", s_x2, c0)
                front_a(0)
                dve.wait_ge(w_in["qkv"], 80 * blk + 80)
                dve.sem_inc(gate, 1)

                def back(i, more):
                    for half in range(2):
                        dve.wait_ge(s_Kh, H + c0 + 2 * i + half + 1)
                        for h in range(2):
                            head = 2 * half + h
                            ins = dve.scalar_tensor_tensor(KT[:, 1, head, at(i, W2P)], pair_half[:, half, h * W2P:(h + 1) * W2P],
                                                           cols[:, 1, head:head + 1], KT[:, 0, head, at(i, W2P)].bitcast(F32),
                                                           ALU.add, ALU.subtract)
                        ins.then_inc(s_Ke, 1)
                    if more:
                        front_a(i + 1)
                    for half in range(2):
                        dve.wait_ge(s_Q, H + c0 + 2 * i + half + 1)
                        for h in range(2):
                            head = 2 * half + h
                            ins = dve.tensor_scalar(QT[:, head, at(i, W2P)], pair_half[:, half, h * W2P:(h + 1) * W2P],
                                                    cols[:, 0, head:head + 1], float(DH) ** -0.5, ALU.add, ALU.mult)
                        ins.then_inc(s_Qe, 1)
                    for u in range(2):
                        dve.wait_ge(s_V, H + c0 + 2 * i + u + 1)
                        dve.tensor_tensor(V[:, at(2 * i + u, D)], pair_row[0:P, u, :], rows["bv"][:, :], ALU.add).then_inc(s_Ve, 1)

                with dve.Fori(0, PAIRS - 1) as i:
                    back(i, True)
                back(PAIRS - 1, False)

                def maximum(i, u, h):
                    c = c0 + 2 * i + u
                    q = HEADS * c + h
                    dve.wait_ge(s_S, H + q + 1)
                    if h == 0:
                        dve.wait_ge(log_in[u], 16 * (PAIRS * blk + i) + 32)
                    dve.wait_ge(s_PT, H + 3 * q - 3)
                    dve.sem_inc(gate, 1)
                    dve.tensor_tensor_reduce(prob[:, h % 2, :], score[:, 0:NODES], log_cur[:, u, :], 1.0, -3.0e38, ALU.add, ALU.max,
                                             top[:, h % 2, :]).then_inc(s_max, 1)
                    dve.wait_ge(s_max, H + q + 1)
                    dve.tensor_scalar(neg[:, h % 2, :], top[:, h % 2, :], -1.0, None, ALU.mult).then_inc(s_neg, 1)

                def slots(i, first, last):
                    for u in range(2):
                        for h in range(HEADS):
                            c = c0 + 2 * i + u
                            q = HEADS * c + h
                            o = h % 2
                            if not (last and u == 1 and h == HEADS - 1):
                                nu, nh = (u, h + 1) if h + 1 < HEADS else (1 - u, 0)
                                maximum(i + (u == 1 and nh == 0), nu, nh)
                            dve.wait_ge(s_O, H + q - 1)
                            for b in range(2):
                                dve.wait_ge(s_PT, H + 3 * q + b + 1)
                                dve.tensor_copy(probT[:, o, 4 * b:4 * b + 4, :].rearrange("p t m -> p (t m)"),
                                                turned[:, b, 0:4 * P]).then_inc(s_e[b], 1)
                            dve.wait_ge(s_P, H + q + 1)
                            dve.sem_inc(gate, 1)
                            dve.wait_ge(s_att, H + q - 1)
                            dve.reciprocal(inv[:, o, :], den[:, o, :]).then_inc(s_inv, 1)
                            dve.wait_ge(s_inv, H + 2 * q + 1)
                            dve.scalar_tensor_tensor(inv[:, o, :], top[:, o, :], EMPTY, inv[:, o, :], ALU.is_gt, ALU.mult).then_inc(s_inv, 1)
                            dve.wait_ge(s_inv, H + 2 * q + 2)
                            if not (first and u == 0 and h == 0):
                                rows_done(c if h > 0 else c - 1, q - 1, u if h > 0 else 1 - u, (h - 1) % HEADS)
                            if h == 3 and not (first and u == 0):
                                add_rows(c, i - 1 if u == 0 else i, 1 - u)

                def rows_done(c, q, u, h):
                    if h == 0:
                        dve.wait_ge(s_aT, H + c - 1)
                    dve.wait_ge(s_O, H + q + 1)
                    dve.tensor_scalar(att[:, u, h * DH:(h + 1) * DH], att_sum[:, h * DH:(h + 1) * DH], inv[:, h % 2, :], None,
                                      ALU.mult).then_inc(s_att, 1)

                def add_rows(c, i, u):
                    x = X[:, at(2 * i + u, D)]
                    dve.wait_ge(s_wo, H + c)
                    dve.wait_ge(st["a", "bias"], H + c)
                    dve.tensor_tensor(x, x, rest[0:P, :], ALU.add).then_inc(s_x, 1)

                maximum(0, 0, 0)
                slots(0, True, False)
                with dve.Fori(1, PAIRS - 1) as i:
                    slots(i, False, False)
                slots(PAIRS - 1, False, True)
                rows_done(c0 + NT - 1, HEADS * (c0 + NT) - 1, 1, HEADS - 1)
                add_rows(c0 + NT, PAIRS - 1, 1)

                front_m = front("m", s_x, c0)
                front_m(0)

                def back_m(i, more):
                    if more:
                        front_m(i + 1)
                    for u in range(2):
                        c = c0 + 2 * i + u
                        x = X[:, at(2 * i + u, D)]
                        dve.wait_ge(s_m2, H + c + 1)
                        dve.wait_ge(st["m", "bias"], H + c + 1)
                        dve.tensor_tensor(x, x, pair_row[0:P, u, :], ALU.add).then_inc(s_x2, 1)

                with dve.Fori(0, PAIRS - 1) as i:
                    back_m(i, True)
                back_m(PAIRS - 1, False)

            blocks(dve, body)


def to_last_layer(nc, core, keep):
    with ExitStack() as ctx:
        old = core.sb("old_x", [P, NT * D], F32, ctx)
        old_in, summed = core.sem("old_in"), core.sem("summed")
        block = ctx.enter_context(nc.Block())

        @block.sync
        def _(sp):
            sp.dma_start(old[:, :].rearrange("p (t d) -> p t d", d=D), keep.x_dram.rearrange("(t p) d -> p t d", p=P)).then_inc(old_in, 16)

        @block.vector
        def _(dve):
            dve.wait_ge(old_in, 16)
            dve.tensor_tensor(keep.x[:, :], old[:, :], keep.xn[:, :], ALU.add).then_inc(summed, 1)
            dve.wait_ge(summed, 1)


def store_rows(nc, core, out, rows):
    with ExitStack() as ctx:
        out_done = core.sem("out_done")
        block = ctx.enter_context(nc.Block())

        @block.sync
        def _(sp):
            sp.dma_start(out.rearrange("(t p) d -> p t d", p=P), rows[:, :].rearrange("p (t d) -> p t d", d=D)).then_inc(out_done, 16)
            sp.wait_ge(out_done, 16)


def layers(nc, core, a, keep, out):
    with ExitStack() as ctx:
        sb = lambda n, s, d=F32: core.sb(n, s, d, ctx)
        keep.x = sb("x", [P, NT * D])
        keep.node_id, keep.node_id16 = sb("node_id", [P, NODES]), sb("node_id16", [P, NODES], F16)
        keep.src_i, keep.dst_i = (sb(n, [P, NG * GT], I32) for n in ("src_i", "dst_i"))
        keep.src_f, keep.dst_f = (sb(n, [P, NG * GT]) for n in ("src_f", "dst_f"))
        keep.ranges = sb("ranges", [1, 3 * NT], I32)
        core.stage(node_products, a, keep)
        core.stage(edge_messages, a, keep)
        keep.log_pairs = sb("log_pairs", [P, NT, NODES])
        core.stage(segment_sums, a, keep)
        core.stage(node_update, a, keep)
        core.stage(experts, a, keep, "f0", keep.self_in, True)
        core.stage(prepare_attention, a, keep)
    core.stage(attention_blocks, a, keep)
    with ExitStack() as ctx:
        keep.x = core.sb("last_x", [P, NT * D], F32, ctx)
        core.stage(to_last_layer, keep)
        core.stage(experts, a, keep, "f1", keep.self_in, False)
        core.stage(store_rows, out, keep.x)


class Keep:
    pass


def build(nc, a, out):
    with ExitStack() as ctx:
        core = Core(nc, ctx)
        keep = Keep()
        keep.xn = core.sb("xn", [P, NT * D])
        keep.self_in = core.sb("self_in", [P, NT * D])
        keep.agg = core.sb("agg", [128, NT * D])
        keep.ident = core.sb("ident", [128, 128])
        keep.minus_half = core.sb("minus_half", [P, 1])
        keep.condT = core.sb("condT", [COND + 1, NODES])
        keep.ends_dram = nc.dram_tensor("ends_rows", (NODES, 2, D), F32, kind="Internal").ap()
        keep.extent_dram = nc.dram_tensor("group_extents", (NG, 2), F32, kind="Internal").ap()
        keep.msg_dram = nc.dram_tensor("messages", (EDGES, D), F32, kind="Internal").ap()
        keep.x_dram = nc.dram_tensor("x_rows", (NODES, D), F32, kind="Internal").ap()
        keep.log_dram = nc.dram_tensor("log_counts", (NT, P, NODES), F32, kind="Internal").ap()
        layers(nc, core, a, keep, out)


def kernel(**inputs):
    import numpy as _np
    import concourse.bacc as _bacc
    from concourse import mybir as _mybir
    from concourse.bass_utils import run_bass_kernel_spmd as _run

    nc = _bacc.Bacc("TRN2", target_bir_lowering=False, num_devices=1)
    data = {k: _np.asarray(v) for k, v in inputs.items()}
    data["src_cols"] = data["src"].reshape(-1, P).T
    data["dst_cols"] = data["dst"].reshape(-1, P).T
    data["attr_T"] = data["edge_attr_64"].T
    data["b1_cols"] = data["L0_gnn_b1"].reshape(KC, 128).T
    data["router0"] = data["L0_ffn_router_w"].reshape(KC, 128, EXPERTS).transpose(1, 0, 2)
    data["router1"] = data["L1_ffn_gate_w"].reshape(EXPERTS, KC, 128).transpose(2, 1, 0)
    data["ffn0_b1_cols"] = data["L0_ffn_b1"].reshape(EXPERTS * FC, 128).T
    data["ffn1_b1_cols"] = data["L1_ffn_b1"].reshape(EXPERTS * FC, 128).T
    for n, s, b in (("cond1", "s1", "b1"), ("cond2", "s2", "b2")):
        data[n] = _np.stack([_np.concatenate([data[f"L1_gnn_{v}_w"], data[f"L1_gnn_{v}_b"][:, None, :]], axis=1)
                             for v in (s, b)], axis=2)
    data["cols"] = _np.stack([data["L1_gnn_" + n].reshape(BLOCKS, KC, 128).transpose(0, 2, 1) for n in ("bq", "bk", "m_b1")], axis=2)
    for unused in ("src", "edge_attr_64"):
        del data[unused]
    arrays, args = {}, {}
    for name, v in data.items():
        v = _np.ascontiguousarray(v)
        arrays["in_" + name] = v
        args[name] = nc.dram_tensor("in_" + name, v.shape, _mybir.dt.from_np(v.dtype), kind="ExternalInput").ap()
    out = nc.dram_tensor("out_0", (NODES, D), F32, kind="ExternalOutput").ap()
    build(nc, args, out)
    r = _run(nc, [arrays], core_ids=[0])
    return r.results[0]["out_0"]
```

```python
from contextlib import ExitStack

import concourse.bass as bass
from concourse import mybir

F32 = mybir.dt.float32
F32R = mybir.dt.float32r
BF16 = mybir.dt.bfloat16
F16 = mybir.dt.float16
I32 = mybir.dt.int32
U32 = mybir.dt.uint32
ALU = mybir.AluOpType
ACT = mybir.ActivationFunctionType
AX_X = mybir.AxisListType.X

NODES, D, EDGES, EDGE_DIM = 1250, 512, 20000, 64
P = 125
NT = NODES // P
KC = D // 128
GT = 4
GE = GT * P
NG = EDGES // GE
MISH_CLAMP = 20.0
LEAD = 2
MASKED = -1.0e30


def after(eng, sem, value):
    if isinstance(value, int) and value <= 0:
        return
    eng.wait_ge(sem, value)


def at(t, width):
    return bass.ds(t * width, width)


class Keep:
    pass


class Core:

    def __init__(self, nc, ctx):
        self.nc, self.ctx = nc, ctx

    def sb(self, name, shape, dt=F32, ctx=None):
        return (ctx or self.ctx).enter_context(self.nc.sbuf_tensor(name, shape, dt))

    def ps(self, name, shape, dt=F32, ctx=None):
        return (ctx or self.ctx).enter_context(self.nc.psum_tensor(name, shape, dt))

    def sem(self, name):
        return self.nc.alloc_semaphore(name=name)

    def stage(self, body, *args):
        with self.nc.cleanup_on_exit():
            body(self.nc, self, *args)


def layer_norm_stats(dve, x, stats, mv, var_eps, eps, s_stats, s_mv, s_var, s_gate, n):
    dve.bn_stats(stats, x).then_inc(s_stats, 1)
    dve.wait_ge(s_stats, n + 1)
    dve.sem_inc(s_gate, 1)
    dve.bn_aggr(mv, stats).then_inc(s_mv, 1)
    dve.wait_ge(s_mv, n + 1)
    dve.tensor_scalar(var_eps, mv[:, 1:2], eps, None, ALU.add).then_inc(s_var, 1)


def node_products(nc, core, a, keep):
    with ExitStack() as ctx:
        sb = lambda n, s, d=F32: core.sb(n, s, d, ctx)
        ps = lambda n, s, d=F32: core.ps(n, s, d, ctx)
        sem = lambda n: core.sem(n)
        w_src, w_dst, w_self = (sb(n, [128, KC, D]) for n in ("w_src", "w_dst", "w_self"))
        b3_rows = sb("b3_rows", [P, D])
        xn = sb("xn_cur", [P, 2, D])
        xnT = sb("xnT_cur", [128, 2, KC, P])
        ends = sb("ends_cur", [P, 2, 2, D])
        stats, mv = sb("p1_stats", [P, 2, 6]), sb("p1_mv", [P, 2, 2])
        var_eps, rstd = sb("p1_var", [P, 2, 1]), sb("p1_rstd", [P, 2, 1])
        dst_rows, extent = sb("dst_rows", [NG, GE], I32), sb("extent", [NG, 2])
        extents = sb("extents", [NT, NG, 2])
        gmax, gmin = extents[:, :, 0], extents[:, :, 1]
        hit, tmp = (sb(n, [NT, NG]) for n in ("hit", "tmp_r"))
        thr, gidx = sb("thr", [NT, 2]), sb("gidx", [NT, NG])
        bounds, bounds_i = sb("bounds", [NT, 2]), sb("bounds_i", [NT, 2])
        row, row_len = sb("bounds_row", [1, 2 * NT]), sb("len_row", [1, NT])
        cum = sb("cum_row", [1, NT])
        ones_row = sb("ones_row", [1, NT])
        pT = ps("p1_T", [128, 2, 512])
        pE = ps("p1_E", [P, 2, 2, 512])
        pS = ps("p1_S", [P, 2, 512])
        x_in, w_in, dst_in, row_in = sem("p1_x_in"), sem("p1_w_in"), sem("p1_dst_in"), sem("p1_row_in")
        src_w_in, dst_w_in, first_x_in = sem("p1_src_w_in"), sem("p1_dst_w_in"), sem("p1_first_x_in")
        consts, s_stats, s_mv, s_var, s_rstd, s_xn, gate = (sem("p1_" + n) for n in
            ("consts", "stats", "mv", "var", "rstd", "xn", "gate"))
        s_kept, s_T, s_xT, s_prod, s_ends, s_self = (sem("p1_" + n) for n in ("kept", "T", "xT", "prod", "ends", "self"))
        s_out = [sem("p1_out0"), sem("p1_out1")]
        s_extent, extent_out, extent_in = sem("p1_extent"), sem("p1_extent_out"), sem("p1_extent_in")
        s_rng, s_bounds = sem("p1_rng"), sem("p1_bounds")
        block = ctx.enter_context(nc.Block())

        @block.sync
        def _(sp):
            for s in (s_stats, s_mv, s_var, s_rstd, s_xn, s_kept, s_T, s_xT, s_prod, s_ends, s_self):
                sp.sem_inc(s, LEAD)
            for s in s_out:
                sp.sem_inc(s, 16)
            for w, r, s, t0, t1, x_sem in ((w_src, 0, src_w_in, 0, 2, first_x_in), (w_dst, D, dst_w_in, 2, NT, x_in)):
                sp.dma_start(keep.x[:, t0 * D:t1 * D].rearrange("p (t d) -> p t d", d=D),
                             a["x"][t0 * P:t1 * P, :].rearrange("(t p) d -> p t d", p=P)).then_inc(x_sem, 16)
                sp.dma_start(w[:, :, :], a["L0_gnn_W1"][r:r + D, :].rearrange("(k p) n -> p k n", p=128)).then_inc(s, 16)
            sp.dma_start(w_self[:, :, :], a["L0_gnn_W3"][0:D, :].rearrange("(k p) n -> p k n", p=128)).then_inc(w_in, 16)
            sp.dma_start(b3_rows[:, :], a["L0_gnn_b3"].rearrange("(a n) -> a n", a=1).broadcast_to([P, D])).then_inc(w_in, 16)
            with sp.Fori(0, NT // 2) as i:
                for u in range(2):
                    t = 2 * i + u
                    sp.wait_ge(s_ends, LEAD + t + 1)
                    sp.dma_start(keep.ends_dram[bass.ds(t * P, P), :, :], ends[:, u, :, :]).then_inc(s_out[u], 16)
            for u in range(2):
                sp.wait_ge(s_out[u], 16 * NT // 2 + 16)

        @block.scalar
        def _(act):
            act.dma_start(dst_rows[:, :], a["dst"].rearrange("(g e) -> g e", g=NG)).then_inc(dst_in, 16)
            act.dma_start(keep.src_i[:, :], a["src_cols"]).then_inc(dst_in, 16)
            act.dma_start(keep.dst_i[:, :], a["dst_cols"]).then_inc(dst_in, 16)
            act.wait_ge(s_extent, 2)
            act.dma_start(keep.extent_dram, extent[:, :]).then_inc(extent_out, 16)
            act.wait_ge(extent_out, 16)
            act.dma_start(extents[:, :, :].rearrange("n g c -> n (g c)"),
                          keep.extent_dram.rearrange("g c -> (g c)").rearrange("(a e) -> a e", a=1).broadcast_to([NT, 2 * NG])
                          ).then_inc(extent_in, 16)
            with act.Fori(0, NT // 2) as i:
                for u in range(2):
                    t = 2 * i + u
                    act.wait_ge(s_T, LEAD + t + 1)
                    act.wait_ge(s_prod, LEAD + t)
                    act.activation(xnT[:, u, :, :].rearrange("p k m -> p (k m)"), pT[:, u, 0:KC * P], ACT.Copy).then_inc(s_xT, 1)
                for u in range(2):
                    t = 2 * i + u
                    act.wait_ge(s_prod, LEAD + t + 1)
                    act.wait_ge(s_out[u], 16 * i + 16)
                    act.activation(ends[:, u, :, :].rearrange("p a n -> p (a n)"), pE[:, u, :, :].rearrange("p a n -> p (a n)"),
                                   ACT.Copy).then_inc(s_ends, 1)
            act.wait_ge(s_bounds, 1)
            act.dma_start(row[:, :].rearrange("a (n c) -> a n c", c=2), bounds[:, :]).then_inc(row_in, 16)
            act.wait_ge(row_in, 16)

        @block.gpsimd
        def _(pool):
            pool.memset(keep.ident[:, :], 0.0).then_inc(consts, 1)
            pool.memset(keep.minus_half[:, :], -0.5).then_inc(consts, 1)
            pool.iota(keep.node_id[:, :], pattern=[[1, NODES]], base=0, channel_multiplier=0,
                      allow_small_or_imprecise_dtypes=True).then_inc(consts, 1)
            pool.iota(keep.node_id16[:, :], pattern=[[1, NODES]], base=0, channel_multiplier=0,
                      allow_small_or_imprecise_dtypes=True).then_inc(consts, 1)
            pool.iota(thr[:, 0:1], pattern=[[0, 1]], base=0, channel_multiplier=P,
                      allow_small_or_imprecise_dtypes=True).then_inc(consts, 1)
            pool.iota(thr[:, 1:2], pattern=[[0, 1]], base=P, channel_multiplier=P,
                      allow_small_or_imprecise_dtypes=True).then_inc(consts, 1)
            pool.iota(gidx[:, :], pattern=[[1, NG]], base=0, channel_multiplier=0,
                      allow_small_or_imprecise_dtypes=True).then_inc(consts, 1)
            pool.memset(ones_row[:, :], 1.0).then_inc(consts, 1)
            pool.wait_ge(consts, 8)
            pool.affine_select(out=keep.ident[:, :], in_=keep.ident[:, :], compare_op=ALU.not_equal, fill=1.0, base=0,
                               pattern=[[-1, 128]], channel_multiplier=1).then_inc(consts, 1)
            with pool.Fori(0, NT // 2) as i:
                for u in range(2):
                    t = 2 * i + u
                    pool.wait_ge(s_var, LEAD + t + 1)
                    pool.tensor_tensor(rstd[:, u, :], var_eps[:, u, :], keep.minus_half[:, :], ALU.pow).then_inc(s_rstd, 1)

        @block.tensor
        def _(pe):
            pe.wait_ge(consts, 9)
            with pe.Fori(0, NT // 2) as i:
                for u in range(2):
                    t = 2 * i + u
                    pe.wait_ge(s_xn, LEAD + t + 1)
                    pe.wait_ge(s_xT, LEAD + t)
                    for k in range(KC):
                        mm = pe.transpose(pT[:, u, k * P:(k + 1) * P], xn[:, u, k * 128:(k + 1) * 128], keep.ident[0:P, 0:P])
                    mm.then_inc(s_T, 1)
                for u in range(2):
                    t = 2 * i + u
                    pe.wait_ge(s_xT, LEAD + t + 1)
                    pe.wait_ge(s_ends, LEAD + t - 1)
                    pe.wait_ge(s_self, LEAD + t - 1)
                    for w, w_sem, n, o in ((w_src, src_w_in, 16, pE[:, u, 0, :]), (w_dst, dst_w_in, 16, pE[:, u, 1, :]),
                                           (w_self, w_in, 32, pS[:, u, :])):
                        pe.wait_ge(w_sem, n)
                        for k in range(KC):
                            mm = pe.matmul(o, xnT[:, u, k, :], w[:, k, :], start=(k == 0), stop=(k == KC - 1))
                    mm.then_inc(s_prod, 1)

        @block.vector
        def _(dve):
            chain = [0]

            def step(ins):
                chain[0] += 1
                ins.then_inc(s_rng, 1)
                dve.wait_ge(s_rng, chain[0])

            def normalise(i):
                for u in range(2):
                    t = 2 * i + u
                    layer_norm_stats(dve, keep.x[:, at(t, D)], stats[:, u, :], mv[:, u, :], var_eps[:, u, :], 1e-5,
                                     s_stats, s_mv, s_var, gate, LEAD + t)
                for u in range(2):
                    t = 2 * i + u
                    dve.wait_ge(s_rstd, LEAD + t + 1)
                    dve.wait_ge(s_T, LEAD + t - 1)
                    dve.wait_ge(s_kept, LEAD + t - 1)
                    dve.tensor_scalar(xn[:, u, :], keep.x[:, at(t, D)], mv[:, u, 0:1], rstd[:, u, :],
                                      ALU.subtract, ALU.mult).then_inc(s_xn, 1)
                for u in range(2):
                    t = 2 * i + u
                    dve.wait_ge(s_xn, LEAD + t + 1)
                    dve.tensor_copy(keep.xn[:, at(t, D)], xn[:, u, :]).then_inc(s_kept, 1)

            def own_part(i):
                for u in range(2):
                    t = 2 * i + u
                    dve.wait_ge(s_prod, LEAD + t + 1)
                    dve.tensor_tensor(keep.self_in[:, at(t, D)], pS[:, u, :], b3_rows[:, :], ALU.add).then_inc(s_self, 1)

            dve.wait_ge(first_x_in, 16)
            normalise(0)
            dve.wait_ge(dst_in, 48)
            dve.wait_ge(consts, 9)
            dve.wait_ge(x_in, 16)
            step(dve.tensor_copy(keep.src_f[:, :], keep.src_i[:, :]))
            step(dve.tensor_copy(keep.dst_f[:, :], keep.dst_i[:, :]))
            step(dve.tensor_scalar(keep.src_i[:, :], keep.src_f[:, :], 2.0, None, ALU.mult))
            step(dve.tensor_scalar(keep.dst_i[:, :], keep.dst_f[:, :], 2.0, 1.0, ALU.mult, ALU.add))
            dve.tensor_reduce(extent[:, 0:1], dst_rows[:, :], AX_X, ALU.max).then_inc(s_extent, 1)
            dve.tensor_reduce(extent[:, 1:2], dst_rows[:, :], AX_X, ALU.min).then_inc(s_extent, 1)
            dve.wait_ge(extent_in, 16)
            step(dve.tensor_scalar(tmp[:, :], gmin, thr[:, 1:2], None, ALU.is_lt))
            step(dve.scalar_tensor_tensor(hit[:, :], gmax, thr[:, 0:1], tmp[:, :], ALU.is_ge, ALU.mult))
            step(dve.scalar_tensor_tensor(tmp[:, :], gidx[:, :], 1.0, hit[:, :], ALU.add, ALU.mult))
            step(dve.tensor_reduce(bounds[:, 1:2], tmp[:, :], AX_X, ALU.max))
            step(dve.tensor_scalar(bounds[:, 1:2], bounds[:, 1:2], 1.0, None, ALU.max))
            step(dve.tensor_scalar(hit[:, :], hit[:, :], -1000.0, 1000.0, ALU.mult, ALU.add))
            step(dve.tensor_tensor(tmp[:, :], gidx[:, :], hit[:, :], ALU.add))
            step(dve.tensor_reduce(bounds[:, 0:1], tmp[:, :], AX_X, ALU.min))
            step(dve.tensor_scalar(bounds_i[:, 0:1], bounds[:, 1:2], -1.0, None, ALU.add))
            dve.tensor_tensor(bounds[:, 0:1], bounds[:, 0:1], bounds_i[:, 0:1], ALU.min).then_inc(s_bounds, 1)

            with dve.Fori(0, NT // 2 - 1) as i:
                normalise(i + 1)
                own_part(i)
            own_part(NT // 2 - 1)
            dve.wait_ge(row_in, 16)
            lo, hi = (row[:, :].rearrange("a (n c) -> a n c", c=2)[:, :, c] for c in (0, 1))
            step(dve.tensor_tensor(row_len[:, :], hi, lo, ALU.subtract))
            step(dve.tensor_tensor_scan(cum[:, :], ones_row[:, :], row_len[:, :], 0.0, ALU.mult, ALU.add))
            step(dve.tensor_tensor(cum[:, :], cum[:, :], hi, ALU.subtract))
            step(dve.tensor_copy(keep.ranges[:, 0:NT], lo))
            step(dve.tensor_copy(keep.ranges[:, NT:2 * NT], hi))
            step(dve.tensor_scalar(keep.ranges[:, 2 * NT:3 * NT], cum[:, :], float(NG), None, ALU.add))


def edge_messages(nc, core, a, keep):
    with ExitStack() as ctx:
        sb = lambda n, s, d=F32: core.sb(n, s, d, ctx)
        sem = lambda n: core.sem("p2_" + n)
        w_attr_raw, w_attr = sb("w_attr_raw", [2 * EDGE_DIM, D]), sb("w_attr", [2 * EDGE_DIM, D], F32R)
        w2 = sb("w2", [128, KC, D])
        b1_col, b2_rows = sb("b1_col", [128, KC]), sb("b2_rows", [P, D])
        idx_src, idx_dst = (sb(n, [P, 2, GT], I32) for n in ("idx_src", "idx_dst"))
        at_src, at_dst = (sb(n, [P, 2, GT, D]) for n in ("at_src", "at_dst"))
        attr = sb("attr", [2 * EDGE_DIM, 2, GE])
        attr_high, attr_low = sb("attr_high", [2 * EDGE_DIM, 2, GE], F32R), sb("attr_low", [EDGE_DIM, 2, GE], F32R)
        pre1, th1 = sb("pre1", [128, 2, KC, GE]), sb("th1", [128, KC, GE])
        pre2, th2 = sb("pre2", [P, 2, GT, D]), sb("th2", [P, GT, D])
        pA = core.ps("p2_A", [128, KC, 512], F32, ctx)
        pB = core.ps("p2_B", [P, GT, 512], F32, ctx)
        w_in, s_idx, s_gate, s_ends = sem("w_in"), sem("idx"), sem("gate"), sem("ends_added")
        s_rows = [sem("rows0"), sem("rows1")]
        s_attr = [sem("attr0"), sem("attr1")]
        s_out = [sem("out0"), sem("out1")]
        s_A, s_preA, s_clA, s_expA, s_lnA, s_tanhA, s_hid = (
            sem(n) for n in ("A", "preA", "clampA", "expA", "lnA", "tanhA", "hidden"))
        s_B, s_preB, s_clB, s_expB, s_lnB, s_tanhB, s_msg = (
            sem(n) for n in ("B", "preB", "clampB", "expB", "lnB", "tanhB", "message"))
        s_w_attr, s_split = sem("w_attr"), sem("attr_split")
        ROWS = 16 * 2 * GT
        no_rows, s_none, s_filled = sb("no_rows", [P, D]), sem("none"), sem("filled")
        block = ctx.enter_context(nc.Block())

        def steps(eng, step):
            for g in range(4):
                step(g, g % 2, g // 2)
            with eng.Fori(2, NG // 2 - 1) as i:
                for u in range(2):
                    step(2 * i + u, u, i)
            for g in range(NG - 2, NG + 3):
                step(g, g % 2, g // 2)

        def in_a(g):
            return not isinstance(g, int) or g < NG

        def in_b(g):
            return not isinstance(g, int) or 1 <= g <= NG

        def in_c(g):
            return not isinstance(g, int) or 2 <= g < NG + 2

        def in_d(g):
            return not isinstance(g, int) or g >= 3

        @block.sync
        def _(sp):
            sp.sem_inc(s_msg, 1)
            for s in s_out:
                sp.sem_inc(s, 16)
            for h in range(2):
                sp.dma_start(w_attr_raw[h * EDGE_DIM:(h + 1) * EDGE_DIM, :], a["L0_gnn_W1"][2 * D:2 * D + EDGE_DIM, :]).then_inc(w_in, 16)
            sp.dma_start(w2[:, :, :], a["L0_gnn_W2"].rearrange("(k p) n -> p k n", p=128)).then_inc(w_in, 16)
            sp.dma_start(b1_col[:, :], a["b1_cols"]).then_inc(w_in, 16)
            sp.dma_start(b2_rows[:, :], a["L0_gnn_b2"].rearrange("(a n) -> a n", a=1).broadcast_to([P, D])).then_inc(w_in, 16)

            def attributes(g, u):
                after(sp, s_split, 2 * (g - 1))
                for h in range(2):
                    sp.dma_start(attr[h * EDGE_DIM:(h + 1) * EDGE_DIM, u, :], a["attr_T"][:, at(g, GE)]).then_inc(s_attr[u], 16)

            def step(g, u, half):
                if not isinstance(g, int) or g + 1 < NG:
                    attributes(g + 1, 1 - u)
                if in_d(g):
                    sp.wait_ge(s_msg, g - 2 + 1)
                    sp.dma_start(keep.msg_dram[at(g - 3, GE), :].rearrange("(j p) n -> p j n", p=P),
                                 pre2[:, 1 - u, :, :]).then_inc(s_out[1 - u], 16)
                if in_a(g):
                    fill(g)

            def fill(g):
                for rows, first, n in ((keep.slots_dram, 0, ROW_FILL), (keep.results_dram, FIRST_FILL, RESULT_FILL)):
                    sp.dma_start(rows[bass.ds(g * n + first, n), :], no_rows[0:n, :]).then_inc(s_filled, 16)

            attributes(0, 0)
            sp.wait_ge(s_none, 1)
            steps(sp, step)
            for u in range(2):
                sp.wait_ge(s_out[u], 16 * NG // 2 + 16)
            sp.wait_ge(s_filled, 16 * 2 * NG)

        @block.gpsimd
        def _(pool):
            pool.memset(no_rows[:, :], 0.0).then_inc(s_none, 1)
            rows = keep.ends_dram.rearrange("n a d -> (n a) d")

            def step(g, u, half):
                if not in_a(g):
                    return
                after(pool, s_rows[u], ROWS * half)
                pool.sem_inc(s_gate, 1)
                pool.tensor_copy(idx_src[:, u, :], keep.src_i[:, at(g, GT)]).then_inc(s_idx, 1)
                pool.tensor_copy(idx_dst[:, u, :], keep.dst_i[:, at(g, GT)]).then_inc(s_idx, 1)
                pool.wait_ge(s_idx, 2 * g + 2)
                pool.sem_inc(s_gate, 1)
                after(pool, s_A, g - 1)
                pool.sem_inc(s_gate, 1)
                for j in range(GT):
                    for to, idx in ((at_src, idx_src), (at_dst, idx_dst)):
                        pool.indirect_dma_start(to[:, u, j, :], None, rows,
                                                bass.IndirectOffsetOnAxis(ap=idx[:, u, j:j + 1], axis=0)
                                                ).then_inc(s_rows[u], 16)
                pool.wait_ge(s_attr[u], 32 * half + 32)
                pool.sem_inc(s_gate, 1)
                pool.tensor_copy(attr_high[:, u, :], attr[:, u, :]).then_inc(s_split, 1)
                pool.wait_ge(s_split, 2 * g + 1)
                pool.tensor_tensor(attr_low[:, u, :], attr[0:EDGE_DIM, u, :], attr_high[0:EDGE_DIM, u, :].bitcast(F32),
                                   ALU.subtract).then_inc(s_split, 1)

            steps(pool, step)

        @block.scalar
        def _(act):
            def step(g, u, half):
                if in_a(g):
                    act.wait_ge(s_clA, g + 1)
                    act.activation(th1[:, :, :], th1[:, :, :], ACT.Exp).then_inc(s_expA, 1)
                    act.wait_ge(s_expA, g + 1)
                    act.activation(th1[:, :, :], th1[:, :, :], ACT.Ln, bias=1.0).then_inc(s_lnA, 1)
                    act.wait_ge(s_lnA, g + 1)
                    act.activation(th1[:, :, :], th1[:, :, :], ACT.Tanh).then_inc(s_tanhA, 1)
                if in_c(g):
                    act.wait_ge(s_clB, g - 1)
                    act.activation(th2[:, :, :], th2[:, :, :], ACT.Exp).then_inc(s_expB, 1)
                    act.wait_ge(s_expB, g - 1)
                    act.activation(th2[:, :, :], th2[:, :, :], ACT.Ln, bias=1.0).then_inc(s_lnB, 1)
                    act.wait_ge(s_lnB, g - 1)
                    act.activation(th2[:, :, :], th2[:, :, :], ACT.Tanh).then_inc(s_tanhB, 1)

            act.wait_ge(w_in, 80)
            act.activation(w_attr[:, :], w_attr_raw[:, :], ACT.Copy).then_inc(s_w_attr, 1)
            steps(act, step)

        @block.tensor
        def _(pe):
            def step(g, u, half):
                if in_a(g):
                    after(pe, s_preA, KC * g)
                    pe.wait_ge(s_split, 2 * g + 2)
                    pe.wait_ge(s_ends, g + 1)
                    for f in range(KC):
                        for j in range(GT):
                            pe.matmul(pA[:, f, j * P:(j + 1) * P], at_src[:, u, j, f * 128:(f + 1) * 128],
                                      keep.ident[0:P, 0:P], start=(j == 0), stop=False,
                                      is_transpose=True, skip_group_check=True)
                        pe.matmul(pA[:, f, 0:GE], w_attr[:, f * 128:(f + 1) * 128], attr_high[:, u, :],
                                  start=False, stop=False, skip_group_check=True)
                        mm = pe.matmul(pA[:, f, 0:GE], w_attr[0:EDGE_DIM, f * 128:(f + 1) * 128], attr_low[:, u, :],
                                       start=False, stop=True, skip_group_check=True)
                    mm.then_inc(s_A, 1)
                if in_b(g):
                    pe.wait_ge(s_hid, g)
                    for j in range(GT):
                        after(pe, s_preB, GT * (g - 2) + j + 1)
                        for k in range(KC):
                            mm = pe.matmul(pB[:, j, :], pre1[:, 1 - u, k, j * P:(j + 1) * P], w2[:, k, :],
                                           start=(k == 0), stop=(k == KC - 1))
                        mm.then_inc(s_B, 1)

            pe.wait_ge(w_in, 80)
            pe.wait_ge(s_w_attr, 2)
            steps(pe, step)

        @block.vector
        def _(dve):
            def add_ends(g, u, half):
                dve.wait_ge(s_rows[u], ROWS * half + ROWS)
                dve.tensor_tensor(at_src[:, u, :, :], at_src[:, u, :, :], at_dst[:, u, :, :], ALU.add).then_inc(s_ends, 1)

            def step(g, u, half):
                if in_c(g):
                    dve.wait_ge(s_out[u], 16 * half)
                    for j in range(GT):
                        dve.wait_ge(s_B, GT * (g - 2) + j + 1)
                        dve.tensor_tensor(pre2[:, u, j, :], pB[:, j, :], b2_rows[:, :], ALU.add).then_inc(s_preB, 1)
                if in_a(g):
                    after(dve, s_B, GT * (g - 1))
                    dve.wait_ge(s_A, g + 1)
                    for f in range(KC):
                        dve.tensor_scalar(pre1[:, u, f, :], pA[:, f, 0:GE], b1_col[:, f:f + 1], None, ALU.add).then_inc(s_preA, 1)
                    dve.wait_ge(s_preA, KC * g + KC)
                    after(dve, s_hid, g)
                    dve.tensor_scalar(th1[:, :, :], pre1[:, u, :, :], MISH_CLAMP, None, ALU.min).then_inc(s_clA, 1)
                if in_d(g):
                    dve.wait_ge(s_tanhB, g - 2)
                    dve.tensor_tensor(pre2[:, 1 - u, :, :], pre2[:, 1 - u, :, :], th2[:, :, :], ALU.mult).then_inc(s_msg, 1)
                if in_c(g):
                    dve.wait_ge(s_preB, GT * (g - 1))
                    dve.wait_ge(s_msg, g - 2 + 1)
                    dve.tensor_scalar(th2[:, :, :], pre2[:, u, :, :], MISH_CLAMP, None, ALU.min).then_inc(s_clB, 1)
                if not isinstance(g, int) or g + 1 < NG:
                    add_ends(g + 1, 1 - u, half + u)
                if in_a(g):
                    dve.wait_ge(s_tanhA, g + 1)
                    dve.tensor_tensor(pre1[:, u, :, :], pre1[:, u, :, :], th1[:, :, :], ALU.mult).then_inc(s_hid, 1)

            dve.wait_ge(w_in, 80)
            dve.wait_ge(s_w_attr, 1)
            low = slice(EDGE_DIM, 2 * EDGE_DIM)
            dve.tensor_tensor(w_attr[low, :], w_attr_raw[low, :], w_attr[low, :].bitcast(F32), ALU.subtract).then_inc(s_w_attr, 1)
            add_ends(0, 0, 0)
            steps(dve, step)


def segment_sums(nc, core, a, keep):
    with ExitStack() as ctx:
        sb = lambda n, s, d=F32: core.sb(n, s, d, ctx)
        sem = lambda n: core.sem("seg_" + n)
        msg = sb("msg_cur", [P, GT, D])
        parts = sb("msg_parts", [P, 2, GT, D], F32R)
        hot = sb("hot_dst", [P, GT, P], F32R)
        hot16 = sb("hot_dst16", [P, GT, P], BF16)
        src16 = sb("hot_src16", [P, GT, NODES], BF16)
        zeros = sb("zeros16", [1, 512], BF16)
        sums = core.ps("p_sums", [P, 2, 512], F32, ctx)
        pairs = core.ps("p_pairs", [P, 2, 3, 512], F32, ctx)
        s_in = [sem(f"in{j}") for j in range(GT)]
        s_high = sem("high")
        s_low_pool, s_low_dve = sem("low_pool"), sem("low_dve")
        ON_POOL = GT - 1
        s_hot, s_seg, s_tile, s_read, s_zero = (sem(n) for n in ("hot", "seg", "tile", "read", "zero"))
        block = ctx.enter_context(nc.Block())

        def low_made(eng, v, j):
            if j < ON_POOL:
                eng.wait_ge(s_low_pool, ON_POOL * v + j + 1)
            else:
                eng.wait_ge(s_low_dve, v + 1)

        def make_low(eng, v, j, done):
            eng.wait_ge(s_high, GT * v + j + 1)
            eng.tensor_tensor(parts[:, 1, j, :], msg[:, j, :], parts[:, 0, j, :].bitcast(F32), ALU.subtract).then_inc(done, 1)

        def visits(eng, body, before=None, behind=None):
            with eng.Fori(0, NT // 2) as i:
                for u in range(2):
                    n = 2 * i + u
                    first = eng.value_load(keep.ranges[0:1, bass.ds(n, 1)], min_val=0, max_val=NG - 1)
                    last = eng.value_load(keep.ranges[0:1, bass.ds(n + NT, 1)], min_val=1, max_val=NG)
                    seen = eng.value_load(keep.ranges[0:1, bass.ds(n + 2 * NT, 1)], min_val=0, max_val=NG * (NT + 1))
                    if before:
                        before(n, u)
                    with eng.Fori(first, last) as g:
                        body(n, u, g, g + seen)
                    if behind:
                        behind(n, u)

        @block.sync
        def _(sp):
            sp.sem_inc(s_seg, GT * NG + GT)
            sp.sem_inc(s_hot, 3 * GT * NG)
            for s in s_in:
                sp.sem_inc(s, 16 * NG)
            sp.sem_inc(s_high, GT * NG)
            sp.sem_inc(s_low_pool, ON_POOL * (NG + 1))
            sp.sem_inc(s_low_dve, NG + 1)
            sp.sem_inc(s_read, 2)

            def body(n, u, g, v):
                for j in range(GT):
                    low_made(sp, v, j)
                    sp.dma_start(msg[:, j, :], keep.msg_dram[at(GT * g + j, P), :]).then_inc(s_in[j], 16)

            visits(sp, body)

        @block.gpsimd
        def _(pool):
            def body(n, u, g, v):
                for j in range(ON_POOL):
                    make_low(pool, v, j, s_low_pool)

            visits(pool, body)

        @block.vector
        def _(dve):
            dve.memset(zeros[:, :], 0.0).then_inc(s_zero, 1)

            def body(n, u, g, v):
                for j in range(GT):
                    dve.wait_ge(s_seg, GT * v + j + 1)
                    dst = keep.dst_f[:, bass.ds(GT * g + j, 1)]
                    dve.tensor_scalar(hot[:, j, :], keep.node_id[:, at(n, P)], dst, None, ALU.is_equal).then_inc(s_hot, 1)
                    dve.tensor_scalar(hot16[:, j, :], keep.node_id[:, at(n, P)], dst, None, ALU.is_equal).then_inc(s_hot, 1)
                    dve.tensor_scalar(src16[:, j, :], keep.node_id16[:, :], keep.src_f[:, bass.ds(GT * g + j, 1)], None,
                                      ALU.is_equal).then_inc(s_hot, 1)
                for j in range(ON_POOL, GT):
                    make_low(dve, v, j, s_low_dve)

            visits(dve, body)

        @block.tensor
        def _(pe):
            pe.wait_ge(s_zero, 1)

            def clear(n, u):
                pe.wait_ge(s_read, n + 1)
                for bank in (sums[:, u, :], *(pairs[:, u, b, :] for b in range(3))):
                    pe.matmul(bank, zeros[0:1, 0:P], zeros[0:1, :], start=True, stop=False, skip_group_check=True)

            def body(n, u, g, v):
                for j in range(GT):
                    pe.wait_ge(s_hot, 3 * (GT * v + j + 1))
                    for s in range(NT):
                        pe.matmul(pairs[:, u, s // 4, (s % 4) * P:(s % 4 + 1) * P], src16[:, j, s * P:(s + 1) * P],
                                  hot16[:, j, :], start=False, stop=False, skip_group_check=True)
                    low_made(pe, v + 1, j)
                    for part in range(2):
                        mm = pe.matmul(sums[:, u, :], hot[:, j, :], parts[:, part, j, :], start=False, stop=False, skip_group_check=True)
                    mm.then_inc(s_seg, 1)

            def close(n, u):
                for bank in (sums[:, u, :], *(pairs[:, u, b, :] for b in range(3))):
                    mm = pe.matmul(bank, zeros[0:1, 0:P], zeros[0:1, :], start=False, stop=True, skip_group_check=True)
                mm.then_inc(s_tile, 1)

            visits(pe, body, clear, close)

        @block.scalar
        def _(act):
            def high(n, u, g, v):
                for j in range(GT):
                    act.wait_ge(s_in[j], 16 * v + 16)
                    act.wait_ge(s_seg, GT * v + j + 1)
                    act.activation(parts[:, 0, j, :], msg[:, j, :], ACT.Copy).then_inc(s_high, 1)

            def evacuate(n, u):
                act.wait_ge(s_tile, n + 1)
                act.activation(keep.agg[0:P, at(n, D)], sums[:, u, :], ACT.Copy)
                for b, tiles in ((0, 4), (1, 4), (2, 2)):
                    copy = act.activation(keep.log_pairs[:, 4 * b:4 * b + tiles, at(n, P)],
                                          pairs[:, u, b, 0:tiles * P].rearrange("p (s d) -> p s d", d=P), ACT.Copy)
                copy.then_inc(s_read, 1)

            visits(act, high, behind=evacuate)


def bcast(v, rows=P):
    return v.rearrange("(a n) -> a n", a=1).broadcast_to([rows, v.shape[0]])


def weight_rows(w):
    return w.rearrange("(k p) n -> p k n", p=128)


def node_update(nc, core, a, keep):
    with ExitStack() as ctx:
        sb = lambda n, s, d=F32: core.sb(n, s, d, ctx)
        sem = lambda n: core.sem("p3_" + n)
        w3, w4 = sb("w3_agg", [128, KC, D]), sb("w4", [128, KC, D])
        b4, gamma, beta = sb("b4_rows", [P, D]), sb("gamma_rows", [P, D]), sb("beta_rows", [P, D])
        cur, curT = sb("p3_cur", [P, 2, D]), sb("p3_curT", [128, 2, KC, P])
        y = sb("p3_y", [P, 2, D])
        stats, mv = sb("p3_stats", [P, 2, 6]), sb("p3_mv", [P, 2, 2])
        var_eps, rstd = sb("p3_var", [P, 2, 1]), sb("p3_rstd", [P, 2, 1])
        pT = core.ps("p3_T", [128, 2, 512], F32, ctx)
        pU = core.ps("p3_U", [P, 2, 512], F32, ctx)
        w_in = sem("w_in")
        s_cur, s_T, s_curT, s_U, s_pre, s_sum, s_bias = (sem(n) for n in ("cur", "T", "curT", "U", "pre", "sum", "bias"))
        s_clamp, s_exp, s_ln, s_tanh, s_mish = (sem(n) for n in ("clamp", "exp", "ln", "tanh", "mish"))
        s_stats, s_mv, s_var, gate, s_rstd, s_y = (sem(n) for n in ("stats", "mv", "var", "gate", "rstd", "y"))
        block = ctx.enter_context(nc.Block())
        HALF = NT // 2 * D

        def pairs(eng, *stages, base=0):
            with eng.Fori(0, NT // 2) as i:
                for stage in stages:
                    for u in range(2):
                        stage(2 * i + u, u, 2 * i + u + base)

        @block.sync
        def _(sp):
            for s in (s_T, s_curT, s_U, s_pre, s_stats, s_mv, s_var, s_y, s_cur):
                sp.sem_inc(s, LEAD)
            sp.dma_start(w3[:, :, :], weight_rows(a["L0_gnn_W3"][D:2 * D, :])).then_inc(w_in, 16)
            sp.dma_start(w4[:, :, :], weight_rows(a["L0_gnn_W4"])).then_inc(w_in, 16)
            for rows, name in ((b4, "b4"), (gamma, "gamma"), (beta, "beta")):
                sp.dma_start(rows[:, :], bcast(a["L0_gnn_" + name])).then_inc(w_in, 16)

        @block.gpsimd
        def _(pool):
            pool.wait_ge(w_in, 80)

            def biases(t, u, c):
                pool.tensor_tensor(keep.xn[:, at(t, D)], keep.xn[:, at(t, D)], b4[:, :], ALU.add).then_inc(s_bias, 1)
                pool.tensor_tensor(keep.x[:, at(t, D)], keep.x[:, at(t, D)], beta[:, :], ALU.add).then_inc(s_bias, 1)

            def power(t, u, c):
                pool.wait_ge(s_var, LEAD + t + 1)
                pool.tensor_tensor(rstd[:, u, :], var_eps[:, u, :], keep.minus_half[:, :], ALU.pow).then_inc(s_rstd, 1)

            pairs(pool, biases)
            pairs(pool, power)

        @block.scalar
        def _(act):
            def take(rows):
                def stage(t, u, c):
                    act.wait_ge(s_T, LEAD + c - 1)
                    act.activation(cur[:, u, :], rows[:, at(t, D)], ACT.Copy).then_inc(s_cur, 1)
                return stage

            pairs(act, take(keep.agg[0:P, :]))
            for func, before, done, bias in ((ACT.Exp, s_clamp, s_exp, 0.0), (ACT.Ln, s_exp, s_ln, 1.0), (ACT.Tanh, s_ln, s_tanh, 0.0)):
                for h in range(2):
                    act.wait_ge(before, h + 1)
                    part = keep.agg[0:P, h * HALF:(h + 1) * HALF]
                    act.activation(part, part, func, bias=bias).then_inc(done, 1)
            act.wait_ge(s_mish, 2)

            def evacuate(t, u, c):
                act.wait_ge(s_T, LEAD + c + 1)
                act.wait_ge(s_U, LEAD + c - 1)
                act.activation(curT[:, u, :, :].rearrange("p k m -> p (k m)"), pT[:, u, 0:KC * P], ACT.Copy).then_inc(s_curT, 1)

            pairs(act, take(keep.self_in), evacuate, base=NT)

        @block.tensor
        def _(pe):
            pe.wait_ge(w_in, 80)

            def transposes(t, u, c):
                pe.wait_ge(s_cur, LEAD + c + 1)
                pe.wait_ge(s_curT, LEAD + c - 1)
                for k in range(KC):
                    mm = pe.transpose(pT[:, u, k * P:(k + 1) * P], cur[:, u, k * 128:(k + 1) * 128], keep.ident[0:P, 0:P])
                mm.then_inc(s_T, 1)

            def product(w):
                def stage(t, u, c):
                    pe.wait_ge(s_curT, LEAD + c + 1)
                    pe.wait_ge(s_pre, LEAD + c - 1)
                    for k in range(KC):
                        mm = pe.matmul(pU[:, u, :], curT[:, u, k, :], w[:, k, :], start=(k == 0), stop=(k == KC - 1))
                    mm.then_inc(s_U, 1)
                return stage

            pairs(pe, transposes, product(w3))
            pairs(pe, transposes, product(w4), base=NT)

        @block.vector
        def _(dve):
            def evacuate(t, u, c):
                dve.wait_ge(s_T, LEAD + c + 1)
                dve.wait_ge(s_U, LEAD + c - 1)
                dve.tensor_copy(curT[:, u, :, :].rearrange("p k m -> p (k m)"), pT[:, u, 0:KC * P]).then_inc(s_curT, 1)

            def add_self(t, u, c):
                dve.wait_ge(s_U, LEAD + c + 1)
                mine = keep.self_in[:, at(t, D)]
                dve.tensor_tensor(mine, pU[:, u, :], mine, ALU.add).then_inc(s_pre, 1)

            pairs(dve, evacuate, add_self)
            dve.wait_ge(s_pre, LEAD + NT)
            for h in range(2):
                part = slice(h * HALF, (h + 1) * HALF)
                dve.tensor_scalar(keep.agg[0:P, part], keep.self_in[:, part], MISH_CLAMP, None, ALU.min).then_inc(s_clamp, 1)
            for h in range(2):
                part = slice(h * HALF, (h + 1) * HALF)
                dve.wait_ge(s_tanh, h + 1)
                dve.tensor_tensor(keep.self_in[:, part], keep.self_in[:, part], keep.agg[0:P, part], ALU.mult).then_inc(s_mish, 1)
            dve.wait_ge(w_in, 80)
            dve.wait_ge(s_bias, 2 * NT)

            def residual(t, u, c):
                dve.wait_ge(s_U, LEAD + c + 1)
                dve.tensor_tensor(y[:, u, :], pU[:, u, :], keep.xn[:, at(t, D)], ALU.add).then_inc(s_pre, 1)
                dve.wait_ge(s_pre, LEAD + c + 1)
                layer_norm_stats(dve, y[:, u, :], stats[:, u, :], mv[:, u, :], var_eps[:, u, :], 1e-5,
                                 s_stats, s_mv, s_var, gate, LEAD + t)

            def norm(t, u, c):
                dve.wait_ge(s_rstd, t + 1)
                dve.tensor_scalar(y[:, u, :], y[:, u, :], mv[:, u, 0:1], rstd[:, u, :], ALU.subtract, ALU.mult).then_inc(s_y, 1)

            def scale(t, u, c):
                dve.tensor_tensor(y[:, u, :], y[:, u, :], gamma[:, :], ALU.mult).then_inc(s_sum, 1)

            def total(t, u, c):
                mine = keep.x[:, at(t, D)]
                dve.wait_ge(s_sum, t + 1)
                dve.tensor_tensor(mine, mine, y[:, u, :], ALU.add).then_inc(s_bias, 1)

            def norm_all(t, u, c):
                norm(t, u, c)
                dve.wait_ge(s_y, LEAD + t + 1)
                scale(t, u, c)
                total(t, u, c)

            pairs(dve, residual, norm_all, base=NT)


ROUND = 12582912.0
EXPERTS, HIDDEN = 8, 256
FC = HIDDEN // 128
CAPACITY = -(-5 * NODES // (4 * EXPERTS))
CHUNKS = ((0, 500), (500, 500), (1000, 250))


SEG = 2 * 98
SR = SEG // 2
TOP = 2
SEGS = (TOP * NODES + EXPERTS * (SEG - 1)) // SEG
LEAST_SEGS = -(-TOP * NODES // SEG)
SLOTS = (SEGS + 1) * SEG
ROW_FILL, RESULT_FILL = -(-SLOTS // NG), -(-(SEGS - LEAST_SEGS) * SEG // NG)
FIRST_FILL = (LEAST_SEGS + 1) * SEG
RESULTS = FIRST_FILL + RESULT_FILL * NG
DROPPED = SLOTS


def experts(nc, core, a, keep, name, acc, norm, out=None):
    with ExitStack() as ctx:
        sb = lambda n, s, d=F32: core.sb(f"{name}_{n}", s, d, ctx)
        sem = lambda n: core.sem(f"{name}_{n}")
        pre = "L0_ffn_" if norm else "L1_ffn_"
        r = Keep()
        r.w1, r.w2 = sb("w1", [128, 2, KC, HIDDEN]), sb("w2", [128, 2, FC, D])
        r.b1 = sb("b1", [128, 2, FC])
        r.b2, r.gamma = sb("b2", [SR, 2, D]), sb("gamma", [SR, 2, D])
        r.ranges = sb("ranges", [1, 2 * EXPERTS], I32)
        r.gates = sb("gates", [P, TOP, NT])
        r.into, r.back = sb("into", [P, TOP, NT], I32), sb("back", [P, TOP, NT], I32)
        r.s_w, r.s_rows = [sem("w0"), sem("w1")], [sem("rows0"), sem("rows1")]

        def load(eng, e, b):
            s = r.s_w[b]
            eng.dma_start(r.w1[:, b, :, :], a[pre + "w1"].rearrange("e (k p) n -> e p k n", p=128)[bass.ds(e, 1), :, :, :]
                          .rearrange("e p k n -> p (e k) n")).then_inc(s, 16)
            eng.dma_start(r.w2[:, b, :, :], a[pre + "w2"].rearrange("e (k p) n -> e p k n", p=128)[bass.ds(e, 1), :, :, :]
                          .rearrange("e p k n -> p (e k) n")).then_inc(s, 16)
            eng.dma_start(r.b1[:, b, :], a["ffn0_b1_cols" if norm else "ffn1_b1_cols"][:, at(e, FC)]).then_inc(s, 16)

        def load_rows(eng, e, b):
            eng.dma_start(r.b2[:, b, :], a[pre + "b2"][bass.ds(e, 1), :].broadcast_to([SR, D])).then_inc(r.s_rows[b], 16)
            eng.dma_start(r.gamma[:, b, :], a[pre + "gamma"][bass.ds(e, 1), :].broadcast_to([SR, D])).then_inc(r.s_rows[b], 16)

        r.load, r.load_rows = load, load_rows
        route(nc, core, a, keep, r, name, acc, norm)
        segments(nc, core, keep, r, name, norm)
        fetch(nc, core, keep, r, name, acc, out)


def route(nc, core, a, keep, r, name, acc, norm):
    with ExitStack() as ctx:
        sb = lambda n, s, d=F32: core.sb(f"{name}_{n}", s, d, ctx)
        ps = lambda n, s: core.ps(f"{name}_{n}", s, F32, ctx)
        sem = lambda n: core.sem(f"{name}_{n}")
        router = sb("router", [128, KC, EXPERTS])
        offsets = sb("offsets", [EXPERTS, D])
        xf = sb("xf", [P, 2, D])
        xfT = keep.agg[:, 0:KC * NODES].rearrange("p (k n) -> p k n", k=KC)
        logT, gateT = sb("logT", [EXPERTS, NODES]), sb("gateT", [EXPERTS, NODES])
        log, m1, m2, gate_w, slot = (sb(n, [P, NT, EXPERTS]) for n in ("log", "m1", "m2", "gate_w", "slot"))
        top, idx, idx_f = sb("top", [P, NT, 8]), sb("idx", [P, NT, 8], U32), sb("idx_f", [P, NT, 8])
        ids = sb("ids", [P, NT, EXPERTS])
        second, total, spill, lost = (sb(n, [P, NT]) for n in ("second", "total", "spill", "lost"))
        mine = sb("mine", [P, TOP, NT])
        before = sb("before", [P, NT + 1, EXPERTS])
        count, base, ends, ones8 = (sb(n, [P, EXPERTS]) for n in ("count", "base", "ends", "ones8"))
        tri, ones = sb("tri", [P, P]), sb("ones", [P, P])
        stats, mv = sb("stats", [P, 2, 6]), sb("mv", [P, 2, 2])
        var_eps, rstd = sb("var", [P, 2, 1]), sb("rstd", [P, 2, 1])
        pT, pA, pY = ps("pT", [128, 2, 512]), ps("pA", [128, 2, 512]), ps("pY", [P, 4, 512])
        pL, pR, pW = pY[0:EXPERTS, 0:3, :], pY[:, 3, :], pY[0:EXPERTS, 0:3, :]
        w_in, consts = sem("w_in"), sem("consts")
        s_stats, s_mv, s_var, gate, s_rstd, s_xf, s_T, s_xfT, s_kept = (
            sem(n) for n in ("stats", "mv", "var", "gate", "rstd", "xf", "T", "xfT", "kept"))
        s_logT, s_logE, s_log, s_lg, s_r, s_exp, s_pos, s_gT, s_gE, s_off, s_acc0, s_ways, s_sent = (
            sem(n) for n in ("logT", "logE", "log", "lg", "route", "exp", "pos", "gT", "gE", "off", "acc0", "ways", "sent"))
        s_chain = sem("chain")
        block = ctx.enter_context(nc.Block())
        PAIRS = NT // 2
        pre = "L0_ffn_" if norm else "L1_ffn_"

        @block.sync
        def _(sp):
            for s in (s_stats, s_mv, s_var, s_xf, s_T, s_xfT, s_rstd, s_kept):
                sp.sem_inc(s, 4)
            sp.dma_start(router[:, :, :], a["router0" if norm else "router1"]).then_inc(w_in, 16)
            sp.dma_start(offsets[:, :], a[pre + ("beta" if norm else "b2")]).then_inc(w_in, 16)
            for e in range(2):
                r.load(sp, e, e)
            for e in range(2):
                sp.wait_ge(r.s_w[e], 48)

        @block.gpsimd
        def _(pool):
            pool.memset(ones[:, :], 1.0).then_inc(consts, 1)
            pool.iota(ids[:, :, :], pattern=[[0, NT], [1, EXPERTS]], base=0, channel_multiplier=0,
                      allow_small_or_imprecise_dtypes=True).then_inc(consts, 1)
            pool.memset(tri[:, :], 1.0).then_inc(consts, 1)
            pool.memset(ones8[:, :], 1.0).then_inc(consts, 1)
            pool.iota(spill[:, :], pattern=[[P, NT]], base=DROPPED, channel_multiplier=1,
                      allow_small_or_imprecise_dtypes=True).then_inc(consts, 1)
            pool.wait_ge(consts, 5)
            pool.affine_select(out=tri[:, :], in_=tri[:, :], compare_op=ALU.is_ge, fill=0.0, base=-1,
                               pattern=[[1, P]], channel_multiplier=-1).then_inc(consts, 1)
            with pool.Fori(0, PAIRS) as i:
                for u in range(2):
                    t = 2 * i + u
                    pool.wait_ge(s_var, 4 + t + 1)
                    pool.tensor_tensor(rstd[:, u, :], var_eps[:, u, :], keep.minus_half[:, :], ALU.pow).then_inc(s_rstd, 1)
            pool.wait_ge(s_kept, 4 + NT)
            pool.wait_ge(s_ways, 1)
            for t in range(NT):
                for k in range(TOP):
                    pool.indirect_dma_start(keep.slots_dram, bass.IndirectOffsetOnAxis(ap=r.into[:, k, t:t + 1], axis=0),
                                            keep.xn[:, t * D:(t + 1) * D], None).then_inc(s_sent, 16)
            if norm:
                for e in range(2):
                    r.load_rows(pool, e, e)
                for e in range(2):
                    pool.wait_ge(r.s_rows[e], 32)
            pool.wait_ge(s_sent, 16 * TOP * NT)

        @block.scalar
        def _(act):
            with act.Fori(0, PAIRS) as i:
                for u in range(2):
                    t = 2 * i + u
                    act.wait_ge(s_T, 4 + t + 1)
                    act.activation(xfT[:, :, at(t, P)], pT[:, u, 0:KC * P].rearrange("p (k m) -> p k m", k=KC),
                                   ACT.Copy).then_inc(s_xfT, 1)
                    act.wait_ge(s_xf, 4 + t + 1)
                    act.activation(keep.xn[:, at(t, D)], xf[:, u, :], ACT.Copy).then_inc(s_kept, 1)
            act.wait_ge(s_logT, 1)
            for j, (c0, n) in enumerate(CHUNKS):
                act.activation(logT[:, c0:c0 + n], pL[:, j, 0:n], ACT.Copy).then_inc(s_logE, 1)
            act.wait_ge(s_r, 3)
            act.activation(second[:, :], second[:, :], ACT.Exp).then_inc(s_exp, 1)
            act.wait_ge(s_gT, 1)
            for j, (c0, n) in enumerate(CHUNKS):
                act.activation(gateT[:, c0:c0 + n], pW[:, j, 0:n], ACT.Copy).then_inc(s_gE, 1)
            for t in range(NT):
                act.wait_ge(s_off, t + 1)
                act.activation(acc[:, at(t, D)], pA[0:P, t % 2, :], ACT.Copy).then_inc(s_acc0, 1)

        @block.tensor
        def _(pe):
            with pe.Fori(0, PAIRS) as i:
                for u in range(2):
                    t = 2 * i + u
                    pe.wait_ge(s_xf, 4 + t + 1)
                    pe.wait_ge(s_xfT, 4 + t - 1)
                    for k in range(KC):
                        mm = pe.transpose(pT[:, u, k * P:(k + 1) * P], xf[:, u, k * 128:(k + 1) * 128], keep.ident[0:P, 0:P])
                    mm.then_inc(s_T, 1)
            pe.wait_ge(w_in, 32)
            pe.wait_ge(s_xfT, 4 + NT)
            for j, (c0, n) in enumerate(CHUNKS):
                for k in range(KC):
                    mm = pe.matmul(pL[:, j, 0:n], router[:, k, :], xfT[:, k, c0:c0 + n], start=(k == 0), stop=(k == KC - 1))
            mm.then_inc(s_logT, 1)
            pe.wait_ge(s_logE, 3)
            for t in range(NT):
                mm = pe.transpose(pR[:, t * EXPERTS:(t + 1) * EXPERTS], logT[:, t * P:(t + 1) * P], keep.ident[0:EXPERTS, 0:EXPERTS])
            mm.then_inc(s_log, 1)
            pe.wait_ge(consts, 6)
            pe.wait_ge(s_pos, 1)
            chosen = log[:, :, :].rearrange("p t e -> p (t e)")
            earlier = before[:, :, :].rearrange("p t e -> p (t e)")
            pe.matmul(pR[:, 256:256 + NT * EXPERTS], tri[:, :], chosen, start=True, stop=False)
            pe.matmul(pR[:, 256:256 + NT * EXPERTS], ones[:, :], earlier[:, 0:NT * EXPERTS], start=False, stop=True)
            pe.matmul(pR[:, 256 + NT * EXPERTS:256 + (NT + 1) * EXPERTS], ones[:, :], earlier[:, NT * EXPERTS:],
                      start=True, stop=True).then_inc(s_pos, 1)
            pe.wait_ge(s_lg, 2)
            for t in range(NT):
                mm = pe.transpose(pW[:, t // 4, (t % 4) * P:(t % 4 + 1) * P], gate_w[:, t, :], keep.ident[0:P, 0:P])
            mm.then_inc(s_gT, 1)
            pe.wait_ge(s_gE, 3)
            for t in range(NT):
                if t >= 2:
                    pe.wait_ge(s_acc0, t - 1)
                pe.matmul(pA[0:P, t % 2, :], gateT[:, t * P:(t + 1) * P], offsets[:, :], start=True, stop=True).then_inc(s_off, 1)
        @block.vector
        def _(dve):
            with dve.Fori(0, PAIRS) as i:
                for u in range(2):
                    t = 2 * i + u
                    layer_norm_stats(dve, keep.x[:, at(t, D)], stats[:, u, :], mv[:, u, :], var_eps[:, u, :], 1e-5,
                                     s_stats, s_mv, s_var, gate, 4 + t)
                for u in range(2):
                    t = 2 * i + u
                    dve.wait_ge(s_rstd, 4 + t + 1)
                    dve.wait_ge(s_T, 4 + t - 1)
                    dve.wait_ge(s_kept, 4 + t - 1)
                    dve.tensor_scalar(xf[:, u, :], keep.x[:, at(t, D)], mv[:, u, 0:1], rstd[:, u, :],
                                      ALU.subtract, ALU.mult).then_inc(s_xf, 1)
            chain = [0]

            def step(ins):
                chain[0] += 1
                ins.then_inc(s_chain, 1)
                dve.wait_ge(s_chain, chain[0])

            dve.wait_ge(s_log, 1)
            step(dve.tensor_copy(log[:, :, :].rearrange("p t e -> p (t e)"), pR[:, 0:NT * EXPERTS]))
            for t in range(NT):
                step(dve.max(top[:, t, :], log[:, t, :]))
                step(dve.max_index(idx[:, t, :], top[:, t, :], log[:, t, :]))
            step(dve.tensor_copy(idx_f[:, :, :], idx[:, :, :]))
            dve.tensor_tensor(second[:, :], top[:, :, 1], top[:, :, 0], ALU.subtract).then_inc(s_r, 3)
            dve.wait_ge(s_exp, 1)
            dve.wait_ge(consts, 6)
            step(dve.tensor_scalar(total[:, :], second[:, :], 1.0, None, ALU.add))
            step(dve.reciprocal(total[:, :], total[:, :]))
            step(dve.tensor_tensor(second[:, :], second[:, :], total[:, :], ALU.mult))
            wide = lambda v: v.broadcast_to([P, NT, EXPERTS])
            step(dve.tensor_tensor(m1[:, :, :], ids[:, :, :], wide(idx_f[:, :, 0:1]), ALU.is_equal))
            step(dve.tensor_tensor(m2[:, :, :], ids[:, :, :], wide(idx_f[:, :, 1:2]), ALU.is_equal))
            step(dve.tensor_tensor(gate_w[:, :, :], m1[:, :, :], wide(total[:, :].rearrange("p (t o) -> p t o", o=1)), ALU.mult))
            step(dve.tensor_tensor(log[:, :, :], m2[:, :, :], wide(second[:, :].rearrange("p (t o) -> p t o", o=1)), ALU.mult))
            step(dve.tensor_tensor(gate_w[:, :, :], gate_w[:, :, :], log[:, :, :], ALU.add))
            step(dve.tensor_tensor(log[:, :, :], m1[:, :, :], m2[:, :, :], ALU.add))
            step(dve.memset(before[:, 0, :], 0.0))
            for t in range(NT):
                step(dve.tensor_tensor(before[:, t + 1, :], before[:, t, :], log[:, t, :], ALU.add))
            dve.sem_inc(s_pos, 1)
            dve.wait_ge(s_pos, 2)
            flat = lambda v: v[:, :, :].rearrange("p t e -> p (t e)")
            place, chose = pR[:, 256:256 + NT * EXPERTS], pR[:, 256 + NT * EXPERTS:256 + (NT + 1) * EXPERTS]
            capacity = NODES if norm else CAPACITY
            if not norm:
                step(dve.scalar_tensor_tensor(flat(gate_w), place, float(capacity), flat(gate_w), ALU.is_lt, ALU.mult))
            dve.sem_inc(s_lg, 2)
            step(dve.tensor_scalar(count[:, :], chose, float(capacity), SEG / 2 - 0.5, ALU.min, ALU.add))
            step(dve.tensor_scalar(count[:, :], count[:, :], 1.0 / SEG, ROUND, ALU.mult, ALU.add))
            step(dve.tensor_scalar(count[:, :], count[:, :], -ROUND, 1.0, ALU.add, ALU.max))
            step(dve.tensor_tensor_scan(ends[:, :], ones8[:, :], count[:, :], 0.0, ALU.mult, ALU.add))
            step(dve.tensor_tensor(base[:, :], ends[:, :], count[:, :], ALU.subtract))
            step(dve.tensor_copy(r.ranges[:, 0:EXPERTS], base[0:1, :]))
            step(dve.tensor_copy(r.ranges[:, EXPERTS:2 * EXPERTS], ends[0:1, :]))
            step(dve.tensor_scalar(base[:, :], base[:, :], float(SEG), None, ALU.mult))
            step(dve.tensor_scalar(flat(slot), place, float(capacity - 1), None, ALU.min))
            step(dve.tensor_tensor(slot[:, :, :], slot[:, :, :], base[:, :].rearrange("p (o e) -> p o e", o=1).broadcast_to([P, NT, EXPERTS]),
                                   ALU.add))
            step(dve.tensor_scalar(flat(log), place, float(capacity), None, ALU.is_ge))
            for k, chosen in enumerate((m1, m2)):
                step(dve.tensor_tensor(before[:, 0:NT, :], chosen[:, :, :], gate_w[:, :, :], ALU.mult))
                step(dve.tensor_reduce(r.gates[:, k, :], before[:, 0:NT, :], AX_X, ALU.add))
                step(dve.tensor_tensor(before[:, 0:NT, :], chosen[:, :, :], slot[:, :, :], ALU.mult))
                step(dve.tensor_reduce(mine[:, k, :], before[:, 0:NT, :], AX_X, ALU.add))
                step(dve.tensor_scalar(r.back[:, k, :], mine[:, k, :], float(SEG), None, ALU.add))
                if not norm:
                    step(dve.tensor_tensor(before[:, 0:NT, :], chosen[:, :, :], log[:, :, :], ALU.mult))
                    step(dve.tensor_reduce(lost[:, :], before[:, 0:NT, :], AX_X, ALU.add))
                    step(dve.scalar_tensor_tensor(total[:, :], spill[:, :], float(NODES * k), mine[:, k, :], ALU.add, ALU.subtract))
                    step(dve.tensor_tensor(total[:, :], total[:, :], lost[:, :], ALU.mult))
                    step(dve.tensor_tensor(mine[:, k, :], mine[:, k, :], total[:, :], ALU.add))
                step(dve.tensor_copy(r.into[:, k, :], mine[:, k, :]))
            dve.sem_inc(s_ways, 1)
            dve.wait_ge(s_acc0, NT)


def segments(nc, core, keep, r, name, norm):
    with ExitStack() as ctx:
        sb = lambda n, s, d=F32: core.sb(f"{name}_{n}", s, d, ctx)
        ps = lambda n, s: core.ps(f"{name}_{n}", s, F32, ctx)
        sem = lambda n: core.sem(f"{name}_s_{n}")
        rows, xT = sb("rows", [SR, 2, D]), sb("xT", [128, KC, SEG])
        hT = sb("hT", [128, FC, SEG])
        again = sb("again", [SR, 2, D])
        xb, y, result = sb("xb", [SR, 2, D]), sb("y", [SR, 2, D]), sb("result", [SR, 2, D])
        stats, mv = sb("seg_stats", [SR, 2, 6]), sb("seg_mv", [SR, 2, 2])
        var_eps, rstd = sb("seg_var", [SR, 2, 1]), sb("seg_rstd", [SR, 2, 1])
        pT, pH, pY = ps("seg_pT", [128, 2, 512]), ps("seg_pH", [128, FC, 512]), ps("seg_pY", [SR, 2, 512])
        s_rows, s_out, s_T, s_xT, s_h, s_act, s_y, s_yr, s_xb, s_free = (
            sem(n) for n in ("rows", "out", "T", "xT", "h", "act", "y", "yr", "xb", "free"))
        s_stats, s_mv, s_var, gate, s_rstd, s_n, s_done, s_zero, gate_sp, gate_pe, s_again, gate_act, gate_pool = (
            sem(n) for n in ("stats", "mv", "var", "gate", "rstd", "norm", "done", "zero", "gate_sp", "gate_pe", "again", "gate_act", "gate_pool"))
        block = ctx.enter_context(nc.Block())

        def by_segment(eng, body, before=None, behind=None):
            def expert(e, b, h, last):
                first = eng.value_load(r.ranges[0:1, bass.ds(e, 1)], min_val=0, max_val=SEGS - 1)
                behind_last = eng.value_load(r.ranges[0:1, bass.ds(e + EXPERTS, 1)], min_val=1, max_val=SEGS)
                if before:
                    before(b, h)
                with eng.Fori(first, behind_last) as g:
                    body(g, b)
                if behind:
                    behind(e, b, last)

            with eng.Fori(0, EXPERTS // 2 - 1) as h:
                for b in range(2):
                    expert(2 * h + b, b, h, False)
            for b in range(2):
                expert(EXPERTS - 2 + b, b, EXPERTS // 2 - 1, True)

        @block.sync
        def _(sp):
            for s in (s_T, s_xT, s_h, s_act, s_y, s_yr, s_xb, s_stats, s_mv, s_var, s_rstd, s_n, s_done, s_again):
                sp.sem_inc(s, LEAD)

            def load(g):
                sp.dma_start(rows[:, :, :], keep.slots_dram[at(g, SEG), :].rearrange("(u p) d -> p u d", p=SR)).then_inc(s_rows, 16)

            def store(g):
                sp.dma_start(keep.results_dram[at(g, SEG), :].rearrange("(u p) d -> p u d", p=SR), result[:, :, :]).then_inc(s_out, 16)

            def body(g, b):
                sp.wait_ge(s_T, LEAD + 2 * g + 2)
                if norm:
                    sp.sem_inc(gate_sp, 1)
                    sp.wait_ge(s_again, LEAD + g + 1)
                    sp.sem_inc(gate_sp, 1)
                load(g + 1)
                sp.wait_ge(s_done, LEAD + 2 * g)
                store(g)

            load(0)
            sp.wait_ge(s_zero, 1)
            by_segment(sp, body)
            end = sp.value_load(r.ranges[0:1, 2 * EXPERTS - 1:2 * EXPERTS], min_val=EXPERTS, max_val=SEGS)
            sp.wait_ge(s_done, LEAD + 2 * end)
            store(end)
            sp.wait_ge(s_out, 16 * end + 16)
            sp.sem_inc(gate_sp, 1)

        @block.gpsimd
        def _(pool):
            pool.memset(result[:, :, :], 0.0).then_inc(s_zero, 1)
            if norm:
                def body(g, b):
                    pool.wait_ge(s_again, LEAD + g + 1)
                    for u in range(2):
                        pool.wait_ge(s_yr, LEAD + 2 * g + u - 1)
                        pool.tensor_tensor(xb[:, u, :], again[:, u, :], r.b2[:, b, :], ALU.add).then_inc(s_xb, 1)
                    for u in range(2):
                        pool.wait_ge(s_var, LEAD + 2 * g + u + 1)
                        pool.tensor_tensor(rstd[:, u, :], var_eps[:, u, :], keep.minus_half[0:SR, :], ALU.pow).then_inc(s_rstd, 1)

                def expert_rows(b, h):
                    pool.wait_ge(r.s_rows[b], 32 * h + 32)
                    pool.sem_inc(gate_pool, 1)

                def next_rows(e, b, last):
                    if not last:
                        pool.wait_ge(s_free, e + 1)
                        pool.sem_inc(gate_pool, 1)
                        r.load_rows(pool, e + 2, b)

                by_segment(pool, body, before=expert_rows, behind=next_rows)

        @block.scalar
        def _(act):
            def columns(g):
                for u in range(2):
                    act.wait_ge(s_T, LEAD + 2 * g + u + 1)
                    act.wait_ge(s_h, LEAD + 2 * g)
                    act.activation(xT[:, :, u * SR:(u + 1) * SR], pT[:, u, 0:KC * SR].rearrange("p (k m) -> p k m", k=KC),
                                   ACT.Copy).then_inc(s_xT, 1)
                if norm:
                    act.wait_ge(s_xb, LEAD + 2 * g)
                    act.activation(again[:, :, :], rows[:, :, :], ACT.Copy).then_inc(s_again, 1)

            def body(g, b):
                for f in range(FC):
                    act.wait_ge(s_h, LEAD + 2 * g + f + 1)
                    act.wait_ge(s_y, LEAD + 2 * g)
                    act.activation(hT[:, f, :], pH[:, f, 0:SEG], ACT.Relu if norm else ACT.Gelu, bias=r.b1[:, b, f:f + 1]).then_inc(s_act, 1)
                columns(g + 1)

            def next_weights(e, b, last):
                if not last:
                    end = act.value_load(r.ranges[0:1, bass.ds(e + EXPERTS, 1)], min_val=1, max_val=SEGS)
                    act.wait_ge(s_y, LEAD + 2 * end)
                    act.sem_inc(gate_act, 1)
                    r.load(act, e + 2, b)

            columns(0)
            by_segment(act, body, behind=next_weights)

        @block.tensor
        def _(pe):
            def transposes(g):
                pe.wait_ge(s_rows, 16 * g + 16)
                for u in range(2):
                    pe.wait_ge(s_xT, LEAD + 2 * g + u - 1)
                    for k in range(KC):
                        mm = pe.transpose(pT[:, u, k * SR:(k + 1) * SR], rows[:, u, k * 128:(k + 1) * 128], keep.ident[0:SR, 0:SR])
                    mm.then_inc(s_T, 1)

            def body(g, b):
                pe.wait_ge(s_xT, LEAD + 2 * g + 2)
                for f in range(FC):
                    pe.wait_ge(s_act, LEAD + 2 * g + f - 1)
                    for k in range(KC):
                        mm = pe.matmul(pH[:, f, 0:SEG], r.w1[:, b, k, f * 128:(f + 1) * 128], xT[:, k, :], start=(k == 0), stop=(k == KC - 1))
                    mm.then_inc(s_h, 1)
                transposes(g + 1)
                pe.wait_ge(s_act, LEAD + 2 * g + 2)
                for u in range(2):
                    pe.wait_ge(s_yr, LEAD + 2 * g + u - 1)
                    for f in range(FC):
                        mm = pe.matmul(pY[:, u, :], hT[:, f, u * SR:(u + 1) * SR], r.w2[:, b, f, :], start=(f == 0), stop=(f == FC - 1))
                    mm.then_inc(s_y, 1)

            def weights(b, h):
                pe.wait_ge(r.s_w[b], 48 * h + 48)
                pe.sem_inc(gate_pe, 1)

            transposes(0)
            by_segment(pe, body, before=weights)

        @block.vector
        def _(dve):
            def plain(g, b):
                for u in range(2):
                    dve.wait_ge(s_out, 16 * g + 16)
                    dve.wait_ge(s_y, LEAD + 2 * g + u + 1)
                    dve.tensor_copy(result[:, u, :], pY[:, u, :]).then_inc(s_yr, 1)
                    dve.wait_ge(s_yr, LEAD + 2 * g + u + 1)
                    dve.sem_inc(s_done, 1)

            def normed(g, b):
                for u in range(2):
                    dve.wait_ge(s_y, LEAD + 2 * g + u + 1)
                    dve.wait_ge(s_xb, LEAD + 2 * g + u + 1)
                    dve.wait_ge(s_done, LEAD + 2 * g + u - 1)
                    dve.tensor_tensor(y[:, u, :], pY[:, u, :], xb[:, u, :], ALU.add).then_inc(s_yr, 1)
                for u in range(2):
                    dve.wait_ge(s_yr, LEAD + 2 * g + u + 1)
                    layer_norm_stats(dve, y[:, u, :], stats[:, u, :], mv[:, u, :], var_eps[:, u, :], 1e-6,
                                     s_stats, s_mv, s_var, gate, LEAD + 2 * g + u)
                for u in range(2):
                    dve.wait_ge(s_rstd, LEAD + 2 * g + u + 1)
                    dve.tensor_scalar(y[:, u, :], y[:, u, :], mv[:, u, 0:1], rstd[:, u, :], ALU.subtract, ALU.mult).then_inc(s_n, 1)
                    dve.wait_ge(s_out, 16 * g + 16)
                    dve.wait_ge(s_n, LEAD + 2 * g + u + 1)
                    dve.tensor_tensor(result[:, u, :], y[:, u, :], r.gamma[:, b, :], ALU.mult).then_inc(s_done, 1)

            def expert_rows(b, h):
                if norm:
                    dve.wait_ge(r.s_rows[b], 32 * h + 32)
                    dve.sem_inc(gate, 1)

            def free(e, b, last):
                end = dve.value_load(r.ranges[0:1, bass.ds(e + EXPERTS, 1)], min_val=1, max_val=SEGS)
                dve.wait_ge(s_done, LEAD + 2 * end)
                dve.sem_inc(s_free, 1)

            by_segment(dve, normed if norm else plain, before=expert_rows, behind=free)


def fetch(nc, core, keep, r, name, acc, out):
    BUFFERS = 4
    with ExitStack() as ctx:
        sem = lambda n: core.sem(f"{name}_f_{n}")
        got = core.sb(f"{name}_got", [P, BUFFERS, TOP, D], F32, ctx)
        s_got = [sem(f"got{b}") for b in range(BUFFERS)]
        s_sum, s_x, s_out = sem("sum"), sem("x"), sem("out")
        block = ctx.enter_context(nc.Block())

        if out is not None:
            @block.sync
            def _(sp):
                for t in range(NT):
                    sp.wait_ge(s_x, t + 1)
                    sp.dma_start(out[t * P:(t + 1) * P, :], keep.x[:, t * D:(t + 1) * D]).then_inc(s_out, 16)
                sp.wait_ge(s_out, 16 * NT)

        @block.gpsimd
        def _(pool):
            for t in range(NT):
                if t >= BUFFERS:
                    pool.wait_ge(s_sum, TOP * (t - BUFFERS + 1))
                for k in range(TOP):
                    pool.indirect_dma_start(got[:, t % BUFFERS, k, :], None, keep.results_dram,
                                            bass.IndirectOffsetOnAxis(ap=r.back[:, k, t:t + 1], axis=0)).then_inc(s_got[t % BUFFERS], 16)

        @block.vector
        def _(dve):
            for t in range(NT):
                dve.wait_ge(s_got[t % BUFFERS], 16 * TOP * (t // BUFFERS + 1))
                part = acc[:, at(t, D)]
                for k in range(TOP):
                    after(dve, s_sum, TOP * t + k)
                    dve.scalar_tensor_tensor(part, got[:, t % BUFFERS, k, :], r.gates[:, k, t:t + 1], part, ALU.mult, ALU.add).then_inc(s_sum, 1)
                dve.wait_ge(s_sum, TOP * t + TOP)
                dve.tensor_tensor(keep.x[:, at(t, D)], keep.x[:, at(t, D)], part, ALU.add).then_inc(s_x, 1)
            dve.wait_ge(s_x, NT)


FREQS, COND = 32, 16
GROUPS = (0, 32, 64)
COND_ROWS = GROUPS[-1] + COND + 1
TWO_PI = 6.283185307179586
TWO_PI_HIGH = 6.28125
TWO_PI_LOW = TWO_PI - TWO_PI_HIGH
SIN_LIMIT = 3.1415925


def prepare_attention(nc, core, a, keep):
    with ExitStack() as ctx:
        sb = lambda n, s, d=F32: core.sb("p5_" + n, s, d, ctx)
        sem = lambda n: core.sem("p5_" + n)
        F2 = 2 * FREQS
        phase, turns, emb = sb("phase", [F2, NODES]), sb("turns", [F2, NODES]), sb("emb", [F2, NODES])
        freq, quarter = sb("freq", [F2, 1]), sb("quarter", [F2, 2])
        fw1, fw2 = sb("fw1", [F2, COND]), sb("fw2", [COND, COND_ROWS - 1])
        fb = sb("fb", [COND_ROWS - 1, 2])
        cond = sb("cond", [COND_ROWS, NODES])
        hid = sb("hid", [COND, NODES])
        none = sb("none", [P, 2, NODES])
        stats, mv = sb("stats", [P, 2, 6]), sb("mv", [P, 2, 2])
        var_eps, rstd = sb("var", [P, 2, 1]), sb("rstd", [P, 2, 1])
        pc = core.ps("p5_pc", [COND_ROWS - 1, 2, 3, 512], F32, ctx)
        w_in, consts, s_emb, s_sin, s_h, s_hid, s_c, s_cond = (
            sem(n) for n in ("w_in", "consts", "emb", "sin", "h", "hid", "c", "cond"))
        s_chain, s_blank, s_high, s_low = sem("chain"), sem("blank"), sem("cond_high"), sem("cond_low")
        s_none, s_one, s_ln, s_log, s_out = (sem(n) for n in ("none", "one", "ln", "log", "out"))
        s_stats, s_mv, s_var, gate, s_rstd, s_xn = (sem(n) for n in ("stats", "mv", "var", "gate", "rstd", "xn"))
        block = ctx.enter_context(nc.Block())

        @block.sync
        def _(sp):
            for s in (s_stats, s_mv, s_var, s_log, s_ln, s_none, s_one):
                sp.sem_inc(s, LEAD)
            sp.dma_start(phase[:, :], a["node_vec1"].rearrange("n o -> o n").broadcast_to([F2, NODES])).then_inc(w_in, 16)
            sp.dma_start(fw1[:, :], a["L1_gnn_f_w1"]).then_inc(w_in, 16)
            sp.wait_ge(s_blank, 2)
            sp.dma_start(fb[0:COND, 0:1], a["L1_gnn_f_b1"].rearrange("(n o) -> n o", o=1)).then_inc(w_in, 16)
            for g in GROUPS:
                sp.dma_start(fw2[:, g:g + COND], a["L1_gnn_f_w2"]).then_inc(w_in, 16)
                sp.dma_start(fb[g:g + COND, 1:2], a["L1_gnn_f_b2"].rearrange("(n o) -> n o", o=1)).then_inc(w_in, 16)
            sp.dma_start(keep.x_dram.rearrange("(t p) d -> p t d", p=P), keep.x[:, :].rearrange("p (t d) -> p t d", d=D)).then_inc(s_out, 16)
            with sp.Fori(0, NT) as t:
                sp.wait_ge(s_log, LEAD + t + 1)
                sp.dma_start(keep.log_dram[bass.ds(t, 1), :, :].rearrange("t p d -> p (t d)"),
                             keep.log_pairs[:, bass.ds(t, 1), :].rearrange("p t d -> p (t d)")).then_inc(s_out, 16)
            sp.wait_ge(s_out, 16 * NT + 16)

        @block.gpsimd
        def _(pool):
            pool.memset(fw2[:, :], 0.0).then_inc(s_blank, 1)
            pool.wait_ge(s_blank, 1)
            pool.memset(fb[:, :], 1.0).then_inc(s_blank, 1)
            pool.wait_ge(s_blank, 2)
            for r in range(2):
                pool.iota(freq[r * FREQS:(r + 1) * FREQS, :], pattern=[[0, 1]], base=1, channel_multiplier=1,
                          allow_small_or_imprecise_dtypes=True).then_inc(consts, 1)
                pool.memset(quarter[r * FREQS:(r + 1) * FREQS, 0:1], 0.25 * r).then_inc(consts, 1)
                pool.memset(quarter[r * FREQS:(r + 1) * FREQS, 1:2], 0.25 * TWO_PI * r).then_inc(consts, 1)
            pool.wait_ge(consts, 6)
            pool.memset(cond[:, :], 1.0).then_inc(consts, 1)
            with pool.Fori(0, NT // 2) as i:
                for u in range(2):
                    pool.wait_ge(s_var, LEAD + 2 * i + u + 1)
                    pool.tensor_tensor(rstd[:, u, :], var_eps[:, u, :], keep.minus_half[:, :], ALU.pow).then_inc(s_rstd, 1)

        @block.scalar
        def _(act):
            act.wait_ge(s_emb, 1)
            act.activation(emb[:, :], emb[:, :], ACT.Sin).then_inc(s_sin, 1)
            act.wait_ge(s_h, 1)
            for j, (c0, n) in enumerate(CHUNKS):
                act.activation(hid[:, c0:c0 + n], pc[0:COND, 0, j, 0:n], ACT.Silu, bias=fb[0:COND, 0:1]).then_inc(s_hid, 1)
            act.wait_ge(s_c, 1)
            act.wait_ge(consts, 7)
            for j, (c0, n) in enumerate(CHUNKS):
                act.activation(cond[0:COND_ROWS - 1, c0:c0 + n], pc[:, 1, j, 0:n], ACT.Identity, bias=fb[:, 1:2]).then_inc(s_cond, 1)
            act.wait_ge(s_cond, 3)
            act.activation(keep.cond_parts[:, :], cond[:, :], ACT.Copy).then_inc(s_high, 1)
            with act.Fori(0, NT) as t:
                act.wait_ge(s_one, LEAD + t + 1)
                part = keep.log_pairs[:, bass.ds(t, 1), :]
                act.activation(part, part, ACT.Ln).then_inc(s_ln, 1)

        @block.tensor
        def _(pe):
            pe.wait_ge(w_in, 144)
            pe.wait_ge(s_sin, 1)
            for j, (c0, n) in enumerate(CHUNKS):
                mm = pe.matmul(pc[0:COND, 0, j, 0:n], fw1[:, :], emb[:, c0:c0 + n], start=True, stop=True)
            mm.then_inc(s_h, 1)
            pe.wait_ge(s_hid, 3)
            for j, (c0, n) in enumerate(CHUNKS):
                mm = pe.matmul(pc[:, 1, j, 0:n], fw2[:, :], hid[:, c0:c0 + n], start=True, stop=True)
            mm.then_inc(s_c, 1)

        @block.vector
        def _(dve):
            chain = [0]

            def step(ins):
                chain[0] += 1
                ins.then_inc(s_chain, 1)
                dve.wait_ge(s_chain, chain[0])

            dve.wait_ge(w_in, 144)
            dve.wait_ge(consts, 7)
            step(dve.tensor_scalar(freq[:, :], freq[:, :], TWO_PI / 16, None, ALU.mult))
            step(dve.tensor_scalar(phase[:, :], phase[:, :], freq[:, :], None, ALU.mult))
            step(dve.tensor_scalar(turns[:, :], phase[:, :], 1.0 / TWO_PI, None, ALU.mult))
            step(dve.tensor_scalar(turns[:, :], turns[:, :], quarter[:, 0:1], None, ALU.add))
            step(dve.tensor_scalar(turns[:, :], turns[:, :], ROUND, -ROUND, ALU.add, ALU.add))
            step(dve.scalar_tensor_tensor(phase[:, :], turns[:, :], -TWO_PI_HIGH, phase[:, :], ALU.mult, ALU.add))
            step(dve.scalar_tensor_tensor(phase[:, :], turns[:, :], -TWO_PI_LOW, phase[:, :], ALU.mult, ALU.add))
            step(dve.tensor_scalar(phase[:, :], phase[:, :], quarter[:, 1:2], None, ALU.add))
            dve.tensor_scalar(emb[:, :], phase[:, :], SIN_LIMIT, -SIN_LIMIT, ALU.min, ALU.max).then_inc(s_emb, 1)
            with dve.Fori(0, NT // 2) as i:
                for u in range(2):
                    t = 2 * i + u
                    layer_norm_stats(dve, keep.x[:, at(t, D)], stats[:, u, :], mv[:, u, :], var_eps[:, u, :], 1e-5,
                                     s_stats, s_mv, s_var, gate, LEAD + t)
                for u in range(2):
                    t = 2 * i + u
                    part = keep.log_pairs[:, bass.ds(t, 1), :]
                    dve.wait_ge(s_log, LEAD + t - 1)
                    dve.tensor_scalar(none[:, u:u + 1, :], part, 0.0, MASKED, ALU.is_equal, ALU.mult).then_inc(s_none, 1)
                    dve.wait_ge(s_none, LEAD + t + 1)
                    dve.tensor_scalar(part, part, 1.0, None, ALU.max).then_inc(s_one, 1)
                for u in range(2):
                    t = 2 * i + u
                    dve.wait_ge(s_rstd, t + 1)
                    dve.tensor_scalar(keep.xn[:, at(t, D)], keep.x[:, at(t, D)], mv[:, u, 0:1], rstd[:, u, :],
                                      ALU.subtract, ALU.mult).then_inc(s_xn, 1)
                for u in range(2):
                    t = 2 * i + u
                    part = keep.log_pairs[:, bass.ds(t, 1), :]
                    dve.wait_ge(s_ln, LEAD + t + 1)
                    dve.tensor_tensor(part, part, none[:, u:u + 1, :], ALU.add).then_inc(s_log, 1)
            dve.wait_ge(s_high, 1)
            low = slice(GROUPS[-1], COND_ROWS)
            dve.tensor_tensor(keep.cond_parts[low, :], cond[low, :], keep.cond_parts[low, :].bitcast(F32), ALU.subtract).then_inc(s_low, 1)
            dve.wait_ge(s_low, 1)


BLOCKS, HEADS, DH = 4, 4, 128
PAIRS = NT // 2
W2P = 2 * P
H = 4
EMPTY = -5.0e29


def attention_blocks(nc, core, a, keep):
    with ExitStack() as ctx:
        sb = lambda n, s, d=F32: core.sb("b_" + n, s, d, ctx)
        ps = lambda n, s: core.ps("b_" + n, s, F32, ctx)
        sem = lambda n: core.sem("b_" + n)
        X = keep.xn
        w = {n: sb(n, [128, KC, D]) for n in ("wo", "m_w1", "m_w2")}
        area = sb("area", [128, 3 * KC * D])
        for n, name in enumerate(("wq", "wk", "wv")):
            w[name] = area[:, n * KC * D:(n + 1) * KC * D].rearrange("p (k d) -> p k d", d=D)
        log_cur = area[0:P, 0:2 * NODES].rearrange("p (b n) -> p b n", b=2)
        prob = area[0:P, 2 * NODES:4 * NODES].rearrange("p (b n) -> p b n", b=2)
        att = area[0:P, 4 * NODES:4 * NODES + 2 * D].rearrange("p (b n) -> p b n", b=2)
        cond_raw, cond_w = sb("cond_raw", [COND_ROWS, 2, D]), sb("cond_w", [COND_ROWS, 2, D], F32R)
        cols = sb("cols", [128, 3, KC])
        rows = {n: sb(n + "_rows", [P, D]) for n in ("bv", "bo", "m_b2")}
        KT, V = sb("KT", [128, 2, HEADS, NODES], F32R), keep.self_in
        q_parts = sb("q_parts", [128, 2, 2, HEADS, P], F32R)
        QT = keep.agg[:, 0:HEADS * NODES].rearrange("p (h n) -> p h n", h=HEADS)
        cond = sb("cond_cur", [COND_ROWS, 2, P], F32R)
        z, zT = sb("z", [P, 2, D]), sb("zT", [128, KC, W2P])
        hT = sb("hT", [128, KC, W2P])
        stats, mv = sb("stats", [P, 2, 6]), sb("mv", [P, 2, 2])
        var_eps, rstd = sb("var", [P, 2, 1]), sb("rstd", [P, 2, 1])
        probT = sb("probT", [P, 2, NT, P])
        top, neg, den, inv = (sb(n, [P, 2, 1]) for n in ("top", "neg", "den", "inv"))
        attT = hT[:, :, 0:P]
        bank = ps("bank", [128, 8, 512])
        pair_row, pair_half = bank[:, 6:8, :], bank[:, 4:6, :]
        score = bank[0:P, 0:3, :].rearrange("p b n -> p (b n)")
        turned, att_sum, rest = bank[0:P, 3:6, :], bank[0:P, 6, :], bank[:, 7, :]
        TURN = ((0, 4), (4, 4), (8, 2))
        SCORE = ((0, 512), (512, 512), (1024, NODES - 1024))

        w_in = {n: sem("in_" + n) for n in ("qkv", "wo", "mlp", "cond_a", "cond_m")}
        log_in = [sem("log0"), sem("log1")]
        st = {}
        for kind in "am":
            for n in ("cond", "C", "stats", "mv", "var", "rstd", "z", "m1", "mod", "T", "zT", "bias"):
                st[kind, n] = sem(f"{n}_{kind}")
        gate, gate_pool, gate_sp = sem("gate"), sem("gate_pool"), sem("gate_sp")
        s_K, s_Ke, s_Q, s_Qe, s_V, s_Ve = (sem(n) for n in ("K", "Ke", "Q", "Qe", "V", "Ve"))
        s_h, s_he, s_m2, s_x2 = (sem(n) for n in ("h", "he", "m2", "x2"))
        s_qc, s_S, s_max, s_neg, s_P, s_PT, s_O, s_inv, s_att = (
            sem(n) for n in ("qc", "S", "max", "neg", "P", "PT", "O", "inv", "att"))
        s_old = sem("old_x")
        s_blank, s_ch, s_cw = sem("blank"), sem("cond_w_high"), sem("cond_w")
        s_qh, s_Kh = sem("q_high"), sem("K_high")
        s_e = [sem(f"turn{b}") for b in range(3)]
        s_aT, s_aTe, s_wo, s_x = (sem(n) for n in ("aT", "aTe", "wo", "x"))
        started = [*(s for s in st.values()), s_K, s_Ke, s_Q, s_Qe, s_V, s_Ve, s_h, s_he, s_m2, s_x2, s_qc, s_S, s_max, s_neg,
                   s_P, s_PT, s_O, s_inv, s_att, *s_e, s_aT, s_aTe, s_wo, s_x, s_qh, s_Kh, s_ch, s_cw]
        block = ctx.enter_context(nc.Block())

        def blocks(eng, body):
            with eng.Fori(0, BLOCKS) as blk:
                body(blk)

        @block.sync
        def _(sp):
            for s in started:
                sp.sem_inc(s, H)
            for s in log_in:
                sp.sem_inc(s, 16)

            def load(to, name, blk, s):
                sp.dma_start(to[:, :, :], a["L1_gnn_" + name][bass.ds(blk, 1), :, :].rearrange("b (k p) n -> p (b k) n", p=128)).then_inc(s, 16)

            def load_cond(name, blk, before, s):
                sp.wait_ge(s_cw, H + before)
                for g in GROUPS:
                    sp.dma_start(cond_raw[g:g + COND + 1, :, :], a[name][bass.ds(blk, 1), :, :, :].rearrange("b c s n -> (b c) s n")).then_inc(s, 16)

            sp.wait_ge(s_blank, 1)
            sp.sem_inc(gate_sp, 1)

            def body(blk):
                c0 = NT * blk
                sp.wait_ge(s_aT, H + c0)
                for n in ("wq", "wk", "wv"):
                    load(w[n], n, blk, w_in["qkv"])
                sp.wait_ge(s_Ve, H + c0)
                sp.wait_ge(s_Qe, H + c0)
                sp.dma_start(rows["bv"][:, :], a["L1_gnn_bv"][bass.ds(blk, 1), :].broadcast_to([P, D])).then_inc(w_in["qkv"], 16)
                sp.wait_ge(s_x, H + c0)
                load(w["wo"], "wo", blk, w_in["wo"])
                sp.wait_ge(st["a", "bias"], H + c0)
                sp.dma_start(rows["bo"][:, :], a["L1_gnn_bo"][bass.ds(blk, 1), :].broadcast_to([P, D])).then_inc(w_in["wo"], 16)
                load_cond("cond1", blk, 2 * blk, w_in["cond_a"])
                sp.wait_ge(s_he, H + c0)
                sp.dma_start(cols[:, :, :], a["cols"][bass.ds(blk, 1), :, :, :].rearrange("b p s k -> (b p) s k")).then_inc(w_in["qkv"], 16)
                sp.wait_ge(s_x2, H + c0)
                load(w["m_w1"], "m_w1", blk, w_in["mlp"])
                load(w["m_w2"], "m_w2", blk, w_in["mlp"])
                sp.wait_ge(st["m", "bias"], H + c0)
                sp.dma_start(rows["m_b2"][:, :], a["L1_gnn_m_b2"][bass.ds(blk, 1), :].broadcast_to([P, D])).then_inc(w_in["mlp"], 16)
                load_cond("cond2", blk, 2 * blk + 1, w_in["cond_m"])
                sp.wait_ge(s_V, H + c0 + NT)
                sp.sem_inc(gate_sp, 1)
                with sp.Fori(0, PAIRS) as i:
                    for u in range(2):
                        sp.wait_ge(s_max, H + HEADS * (c0 + 2 * i + u - 1))
                        sp.dma_start(log_cur[:, u, :], keep.log_dram[bass.ds(2 * i + u, 1), :, :].rearrange("t p d -> p (t d)")).then_inc(log_in[u], 16)

            blocks(sp, body)
            sp.wait_ge(s_O, H + HEADS * NT * BLOCKS)
            sp.dma_start(V[:, :].rearrange("p (t d) -> p t d", d=D), keep.x_dram.rearrange("(t p) d -> p t d", p=P)).then_inc(s_old, 16)
            sp.wait_ge(s_old, 16)

        @block.gpsimd
        def _(pool):
            def stage(kind, bias, w_sem, per, blk, c0):
                pool.wait_ge(w_sem, per * blk + per)
                pool.sem_inc(gate_pool, 1)
                with pool.Fori(0, PAIRS) as i:
                    for u in range(2):
                        c = c0 + 2 * i + u
                        pool.wait_ge(st[kind, "var"], H + c + 1)
                        pool.tensor_tensor(rstd[:, u, :], var_eps[:, u, :], keep.minus_half[:, :], ALU.pow).then_inc(st[kind, "rstd"], 1)
                    for u in range(2):
                        c = c0 + 2 * i + u
                        x = X[:, at(2 * i + u, D)]
                        pool.wait_ge(st[kind, "z"], H + c + 1)
                        pool.tensor_tensor(x, x, bias[:, :], ALU.add).then_inc(st[kind, "bias"], 1)

            def body(blk):
                stage("a", rows["bo"], w_in["wo"], 32, blk, NT * blk)
                with pool.Fori(0, PAIRS) as i:
                    for u in range(2):
                        c = NT * blk + 2 * i + u
                        pool.wait_ge(s_qh, H + c + 1)
                        pool.tensor_tensor(q_parts[:, u, 1, :, :], QT[:, :, at(2 * i + u, P)], q_parts[:, u, 0, :, :].bitcast(F32),
                                           ALU.subtract).then_inc(s_qc, 1)
                stage("m", rows["m_b2"], w_in["mlp"], 48, blk, NT * blk)

            pool.memset(cond_raw[:, :, :], 0.0).then_inc(s_blank, 1)
            blocks(pool, body)

        @block.scalar
        def _(act):
            def front(kind, c0):
                def conds(i):
                    for u in range(2):
                        act.wait_ge(st[kind, "C"], H + c0 + 2 * i + u - 1)
                        act.activation(cond[:, u, :], keep.cond_parts[:, at(2 * i + u, P)], ACT.Copy).then_inc(st[kind, "cond"], 1)
                return conds

            def turn(kind, used, c0):
                def stage(i):
                    act.wait_ge(st[kind, "T"], H + c0 + 2 * i + 2)
                    act.wait_ge(used, H + c0 + 2 * i)
                    for u in range(2):
                        ins = act.activation(zT[:, :, u * P:(u + 1) * P], bank[:, 2 * u, 0:KC * P].rearrange("p (k m) -> p k m", k=KC), ACT.Copy)
                    ins.then_inc(st[kind, "zT"], 2)
                return stage

            def split_cond(kind, blk, used):
                act.wait_ge(w_in["cond_" + kind], 48 * blk + 48)
                act.wait_ge(st["m" if kind == "a" else "a", "C"], used)
                act.activation(cond_w[:, :, :], cond_raw[:, :, :], ACT.Copy).then_inc(s_ch, 1)

            def body(blk):
                c0 = NT * blk
                split_cond("a", blk, H + c0)
                act.wait_ge(w_in["qkv"], 80 * blk + 80)
                conds, turned_a = front("a", c0), turn("a", s_V, c0)
                conds(0)
                turned_a(0)

                def back(i, ahead):
                    ahead()
                    for half in range(2):
                        act.wait_ge(s_K, H + c0 + 2 * i + half + 1)
                        for h in range(2):
                            head = 2 * half + h
                            ins = act.activation(KT[:, 0, head, at(i, W2P)], pair_half[:, half, h * W2P:(h + 1) * W2P], ACT.Identity,
                                                 bias=cols[:, 1, head:head + 1])
                        ins.then_inc(s_Kh, 1)

                with act.Fori(0, PAIRS - 1) as i:
                    back(i, lambda: conds(i + 1))
                    turned_a(i + 1)
                back(PAIRS - 1, lambda: None)

                def queries(i, u):
                    act.wait_ge(s_S, H + HEADS * (c0 + 2 * i + u - 1))
                    act.activation(q_parts[:, u, 0, :, :], QT[:, :, at(2 * i + u, P)], ACT.Copy).then_inc(s_qh, 1)

                def exponent(i, u, h):
                    q = HEADS * (c0 + 2 * i + u) + h
                    act.wait_ge(s_neg, H + q + 1)
                    act.activation(prob[:, h % 2, :], prob[:, h % 2, :], ACT.Exp, bias=neg[:, h % 2, :],
                                   accum_out=den[:, h % 2, :]).then_inc(s_P, 1)

                def slots(i, first, last):
                    for u in range(2):
                        for h in range(HEADS):
                            c = c0 + 2 * i + u
                            q = HEADS * c + h
                            more = not (last and u == 1 and h == HEADS - 1)
                            if h == 2 and not (last and u == 1):
                                queries(i + (u == 1), 1 - u)
                            if more:
                                nu, nh = (u, h + 1) if h + 1 < HEADS else (1 - u, 0)
                                exponent(i + (u == 1 and nh == 0), nu, nh)
                            act.wait_ge(s_PT, H + 3 * q + 3)
                            act.wait_ge(s_O, H + q - 1)
                            act.activation(probT[:, h % 2, 8:10, :], turned[:, 2, 0:2 * P].rearrange("p (t m) -> p t m", t=2),
                                           ACT.Copy).then_inc(s_e[2], 1)
                            if h == 2 and not (first and u == 0):
                                turn_att(c)

                def turn_att(c):
                    act.wait_ge(s_aT, H + c)
                    act.activation(attT, rest[:, 0:KC * P].rearrange("p (k m) -> p k m", k=KC), ACT.Copy).then_inc(s_aTe, 1)

                act.wait_ge(s_Qe, H + c0 + NT)
                queries(0, 0)
                exponent(0, 0, 0)
                slots(0, True, False)
                with act.Fori(1, PAIRS - 1) as i:
                    slots(i, False, False)
                slots(PAIRS - 1, False, True)
                turn_att(c0 + NT)

                split_cond("m", blk, H + c0 + NT)
                conds, turned_m = front("m", c0), turn("m", s_h, c0)
                conds(0)
                turned_m(0)

                def back_m(i, ahead):
                    ahead()
                    for half in range(2):
                        act.wait_ge(s_h, H + c0 + 2 * i + half + 1)
                        act.wait_ge(s_m2, H + c0 + 2 * i)
                        for f in range(2):
                            ins = act.activation(hT[:, 2 * half + f, :], pair_half[:, half, f * W2P:(f + 1) * W2P], ACT.Relu,
                                                 bias=cols[:, 2, 2 * half + f:2 * half + f + 1])
                        ins.then_inc(s_he, 1)

                with act.Fori(0, PAIRS - 1) as i:
                    back_m(i, lambda: conds(i + 1))
                    turned_m(i + 1)
                back_m(PAIRS - 1, lambda: None)

            blocks(act, body)

        @block.tensor
        def _(pe):
            def modulation(kind, c0, i):
                for u in range(2):
                    c = c0 + 2 * i + u
                    pe.wait_ge(st[kind, "cond"], H + c + 1)
                    pe.wait_ge(st[kind, "zT"], H + c0 + 2 * i)
                    for s in range(2):
                        mm = pe.matmul(bank[0:P, 2 * u + s, :], cond[:, u, :], cond_w[:, s, :], start=True, stop=True)
                    mm.then_inc(st[kind, "C"], 1)

            def transposes(kind, c0, i):
                for u in range(2):
                    pe.wait_ge(st[kind, "mod"], H + c0 + 2 * i + u + 1)
                    for k in range(KC):
                        mm = pe.transpose(bank[:, 2 * u, k * P:(k + 1) * P], z[:, u, k * 128:(k + 1) * 128], keep.ident[0:P, 0:P])
                    mm.then_inc(st[kind, "T"], 1)

            def halves(weight, half, done):
                for h in range(2):
                    head = 2 * half + h
                    for k in range(KC):
                        mm = pe.matmul(pair_half[:, half, h * W2P:(h + 1) * W2P], weight[:, k, head * 128:(head + 1) * 128],
                                       zT[:, k, :], start=(k == 0), stop=(k == KC - 1))
                mm.then_inc(done, 1)

            def rows_of(source, weight, u, done):
                for k in range(KC):
                    mm = pe.matmul(pair_row[0:P, u, :], source[:, k, u * P:(u + 1) * P], weight[:, k, :], start=(k == 0), stop=(k == KC - 1))
                mm.then_inc(done, 1)

            def body(blk):
                c0 = NT * blk
                pe.wait_ge(s_cw, H + 2 * blk + 1)
                pe.wait_ge(w_in["qkv"], 80 * blk + 80)
                modulation("a", c0, 0)
                transposes("a", c0, 0)

                def back(i, more):
                    if more:
                        modulation("a", c0, i + 1)
                    pe.wait_ge(st["a", "zT"], H + c0 + 2 * i + 2)
                    for half in range(2):
                        pe.wait_ge(s_Qe, H + c0 + 2 * i + half - 1)
                        halves(w["wk"], half, s_K)
                    for half in range(2):
                        pe.wait_ge(s_Ke, H + c0 + 2 * i + half + 1)
                        halves(w["wq"], half, s_Q)
                    for u in range(2):
                        pe.wait_ge(s_Ve, H + c0 + 2 * i + u - 1)
                        rows_of(zT, w["wv"], u, s_V)
                    if more:
                        transposes("a", c0, i + 1)

                with pe.Fori(0, PAIRS - 1) as i:
                    back(i, True)
                back(PAIRS - 1, False)

                def scores(i, u, h):
                    c = c0 + 2 * i + u
                    q = HEADS * c + h
                    pe.wait_ge(s_qc, H + c + 1)
                    pe.wait_ge(s_max, H + q)
                    for mine, other in ((0, 0), (0, 1), (1, 0)):
                        for at0, n in SCORE:
                            mm = pe.matmul(score[:, at0:at0 + n], q_parts[:, u, mine, h, :], KT[:, other, h, at0:at0 + n],
                                           start=(mine + other == 0), stop=(mine == 1))
                    mm.then_inc(s_S, 1)

                def slots(i, first, last):
                    for u in range(2):
                        for h in range(HEADS):
                            c = c0 + 2 * i + u
                            q = HEADS * c + h
                            if not (last and u == 1 and h == HEADS - 1):
                                nu, nh = (u, h + 1) if h + 1 < HEADS else (1 - u, 0)
                                scores(i + (u == 1 and nh == 0), nu, nh)
                            pe.wait_ge(s_P, H + q + 1)
                            for b, (t0, n) in enumerate(TURN):
                                pe.wait_ge(s_e[b], H + q)
                                for t in range(n):
                                    mm = pe.transpose(turned[:, b, t * P:(t + 1) * P], prob[:, h % 2, (t0 + t) * P:(t0 + t + 1) * P],
                                                      keep.ident[0:P, 0:P])
                                mm.then_inc(s_PT, 1)
                            if h == 2 and not (first and u == 0):
                                turn_att(c, 1 - u)
                            if h == 3 and not (first and u == 0):
                                project(c)
                            if not (first and u == 0 and h == 0):
                                values(q - 1, (h - 1) % HEADS)

                def values(q, h):
                    pe.wait_ge(s_att, H + q)
                    for b, (t0, n) in enumerate(TURN):
                        pe.wait_ge(s_e[b], H + q + 1)
                        for t in range(t0, t0 + n):
                            mm = pe.matmul(att_sum[:, h * DH:(h + 1) * DH], probT[:, h % 2, t, :],
                                           V[:, t * D + h * DH:t * D + (h + 1) * DH], start=(t == 0), stop=(t == NT - 1))
                    mm.then_inc(s_O, 1)

                def turn_att(c, u):
                    pe.wait_ge(s_att, H + HEADS * c)
                    pe.wait_ge(s_x, H + c - 1)
                    for k in range(KC):
                        mm = pe.transpose(rest[:, k * P:(k + 1) * P], att[:, u, k * 128:(k + 1) * 128], keep.ident[0:P, 0:P])
                    mm.then_inc(s_aT, 1)

                def project(c):
                    pe.wait_ge(s_aTe, H + c)
                    for k in range(KC):
                        mm = pe.matmul(rest[0:P, :], attT[:, k, :], w["wo"][:, k, :], start=(k == 0), stop=(k == KC - 1))
                    mm.then_inc(s_wo, 1)

                pe.wait_ge(w_in["wo"], 32 * blk + 32)
                pe.wait_ge(s_Ke, H + c0 + NT)
                pe.wait_ge(s_Qe, H + c0 + NT)
                pe.wait_ge(s_Ve, H + c0 + NT)
                scores(0, 0, 0)
                slots(0, True, False)
                with pe.Fori(1, PAIRS - 1) as i:
                    slots(i, False, False)
                slots(PAIRS - 1, False, True)
                values(HEADS * (c0 + NT) - 1, HEADS - 1)
                turn_att(c0 + NT, 1)
                project(c0 + NT)

                pe.wait_ge(s_cw, H + 2 * blk + 2)
                pe.wait_ge(w_in["mlp"], 48 * blk + 48)
                pe.wait_ge(s_x, H + c0 + NT)
                modulation("m", c0, 0)
                transposes("m", c0, 0)

                def back_m(i, more):
                    if more:
                        modulation("m", c0, i + 1)
                    pe.wait_ge(st["m", "zT"], H + c0 + 2 * i + 2)
                    for half in range(2):
                        pe.wait_ge(s_he, H + c0 + 2 * i + half - 1)
                        halves(w["m_w1"], half, s_h)
                    if more:
                        transposes("m", c0, i + 1)
                    pe.wait_ge(s_he, H + c0 + 2 * i + 2)
                    for u in range(2):
                        pe.wait_ge(s_x2, H + c0 + 2 * i + u - 1)
                        rows_of(hT, w["m_w2"], u, s_m2)

                with pe.Fori(0, PAIRS - 1) as i:
                    back_m(i, True)
                back_m(PAIRS - 1, False)
                pe.wait_ge(s_x2, H + c0 + NT)

            blocks(pe, body)

        @block.vector
        def _(dve):
            def front(kind, ready, c0):
                S = lambda n: st[kind, n]

                def stage(i):
                    for u in range(2):
                        c = c0 + 2 * i + u
                        dve.wait_ge(ready, ready_at(kind, c0, c))
                        layer_norm_stats(dve, X[:, at(2 * i + u, D)], stats[:, u, :], mv[:, u, :], var_eps[:, u, :], 1e-5,
                                         S("stats"), S("mv"), S("var"), gate, H + c)
                    for u in range(2):
                        c = c0 + 2 * i + u
                        dve.wait_ge(S("rstd"), H + c + 1)
                        dve.wait_ge(S("T"), H + c - 1)
                        dve.tensor_scalar(z[:, u, :], X[:, at(2 * i + u, D)], mv[:, u, 0:1], rstd[:, u, :],
                                          ALU.subtract, ALU.mult).then_inc(S("z"), 1)
                        dve.wait_ge(S("C"), H + c + 1)
                        dve.wait_ge(S("z"), H + c + 1)
                        dve.scalar_tensor_tensor(z[:, u, :], bank[0:P, 2 * u, :], 1.0, z[:, u, :], ALU.add, ALU.mult).then_inc(S("m1"), 1)
                        dve.wait_ge(S("m1"), H + c + 1)
                        dve.tensor_tensor(z[:, u, :], z[:, u, :], bank[0:P, 2 * u + 1, :], ALU.add).then_inc(S("mod"), 1)
                return stage

            def low_cond(n):
                dve.wait_ge(s_ch, H + n + 1)
                low = slice(GROUPS[1], GROUPS[1] + COND + 1)
                dve.tensor_tensor(cond_w[low, :, :], cond_raw[low, :, :], cond_w[low, :, :].bitcast(F32), ALU.subtract).then_inc(s_cw, 1)

            def ready_at(kind, c0, c):
                return H + c0 if kind == "a" else H + c + 1

            def body(blk):
                c0 = NT * blk
                low_cond(2 * blk)
                front_a = front("a", s_x2, c0)
                front_a(0)
                dve.wait_ge(w_in["qkv"], 80 * blk + 80)
                dve.sem_inc(gate, 1)

                def back(i, more):
                    for half in range(2):
                        dve.wait_ge(s_Kh, H + c0 + 2 * i + half + 1)
                        for h in range(2):
                            head = 2 * half + h
                            ins = dve.scalar_tensor_tensor(KT[:, 1, head, at(i, W2P)], pair_half[:, half, h * W2P:(h + 1) * W2P],
                                                           cols[:, 1, head:head + 1], KT[:, 0, head, at(i, W2P)].bitcast(F32),
                                                           ALU.add, ALU.subtract)
                        ins.then_inc(s_Ke, 1)
                    if more:
                        front_a(i + 1)
                    for half in range(2):
                        dve.wait_ge(s_Q, H + c0 + 2 * i + half + 1)
                        for h in range(2):
                            head = 2 * half + h
                            ins = dve.tensor_scalar(QT[:, head, at(i, W2P)], pair_half[:, half, h * W2P:(h + 1) * W2P],
                                                    cols[:, 0, head:head + 1], float(DH) ** -0.5, ALU.add, ALU.mult)
                        ins.then_inc(s_Qe, 1)
                    for u in range(2):
                        dve.wait_ge(s_V, H + c0 + 2 * i + u + 1)
                        dve.tensor_tensor(V[:, at(2 * i + u, D)], pair_row[0:P, u, :], rows["bv"][:, :], ALU.add).then_inc(s_Ve, 1)

                with dve.Fori(0, PAIRS - 1) as i:
                    back(i, True)
                back(PAIRS - 1, False)

                def maximum(i, u, h):
                    c = c0 + 2 * i + u
                    q = HEADS * c + h
                    dve.wait_ge(s_S, H + q + 1)
                    if h == 0:
                        dve.wait_ge(log_in[u], 16 * (PAIRS * blk + i) + 32)
                    dve.wait_ge(s_PT, H + 3 * q - 3)
                    dve.sem_inc(gate, 1)
                    dve.tensor_tensor_reduce(prob[:, h % 2, :], score[:, 0:NODES], log_cur[:, u, :], 1.0, -3.0e38, ALU.add, ALU.max,
                                             top[:, h % 2, :]).then_inc(s_max, 1)
                    dve.wait_ge(s_max, H + q + 1)
                    dve.tensor_scalar(neg[:, h % 2, :], top[:, h % 2, :], -1.0, None, ALU.mult).then_inc(s_neg, 1)

                def slots(i, first, last):
                    for u in range(2):
                        for h in range(HEADS):
                            c = c0 + 2 * i + u
                            q = HEADS * c + h
                            o = h % 2
                            if not (last and u == 1 and h == HEADS - 1):
                                nu, nh = (u, h + 1) if h + 1 < HEADS else (1 - u, 0)
                                maximum(i + (u == 1 and nh == 0), nu, nh)
                            dve.wait_ge(s_O, H + q - 1)
                            for b in range(2):
                                dve.wait_ge(s_PT, H + 3 * q + b + 1)
                                dve.tensor_copy(probT[:, o, 4 * b:4 * b + 4, :].rearrange("p t m -> p (t m)"),
                                                turned[:, b, 0:4 * P]).then_inc(s_e[b], 1)
                            dve.wait_ge(s_P, H + q + 1)
                            dve.sem_inc(gate, 1)
                            dve.wait_ge(s_att, H + q - 1)
                            dve.reciprocal(inv[:, o, :], den[:, o, :]).then_inc(s_inv, 1)
                            dve.wait_ge(s_inv, H + 2 * q + 1)
                            dve.scalar_tensor_tensor(inv[:, o, :], top[:, o, :], EMPTY, inv[:, o, :], ALU.is_gt, ALU.mult).then_inc(s_inv, 1)
                            dve.wait_ge(s_inv, H + 2 * q + 2)
                            if not (first and u == 0 and h == 0):
                                rows_done(c if h > 0 else c - 1, q - 1, u if h > 0 else 1 - u, (h - 1) % HEADS)
                            if h == 3 and not (first and u == 0):
                                add_rows(c, i - 1 if u == 0 else i, 1 - u)

                def rows_done(c, q, u, h):
                    if h == 0:
                        dve.wait_ge(s_aT, H + c - 1)
                    dve.wait_ge(s_O, H + q + 1)
                    dve.tensor_scalar(att[:, u, h * DH:(h + 1) * DH], att_sum[:, h * DH:(h + 1) * DH], inv[:, h % 2, :], None,
                                      ALU.mult).then_inc(s_att, 1)

                def add_rows(c, i, u):
                    x = X[:, at(2 * i + u, D)]
                    dve.wait_ge(s_wo, H + c)
                    dve.wait_ge(st["a", "bias"], H + c)
                    dve.tensor_tensor(x, x, rest[0:P, :], ALU.add).then_inc(s_x, 1)

                maximum(0, 0, 0)
                slots(0, True, False)
                with dve.Fori(1, PAIRS - 1) as i:
                    slots(i, False, False)
                slots(PAIRS - 1, False, True)
                rows_done(c0 + NT - 1, HEADS * (c0 + NT) - 1, 1, HEADS - 1)
                add_rows(c0 + NT, PAIRS - 1, 1)

                low_cond(2 * blk + 1)
                front_m = front("m", s_x, c0)
                front_m(0)

                def back_m(i, more):
                    if more:
                        front_m(i + 1)
                    for u in range(2):
                        c = c0 + 2 * i + u
                        x = X[:, at(2 * i + u, D)]
                        dve.wait_ge(s_m2, H + c + 1)
                        dve.wait_ge(st["m", "bias"], H + c + 1)
                        dve.tensor_tensor(x, x, pair_row[0:P, u, :], ALU.add).then_inc(s_x2, 1)

                with dve.Fori(0, PAIRS - 1) as i:
                    back_m(i, True)
                back_m(PAIRS - 1, False)

            blocks(dve, body)


def to_last_layer(nc, core, keep):
    with ExitStack() as ctx:
        summed = core.sem("summed")
        block = ctx.enter_context(nc.Block())

        @block.vector
        def _(dve):
            dve.tensor_tensor(keep.x[:, :], keep.self_in[:, :], keep.xn[:, :], ALU.add).then_inc(summed, 1)
            dve.wait_ge(summed, 1)


def layers(nc, core, a, keep, out):
    with ExitStack() as ctx:
        sb = lambda n, s, d=F32: core.sb(n, s, d, ctx)
        keep.x = sb("x", [P, NT * D])
        keep.node_id, keep.node_id16 = sb("node_id", [P, NODES]), sb("node_id16", [P, NODES], F16)
        keep.src_i, keep.dst_i = (sb(n, [P, NG * GT], I32) for n in ("src_i", "dst_i"))
        keep.src_f, keep.dst_f = (sb(n, [P, NG * GT]) for n in ("src_f", "dst_f"))
        keep.ranges = sb("ranges", [1, 3 * NT], I32)
        core.stage(node_products, a, keep)
        core.stage(edge_messages, a, keep)
        keep.log_pairs = sb("log_pairs", [P, NT, NODES])
        core.stage(segment_sums, a, keep)
        core.stage(node_update, a, keep)
        core.stage(experts, a, keep, "f0", keep.self_in, True)
        core.stage(prepare_attention, a, keep)
    core.stage(attention_blocks, a, keep)
    with ExitStack() as ctx:
        keep.x = core.sb("last_x", [P, NT * D], F32, ctx)
        core.stage(to_last_layer, keep)
        core.stage(experts, a, keep, "f1", keep.self_in, False, out)


def build(nc, a, out):
    with ExitStack() as ctx:
        core = Core(nc, ctx)
        keep = Keep()
        keep.xn = core.sb("xn", [P, NT * D])
        keep.self_in = core.sb("self_in", [P, NT * D])
        keep.agg = core.sb("agg", [128, NT * D])
        keep.ident = core.sb("ident", [128, 128])
        keep.minus_half = core.sb("minus_half", [P, 1])
        keep.cond_parts = core.sb("cond_parts", [COND_ROWS, NODES], F32R)
        keep.ends_dram = nc.dram_tensor("ends_rows", (NODES, 2, D), F32, kind="Internal").ap()
        keep.extent_dram = nc.dram_tensor("group_extents", (NG, 2), F32, kind="Internal").ap()
        keep.msg_dram = nc.dram_tensor("messages", (EDGES, D), F32, kind="Internal").ap()
        keep.slots_dram = nc.dram_tensor("expert_rows", (SLOTS + TOP * NODES, D), F32, kind="Internal").ap()
        keep.results_dram = nc.dram_tensor("expert_results", (RESULTS, D), F32, kind="Internal").ap()
        keep.x_dram = nc.dram_tensor("x_rows", (NODES, D), F32, kind="Internal").ap()
        keep.log_dram = nc.dram_tensor("log_counts", (NT, P, NODES), F32, kind="Internal").ap()
        layers(nc, core, a, keep, out)


def kernel(**inputs):
    import numpy as _np
    import concourse.bacc as _bacc
    from concourse import mybir as _mybir
    from concourse.bass_utils import run_bass_kernel_spmd as _run

    nc = _bacc.Bacc("TRN2", target_bir_lowering=False, num_devices=1)
    data = {k: _np.asarray(v) for k, v in inputs.items()}
    data["src_cols"] = data["src"].reshape(-1, P).T
    data["dst_cols"] = data["dst"].reshape(-1, P).T
    data["attr_T"] = data["edge_attr_64"].T
    data["b1_cols"] = data["L0_gnn_b1"].reshape(KC, 128).T
    data["router0"] = data["L0_ffn_router_w"].reshape(KC, 128, EXPERTS).transpose(1, 0, 2)
    data["router1"] = data["L1_ffn_gate_w"].reshape(EXPERTS, KC, 128).transpose(2, 1, 0)
    data["ffn0_b1_cols"] = data["L0_ffn_b1"].reshape(EXPERTS * FC, 128).T
    data["ffn1_b1_cols"] = data["L1_ffn_b1"].reshape(EXPERTS * FC, 128).T
    for n, s, b in (("cond1", "s1", "b1"), ("cond2", "s2", "b2")):
        data[n] = _np.stack([_np.concatenate([data[f"L1_gnn_{v}_w"], data[f"L1_gnn_{v}_b"][:, None, :]], axis=1)
                             for v in (s, b)], axis=2)
    data["cols"] = _np.stack([data["L1_gnn_" + n].reshape(BLOCKS, KC, 128).transpose(0, 2, 1) for n in ("bq", "bk", "m_b1")], axis=2)
    for unused in ("src", "edge_attr_64"):
        del data[unused]
    arrays, args = {}, {}
    for name, v in data.items():
        v = _np.ascontiguousarray(v)
        arrays["in_" + name] = v
        args[name] = nc.dram_tensor("in_" + name, v.shape, _mybir.dt.from_np(v.dtype), kind="ExternalInput").ap()
    out = nc.dram_tensor("out_0", (NODES, D), F32, kind="ExternalOutput").ap()
    build(nc, args, out)
    r = _run(nc, [arrays], core_ids=[0])
    return r.results[0]["out_0"]
```
